# Optimizing a Trainium2 kernel written in Bass

```python
import numpy as np
import jax
import jax.numpy as jnp

def _softmax(x, axis=-1):
    return jax.nn.softmax(x, axis=axis)

def _gelu(x):
    return jax.nn.gelu(x, approximate=True)

def _silu(x):
    return jax.nn.silu(x)

def _sigmoid(x):
    return jax.nn.sigmoid(x)

def _layernorm(x, axis=-1, eps=1e-05):
    m = jnp.mean(x, axis=axis, keepdims=True)
    v = jnp.var(x, axis=axis, keepdims=True)
    return (x - m) / jnp.sqrt(v + eps)

def _scatter_add(tgt, idx, src, axis=0):
    return tgt.at[idx].add(src)

def _segment_sum(src, seg, n):
    return jax.ops.segment_sum(src, seg, n)
kernel_name = 'mk_decoder_preln_d2_seqx_r8_e95c0d'

def setup_inputs(seed: int=0):
    np.random.seed(seed)
    _w = jnp.asarray

    def _rec_inputs():
        import jax
        import jax.numpy as jnp
        _rk = jax.random.key(seed)
        x = -0.000125 + 0.9999 * jax.random.normal(jax.random.fold_in(_rk, 1), (8, 128, 128), jnp.float32)
        _lenS = 128 - jax.random.randint(jax.random.fold_in(_rk, 7), (8,), 0, max(1, 128 // 4) + 1, jnp.int32)
        _lenS2 = 77 - jax.random.randint(jax.random.fold_in(_rk, 8), (8,), 0, max(1, 77 // 4) + 1, jnp.int32)
        _ctx_768P = jax.random.normal(jax.random.fold_in(_rk, 11), (8, 16, 96), jnp.float32)
        _ctx_768c = jax.random.dirichlet(jax.random.fold_in(_rk, 511), 0.3 * jnp.ones((16,), jnp.float32), (8, 77))
        _ctx_768t = jnp.einsum('bsk,bkd->bsd', _ctx_768c, _ctx_768P)
        _ctx_768t = _ctx_768t * jax.lax.rsqrt(jnp.mean(jnp.square(_ctx_768t)) + 1e-12) * 0.953939
        ctx_768 = 0.00243539 + 0.99952 * (_ctx_768t + 0.3 * jax.random.normal(jax.random.fold_in(_rk, 611), (8, 77, 96), jnp.float32))
        return (x, ctx_768)
    x, ctx_768 = _rec_inputs()

    def _L0_attn_setup():
        import jax, jax.numpy as jnp
        import numpy as np
        D_MODEL = 128
        N_SH = 16
        N_BR = 4
        H_TOT = N_BR * N_SH
        DH = D_MODEL // N_SH
        BRANCH_CONFIGS = [(16, 0), (128, 16), (128, 0), (64, 144)]

        def rms_norm(x):
            eps = jnp.finfo(x.dtype).eps
            return x * jax.lax.rsqrt(jnp.mean(x * x, axis=-1, keepdims=True) + eps)

        def rope(x):
            T, Dh = (x.shape[2], x.shape[3])
            inv_freq = 1.0 / 10000.0 ** (jnp.arange(0, Dh, 2, dtype=jnp.float32) / Dh)
            freqs = jnp.arange(T, dtype=jnp.float32)[:, None] * inv_freq[None, :]
            cos = jnp.cos(freqs)[None, None]
            sin = jnp.sin(freqs)[None, None]
            x1 = x[..., 0::2]
            x2 = x[..., 1::2]
            return jnp.concatenate([-x2 * sin + x1 * cos, x1 * sin + x2 * cos], axis=-1)
        key = jax.random.key(seed)
        ks = jax.random.split(key, 12)
        B, T, C = (2, 128, D_MODEL)
        s = 0.02
        return {'X': jax.random.normal(ks[0], (B, T, C), jnp.float32), 'WQ': jax.random.normal(ks[1], (C, H_TOT * DH), jnp.float32) * s, 'bQ': jax.random.normal(ks[2], (H_TOT * DH,), jnp.float32) * s, 'WK': jax.random.normal(ks[3], (C, C), jnp.float32) * s, 'bK': jax.random.normal(ks[4], (C,), jnp.float32) * s, 'WV': jax.random.normal(ks[5], (C, H_TOT * DH), jnp.float32) * s, 'bV': jax.random.normal(ks[6], (H_TOT * DH,), jnp.float32) * s, 'WO': jax.random.normal(ks[7], (C, C), jnp.float32) * s, 'bO': jax.random.normal(ks[8], (C,), jnp.float32) * s, 'sink_scalars': jax.random.normal(ks[9], (H_TOT,), jnp.float32) * s, 'v_nulls': jax.random.normal(ks[10], (H_TOT, DH), jnp.float32) * s}
    _L0_attn_all = _L0_attn_setup()
    _L0_attn_in = {k: v for k, v in _L0_attn_all.items() if k in ('WQ', 'bQ', 'WK', 'bK', 'WV', 'bV', 'WO', 'bO', 'sink_scalars', 'v_nulls')}
    del _L0_attn_all

    def _L0_xattn_setup():
        import jax, jax.numpy as jnp
        import numpy as np
        HEADS = 16
        DIM_HEAD = 64
        RANK = 32
        LORA_W = 1.0
        IPA_SCALE = 1.0
        IPA_TOKENS = 4
        SCALE = DIM_HEAD ** (-0.5)

        def _split_heads(t):
            b, n, _ = t.shape
            return t.reshape(b, n, HEADS, DIM_HEAD).transpose(0, 2, 1, 3)

        def _merge_heads(t):
            b, h, n, d = t.shape
            return t.transpose(0, 2, 1, 3).reshape(b, n, h * d)

        def _attention(q_in, k_in, v_in):
            q = _split_heads(q_in)
            k = _split_heads(k_in)
            v = _split_heads(v_in)
            s = jnp.einsum('bhid,bhjd->bhij', q, k) * SCALE
            p = jax.nn.softmax(s, axis=-1)
            o = jnp.einsum('bhij,bhjd->bhid', p, v)
            return _merge_heads(o)

        def _lora(t, down, up, alpha):
            return t @ down @ up * (LORA_W * alpha[0] / RANK)
        key = jax.random.key(seed)
        ks = jax.random.split(key, 20)
        B, N, QD, CD, ID = (8, 512, 128, 96, HEADS * DIM_HEAD)
        CTX = 77 + IPA_TOKENS
        s = 0.02
        return {'x': jax.random.normal(ks[0], (B, N, QD), jnp.float32), 'context': jax.random.normal(ks[1], (B, CTX, CD), jnp.float32), 'Wq': jax.random.normal(ks[2], (QD, ID), jnp.float32) * s, 'Wk': jax.random.normal(ks[3], (CD, ID), jnp.float32) * s, 'Wv': jax.random.normal(ks[4], (CD, ID), jnp.float32) * s, 'Wo': jax.random.normal(ks[5], (ID, QD), jnp.float32) * s, 'bo': jnp.zeros((QD,), jnp.float32), 'q_down': jax.random.normal(ks[6], (QD, RANK), jnp.float32) * s, 'q_up': jax.random.normal(ks[7], (RANK, ID), jnp.float32) * s, 'q_alpha': jnp.ones((1,), jnp.float32) * RANK, 'k_down': jax.random.normal(ks[8], (CD, RANK), jnp.float32) * s, 'k_up': jax.random.normal(ks[9], (RANK, ID), jnp.float32) * s, 'k_alpha': jnp.ones((1,), jnp.float32) * RANK, 'v_down': jax.random.normal(ks[10], (CD, RANK), jnp.float32) * s, 'v_up': jax.random.normal(ks[11], (RANK, ID), jnp.float32) * s, 'v_alpha': jnp.ones((1,), jnp.float32) * RANK, 'o_down': jax.random.normal(ks[12], (ID, RANK), jnp.float32) * s, 'o_up': jax.random.normal(ks[13], (RANK, QD), jnp.float32) * s, 'o_alpha': jnp.ones((1,), jnp.float32) * RANK, 'Wk_ipa': jax.random.normal(ks[14], (CD, ID), jnp.float32) * s, 'Wv_ipa': jax.random.normal(ks[15], (CD, ID), jnp.float32) * s}
    _L0_xattn_all = _L0_xattn_setup()
    _L0_xattn_in = {k: v for k, v in _L0_xattn_all.items() if k in ('Wq', 'Wk', 'Wv', 'Wo', 'bo', 'q_down', 'q_up', 'q_alpha', 'k_down', 'k_up', 'k_alpha', 'v_down', 'v_up', 'v_alpha', 'o_down', 'o_up', 'o_alpha', 'Wk_ipa', 'Wv_ipa')}
    del _L0_xattn_all

    def _L0_ffn_setup():
        import math
        import jax, jax.numpy as jnp
        import numpy as np
        CAPACITY_FACTOR = 1.25
        key = jax.random.key(seed)
        ks = jax.random.split(key, 5)
        B, S, H, F, E = (4, 512, 128, 128, 32)
        scale_in = 1.0 / math.sqrt(H)
        scale_mid = 1.0 / math.sqrt(F)
        return {'x': jax.random.normal(ks[0], (B, S, H), dtype=jnp.float32), 'w_router': jax.random.normal(ks[1], (H, E), dtype=jnp.float32) * scale_in, 'w_gate': jax.random.normal(ks[2], (E, H, F), dtype=jnp.float32) * scale_in, 'w_up': jax.random.normal(ks[3], (E, H, F), dtype=jnp.float32) * scale_in, 'w_down': jax.random.normal(ks[4], (E, F, H), dtype=jnp.float32) * scale_mid}
    _L0_ffn_all = _L0_ffn_setup()
    _L0_ffn_in = {k: v for k, v in _L0_ffn_all.items() if k in ('w_router', 'w_gate', 'w_up', 'w_down')}
    del _L0_ffn_all

    def _L1_attn_setup():
        import jax, jax.numpy as jnp
        import numpy as np
        N_HEAD = 16
        NEG_BIG = -10000000000.0

        def _rope_cos_sin(T, head_dim, dtype):
            half = head_dim // 2
            i = jnp.arange(half, dtype=jnp.float32)
            theta = 1.0 / 10000.0 ** (2.0 * i / head_dim)
            t = jnp.arange(T, dtype=jnp.float32)[:, None]
            ang = t * theta[None, :]
            return (jnp.cos(ang).astype(dtype), jnp.sin(ang).astype(dtype))

        def _apply_rope(x, cos, sin):
            B, H, T, D = x.shape
            xr = x.reshape(B, H, T, D // 2, 2)
            x0, x1 = (xr[..., 0], xr[..., 1])
            c = cos[None, None, :, :]
            s = sin[None, None, :, :]
            out = jnp.stack((x0 * c - x1 * s, x0 * s + x1 * c), axis=-1)
            return out.reshape(B, H, T, D)
        key = jax.random.key(seed)
        ks = jax.random.split(key, 9)
        B, T, C = (4, 256, 128)
        sc = 1.0 / np.sqrt(C)
        return {'x': jax.random.normal(ks[0], (B, T, C), jnp.float32), 'wq': jax.random.normal(ks[1], (C, C), jnp.float32) * sc, 'bq': jax.random.normal(ks[2], (C,), jnp.float32) * 0.02, 'wk': jax.random.normal(ks[3], (C, C), jnp.float32) * sc, 'bk': jax.random.normal(ks[4], (C,), jnp.float32) * 0.02, 'wv': jax.random.normal(ks[5], (C, C), jnp.float32) * sc, 'bv': jax.random.normal(ks[6], (C,), jnp.float32) * 0.02, 'wp': jax.random.normal(ks[7], (C, C), jnp.float32) * sc, 'bp': jax.random.normal(ks[8], (C,), jnp.float32) * 0.02}
    _L1_attn_all = _L1_attn_setup()
    _L1_attn_in = {k: v for k, v in _L1_attn_all.items() if k in ('wq', 'bq', 'wk', 'bk', 'wv', 'bv', 'wp', 'bp')}
    del _L1_attn_all

    def _L1_xattn_setup():
        import jax, jax.numpy as jnp
        import numpy as np
        NUM_HEADS = 16
        CLAMP = 10000.0
        key = jax.random.key(seed)
        ks = jax.random.split(key, 8)
        B, Nq, Nkv, Cq, Ckv = (4, 256, 256, 128, 96)
        s_q = 1.0 / np.sqrt(Cq)
        s_kv = 1.0 / np.sqrt(Ckv)
        return {'query': jax.random.normal(ks[0], (B, Nq, Cq), jnp.float32), 'key_value': jax.random.normal(ks[1], (B, Nkv, Ckv), jnp.float32), 'Wq': jax.random.normal(ks[2], (Cq, Cq), jnp.float32) * s_q, 'bq': jnp.zeros((Cq,), jnp.float32), 'Wk': jax.random.normal(ks[3], (Ckv, Cq), jnp.float32) * s_kv, 'bk': jnp.zeros((Cq,), jnp.float32), 'Wv': jax.random.normal(ks[4], (Ckv, Cq), jnp.float32) * s_kv, 'bv': jnp.zeros((Cq,), jnp.float32), 'Wo': jax.random.normal(ks[5], (Cq, Cq), jnp.float32) * s_q, 'bo': jnp.zeros((Cq,), jnp.float32)}
    _L1_xattn_all = _L1_xattn_setup()
    _L1_xattn_in = {k: v for k, v in _L1_xattn_all.items() if k in ('Wq', 'bq', 'Wk', 'bk', 'Wv', 'bv', 'Wo', 'bo')}
    del _L1_xattn_all

    def _L1_ffn_setup():
        import jax, jax.numpy as jnp
        import numpy as np
        TOP_K = 4
        CAP_FACTOR = 4

        def swiglu(x, w1, w2, w3):
            return jax.nn.silu(x @ w1) * (x @ w3) @ w2
        key = jax.random.key(seed)
        ks = jax.random.split(key, 8)
        B, S, D, H, E = (2, 256, 128, 64, 32)
        Hs = 2 * H
        sd = lambda *sh: 1.0 / np.sqrt(sh[-2])
        x = jax.random.normal(ks[0], (B, S, D), dtype=jnp.float32)
        Wg = jax.random.normal(ks[1], (D, E), dtype=jnp.float32) * (1.0 / np.sqrt(D))
        W1 = jax.random.normal(ks[2], (E, D, H), dtype=jnp.float32) * (1.0 / np.sqrt(D))
        W3 = jax.random.normal(ks[3], (E, D, H), dtype=jnp.float32) * (1.0 / np.sqrt(D))
        W2 = jax.random.normal(ks[4], (E, H, D), dtype=jnp.float32) * (1.0 / np.sqrt(H))
        Ws1 = jax.random.normal(ks[5], (D, Hs), dtype=jnp.float32) * (1.0 / np.sqrt(D))
        Ws3 = jax.random.normal(ks[6], (D, Hs), dtype=jnp.float32) * (1.0 / np.sqrt(D))
        Ws2 = jax.random.normal(ks[7], (Hs, D), dtype=jnp.float32) * (1.0 / np.sqrt(Hs))
        return {'x': x, 'Wg': Wg, 'W1': W1, 'W2': W2, 'W3': W3, 'Ws1': Ws1, 'Ws2': Ws2, 'Ws3': Ws3}
    _L1_ffn_all = _L1_ffn_setup()
    _L1_ffn_in = {k: v for k, v in _L1_ffn_all.items() if k in ('Wg', 'W1', 'W2', 'W3', 'Ws1', 'Ws2', 'Ws3')}
    del _L1_ffn_all
    return {'x': x, 'ctx_768': ctx_768, 'L0_attn_WQ': _L0_attn_in['WQ'], 'L0_attn_bQ': _L0_attn_in['bQ'], 'L0_attn_WK': _L0_attn_in['WK'], 'L0_attn_bK': _L0_attn_in['bK'], 'L0_attn_WV': _L0_attn_in['WV'], 'L0_attn_bV': _L0_attn_in['bV'], 'L0_attn_WO': _L0_attn_in['WO'], 'L0_attn_bO': _L0_attn_in['bO'], 'L0_attn_sink_scalars': _L0_attn_in['sink_scalars'], 'L0_attn_v_nulls': _L0_attn_in['v_nulls'], 'L0_xattn_Wq': _L0_xattn_in['Wq'], 'L0_xattn_Wk': _L0_xattn_in['Wk'], 'L0_xattn_Wv': _L0_xattn_in['Wv'], 'L0_xattn_Wo': _L0_xattn_in['Wo'], 'L0_xattn_bo': _L0_xattn_in['bo'], 'L0_xattn_q_down': _L0_xattn_in['q_down'], 'L0_xattn_q_up': _L0_xattn_in['q_up'], 'L0_xattn_q_alpha': _L0_xattn_in['q_alpha'], 'L0_xattn_k_down': _L0_xattn_in['k_down'], 'L0_xattn_k_up': _L0_xattn_in['k_up'], 'L0_xattn_k_alpha': _L0_xattn_in['k_alpha'], 'L0_xattn_v_down': _L0_xattn_in['v_down'], 'L0_xattn_v_up': _L0_xattn_in['v_up'], 'L0_xattn_v_alpha': _L0_xattn_in['v_alpha'], 'L0_xattn_o_down': _L0_xattn_in['o_down'], 'L0_xattn_o_up': _L0_xattn_in['o_up'], 'L0_xattn_o_alpha': _L0_xattn_in['o_alpha'], 'L0_xattn_Wk_ipa': _L0_xattn_in['Wk_ipa'], 'L0_xattn_Wv_ipa': _L0_xattn_in['Wv_ipa'], 'L0_ffn_w_router': _L0_ffn_in['w_router'], 'L0_ffn_w_gate': _L0_ffn_in['w_gate'], 'L0_ffn_w_up': _L0_ffn_in['w_up'], 'L0_ffn_w_down': _L0_ffn_in['w_down'], 'L1_attn_wq': _L1_attn_in['wq'], 'L1_attn_bq': _L1_attn_in['bq'], 'L1_attn_wk': _L1_attn_in['wk'], 'L1_attn_bk': _L1_attn_in['bk'], 'L1_attn_wv': _L1_attn_in['wv'], 'L1_attn_bv': _L1_attn_in['bv'], 'L1_attn_wp': _L1_attn_in['wp'], 'L1_attn_bp': _L1_attn_in['bp'], 'L1_xattn_Wq': _L1_xattn_in['Wq'], 'L1_xattn_bq': _L1_xattn_in['bq'], 'L1_xattn_Wk': _L1_xattn_in['Wk'], 'L1_xattn_bk': _L1_xattn_in['bk'], 'L1_xattn_Wv': _L1_xattn_in['Wv'], 'L1_xattn_bv': _L1_xattn_in['bv'], 'L1_xattn_Wo': _L1_xattn_in['Wo'], 'L1_xattn_bo': _L1_xattn_in['bo'], 'L1_ffn_Wg': _L1_ffn_in['Wg'], 'L1_ffn_W1': _L1_ffn_in['W1'], 'L1_ffn_W2': _L1_ffn_in['W2'], 'L1_ffn_W3': _L1_ffn_in['W3'], 'L1_ffn_Ws1': _L1_ffn_in['Ws1'], 'L1_ffn_Ws2': _L1_ffn_in['Ws2'], 'L1_ffn_Ws3': _L1_ffn_in['Ws3']}

def reference(x, ctx_768, L0_attn_WQ, L0_attn_bQ, L0_attn_WK, L0_attn_bK, L0_attn_WV, L0_attn_bV, L0_attn_WO, L0_attn_bO, L0_attn_sink_scalars, L0_attn_v_nulls, L0_xattn_Wq, L0_xattn_Wk, L0_xattn_Wv, L0_xattn_Wo, L0_xattn_bo, L0_xattn_q_down, L0_xattn_q_up, L0_xattn_q_alpha, L0_xattn_k_down, L0_xattn_k_up, L0_xattn_k_alpha, L0_xattn_v_down, L0_xattn_v_up, L0_xattn_v_alpha, L0_xattn_o_down, L0_xattn_o_up, L0_xattn_o_alpha, L0_xattn_Wk_ipa, L0_xattn_Wv_ipa, L0_ffn_w_router, L0_ffn_w_gate, L0_ffn_w_up, L0_ffn_w_down, L1_attn_wq, L1_attn_bq, L1_attn_wk, L1_attn_bk, L1_attn_wv, L1_attn_bv, L1_attn_wp, L1_attn_bp, L1_xattn_Wq, L1_xattn_bq, L1_xattn_Wk, L1_xattn_bk, L1_xattn_Wv, L1_xattn_bv, L1_xattn_Wo, L1_xattn_bo, L1_ffn_Wg, L1_ffn_W1, L1_ffn_W2, L1_ffn_W3, L1_ffn_Ws1, L1_ffn_Ws2, L1_ffn_Ws3):
    import jax
    import jax.numpy as jnp

    def _L0_attn_ref(X, WQ, bQ, WK, bK, WV, bV, WO, bO, sink_scalars, v_nulls):
        import jax, jax.numpy as jnp
        import numpy as np
        D_MODEL = 128
        N_SH = 16
        N_BR = 4
        H_TOT = N_BR * N_SH
        DH = D_MODEL // N_SH
        BRANCH_CONFIGS = [(16, 0), (128, 16), (128, 0), (64, 144)]

        def rms_norm(x):
            eps = jnp.finfo(x.dtype).eps
            return x * jax.lax.rsqrt(jnp.mean(x * x, axis=-1, keepdims=True) + eps)

        def rope(x):
            T, Dh = (x.shape[2], x.shape[3])
            inv_freq = 1.0 / 10000.0 ** (jnp.arange(0, Dh, 2, dtype=jnp.float32) / Dh)
            freqs = jnp.arange(T, dtype=jnp.float32)[:, None] * inv_freq[None, :]
            cos = jnp.cos(freqs)[None, None]
            sin = jnp.sin(freqs)[None, None]
            x1 = x[..., 0::2]
            x2 = x[..., 1::2]
            return jnp.concatenate([-x2 * sin + x1 * cos, x1 * sin + x2 * cos], axis=-1)
        B, T, C = X.shape
        q = (X @ WQ + bQ).reshape(B, T, H_TOT, DH).transpose(0, 2, 1, 3)
        q = rope(rms_norm(q))
        v = (X @ WV + bV).reshape(B, T, H_TOT, DH).transpose(0, 2, 1, 3)
        k = rope((X @ WK + bK).reshape(B, T, N_SH, DH).transpose(0, 2, 1, 3))
        k = jnp.tile(k, (1, N_BR, 1, 1))
        scores = jnp.einsum('bhqd,bhkd->bhqk', q, k)
        denom = jnp.sqrt(jnp.sum(k * k, axis=-1))[:, :, None, :]
        w = scores / denom
        idx = jnp.arange(T)
        dist = idx[:, None] - idx[None, :]
        bmasks = jnp.stack([((dist >= g) & (dist < h)).astype(w.dtype) for h, g in BRANCH_CONFIGS], axis=0)
        full_mask = jnp.repeat(bmasks, N_SH, axis=0)[None]
        w = w * full_mask
        sinks = jnp.broadcast_to(jnp.tanh(sink_scalars).reshape(1, H_TOT, 1, 1), (B, H_TOT, T, 1))
        probs = jax.nn.softmax(jnp.concatenate([w, sinks], axis=-1), axis=-1)
        out = jnp.einsum('bhqk,bhkd->bhqd', probs[..., :T], v)
        out = out + probs[..., T:] * v_nulls.reshape(1, H_TOT, 1, DH)
        ctx = out.reshape(B, N_BR, N_SH, T, DH).transpose(0, 1, 3, 2, 4).reshape(B, N_BR, T, C)
        y = ctx @ WO + bO
        return y.mean(axis=1)

    def _L0_xattn_ref(x, context, Wq, Wk, Wv, Wo, bo, q_down, q_up, q_alpha, k_down, k_up, k_alpha, v_down, v_up, v_alpha, o_down, o_up, o_alpha, Wk_ipa, Wv_ipa):
        import jax, jax.numpy as jnp
        import numpy as np
        HEADS = 16
        DIM_HEAD = 64
        RANK = 32
        LORA_W = 1.0
        IPA_SCALE = 1.0
        IPA_TOKENS = 4
        SCALE = DIM_HEAD ** (-0.5)

        def _split_heads(t):
            b, n, _ = t.shape
            return t.reshape(b, n, HEADS, DIM_HEAD).transpose(0, 2, 1, 3)

        def _merge_heads(t):
            b, h, n, d = t.shape
            return t.transpose(0, 2, 1, 3).reshape(b, n, h * d)

        def _attention(q_in, k_in, v_in):
            q = _split_heads(q_in)
            k = _split_heads(k_in)
            v = _split_heads(v_in)
            s = jnp.einsum('bhid,bhjd->bhij', q, k) * SCALE
            p = jax.nn.softmax(s, axis=-1)
            o = jnp.einsum('bhij,bhjd->bhid', p, v)
            return _merge_heads(o)

        def _lora(t, down, up, alpha):
            return t @ down @ up * (LORA_W * alpha[0] / RANK)
        q_in = x @ Wq + _lora(x, q_down, q_up, q_alpha)
        end = context.shape[1] - IPA_TOKENS
        org_ctx = context[:, :end, :]
        ipa_ctx = context[:, end:, :]
        k_in = org_ctx @ Wk + _lora(org_ctx, k_down, k_up, k_alpha)
        v_in = org_ctx @ Wv + _lora(org_ctx, v_down, v_up, v_alpha)
        out = _attention(q_in, k_in, v_in)
        ipa_k = ipa_ctx @ Wk_ipa
        ipa_v = ipa_ctx @ Wv_ipa
        out_ipa = _attention(q_in, ipa_k, ipa_v)
        out = out + IPA_SCALE * out_ipa
        return out @ Wo + bo + _lora(out, o_down, o_up, o_alpha)

    def _L0_ffn_ref(x, w_router, w_gate, w_up, w_down):
        import math
        import jax, jax.numpy as jnp
        import numpy as np
        CAPACITY_FACTOR = 1.25
        B, S, H = x.shape
        E = w_gate.shape[0]
        T = B * S
        C = int(math.ceil(CAPACITY_FACTOR * T / E))
        xt = x.reshape(T, H)
        logits = xt @ w_router
        probs = jax.nn.softmax(logits, axis=-1)
        top1 = jnp.argmax(probs, axis=-1)
        gate = jnp.take_along_axis(probs, top1[:, None], axis=1)[:, 0]
        onehot = jax.nn.one_hot(top1, E, dtype=jnp.int32)
        pos = jnp.cumsum(onehot, axis=0)[jnp.arange(T), top1] - 1
        accepted = pos < C
        slot = jnp.where(accepted, top1 * C + pos, E * C)
        buf = jnp.zeros((E * C + 1, H), dtype=x.dtype).at[slot].set(xt)
        buf = buf[:E * C].reshape(E, C, H)
        g = jnp.einsum('ech,ehf->ecf', buf, w_gate)
        u = jnp.einsum('ech,ehf->ecf', buf, w_up)
        y = jnp.einsum('ecf,efh->ech', jax.nn.silu(g) * u, w_down)
        out_tok = y.reshape(E * C, H)[jnp.clip(slot, 0, E * C - 1)]
        out_tok = jnp.where(accepted[:, None], out_tok * gate[:, None], 0.0)
        return (xt + out_tok).reshape(B, S, H)

    def _L1_attn_ref(x, wq, bq, wk, bk, wv, bv, wp, bp):
        import jax, jax.numpy as jnp
        import numpy as np
        N_HEAD = 16
        NEG_BIG = -10000000000.0

        def _rope_cos_sin(T, head_dim, dtype):
            half = head_dim // 2
            i = jnp.arange(half, dtype=jnp.float32)
            theta = 1.0 / 10000.0 ** (2.0 * i / head_dim)
            t = jnp.arange(T, dtype=jnp.float32)[:, None]
            ang = t * theta[None, :]
            return (jnp.cos(ang).astype(dtype), jnp.sin(ang).astype(dtype))

        def _apply_rope(x, cos, sin):
            B, H, T, D = x.shape
            xr = x.reshape(B, H, T, D // 2, 2)
            x0, x1 = (xr[..., 0], xr[..., 1])
            c = cos[None, None, :, :]
            s = sin[None, None, :, :]
            out = jnp.stack((x0 * c - x1 * s, x0 * s + x1 * c), axis=-1)
            return out.reshape(B, H, T, D)
        B, T, C = x.shape
        H = N_HEAD
        D = C // H

        def proj(w, b):
            return (jnp.einsum('btc,oc->bto', x, w) + b).reshape(B, T, H, D).transpose(0, 2, 1, 3)
        q = proj(wq, bq)
        k = proj(wk, bk)
        v = proj(wv, bv)
        cos, sin = _rope_cos_sin(T, D, x.dtype)
        q = _apply_rope(q, cos, sin)
        k = _apply_rope(k, cos, sin)
        att = jnp.einsum('bhtd,bhsd->bhts', q, k) * (1.0 / np.sqrt(D))
        causal = jnp.tril(jnp.ones((T, T), bool))
        att = jnp.where(causal[None, None], att, jnp.asarray(NEG_BIG, att.dtype))
        att = jax.nn.softmax(att, axis=-1)
        y = jnp.einsum('bhts,bhsd->bhtd', att, v)
        y = y.transpose(0, 2, 1, 3).reshape(B, T, C)
        return jnp.einsum('btc,oc->bto', y, wp) + bp

    def _L1_xattn_ref(query, key_value, Wq, bq, Wk, bk, Wv, bv, Wo, bo):
        import jax, jax.numpy as jnp
        import numpy as np
        NUM_HEADS = 16
        CLAMP = 10000.0
        B, Nq, Cq = query.shape
        Nkv = key_value.shape[1]
        H = NUM_HEADS
        D = Cq // H
        scale = D ** (-0.5)
        q = (query @ Wq + bq).reshape(B, Nq, H, D).transpose(0, 2, 1, 3)
        k = (key_value @ Wk + bk).reshape(B, Nkv, H, D).transpose(0, 2, 1, 3)
        v = (key_value @ Wv + bv).reshape(B, Nkv, H, D).transpose(0, 2, 1, 3)
        attn = jnp.einsum('bhqd,bhkd->bhqk', q, k) * scale
        attn = jnp.clip(attn, -CLAMP, CLAMP)
        attn = jax.nn.softmax(attn, axis=-1)
        attn = jnp.where(jnp.any(jnp.isnan(attn)), jnp.asarray(1.0 / Nkv, attn.dtype), attn)
        x = jnp.einsum('bhqk,bhkd->bqhd', attn, v).reshape(B, Nq, Cq)
        return x @ Wo + bo

    def _L1_ffn_ref(x, Wg, W1, W2, W3, Ws1, Ws2, Ws3):
        import jax, jax.numpy as jnp
        import numpy as np
        TOP_K = 4
        CAP_FACTOR = 4

        def swiglu(x, w1, w2, w3):
            return jax.nn.silu(x @ w1) * (x @ w3) @ w2
        B, S, D = x.shape
        E = Wg.shape[1]
        T = B * S
        xf = x.reshape(T, D)
        scores = jax.nn.softmax(xf @ Wg, axis=-1)
        weights, indices = jax.lax.top_k(scores, TOP_K)
        P = T * TOP_K
        pair_expert = indices.reshape(-1)
        pair_token = jnp.repeat(jnp.arange(T), TOP_K)
        pair_weight = weights.reshape(-1).astype(xf.dtype)
        C = CAP_FACTOR * P // E
        y = jnp.zeros_like(xf)
        for e in range(E):
            pos = jnp.nonzero(pair_expert == e, size=C, fill_value=P)[0]
            valid = pos < P
            safe = jnp.minimum(pos, P - 1)
            tok = jnp.where(valid, pair_token[safe], 0)
            w = jnp.where(valid, pair_weight[safe], 0.0)
            xg = xf[tok]
            out = swiglu(xg, W1[e], W2[e], W3[e]) * w[:, None]
            y = y.at[tok].add(out)
        z = swiglu(xf, Ws1, Ws2, Ws3)
        return (y + z).reshape(B, S, D)
    x = x + _L0_attn_ref(_layernorm(x, axis=-1), L0_attn_WQ, L0_attn_bQ, L0_attn_WK, L0_attn_bK, L0_attn_WV, L0_attn_bV, L0_attn_WO, L0_attn_bO, L0_attn_sink_scalars, L0_attn_v_nulls)
    x = x + _L0_xattn_ref(_layernorm(x, axis=-1), ctx_768, L0_xattn_Wq, L0_xattn_Wk, L0_xattn_Wv, L0_xattn_Wo, L0_xattn_bo, L0_xattn_q_down, L0_xattn_q_up, L0_xattn_q_alpha, L0_xattn_k_down, L0_xattn_k_up, L0_xattn_k_alpha, L0_xattn_v_down, L0_xattn_v_up, L0_xattn_v_alpha, L0_xattn_o_down, L0_xattn_o_up, L0_xattn_o_alpha, L0_xattn_Wk_ipa, L0_xattn_Wv_ipa)
    x = x + _L0_ffn_ref(_layernorm(x, axis=-1), L0_ffn_w_router, L0_ffn_w_gate, L0_ffn_w_up, L0_ffn_w_down)
    x = x + _L1_attn_ref(_layernorm(x, axis=-1), L1_attn_wq, L1_attn_bq, L1_attn_wk, L1_attn_bk, L1_attn_wv, L1_attn_bv, L1_attn_wp, L1_attn_bp)
    x = x + _L1_xattn_ref(_layernorm(x, axis=-1), ctx_768, L1_xattn_Wq, L1_xattn_bq, L1_xattn_Wk, L1_xattn_bk, L1_xattn_Wv, L1_xattn_bv, L1_xattn_Wo, L1_xattn_bo)
    x = x + _L1_ffn_ref(_layernorm(x, axis=-1), L1_ffn_Wg, L1_ffn_W1, L1_ffn_W2, L1_ffn_W3, L1_ffn_Ws1, L1_ffn_Ws2, L1_ffn_Ws3)
    return x

_drawn_inputs = setup_inputs


def setup_inputs(seed=0):
    import zlib

    import numpy as np

    out = dict(_drawn_inputs(seed))
    spreads = {'L0_xattn_bo': (0.0, 0.1),
     'L1_xattn_bq': (0.0, 0.631),
     'L1_xattn_bk': (0.0, 2.0),
     'L1_xattn_bv': (0.0, 0.1),
     'L1_xattn_bo': (0.0, 0.1)}
    factors = {'L0_attn_WQ': 8.0,
     'L0_attn_bQ': 32.981,
     'L0_attn_WK': 8.0,
     'L0_attn_bK': 38.999,
     'L0_attn_WV': 8.0,
     'L0_attn_bV': 8.0,
     'L0_attn_WO': 8.0,
     'L0_attn_sink_scalars': 200.0,
     'L0_attn_v_nulls': 200.0,
     'L0_xattn_Wq': 8.0,
     'L0_xattn_Wk': 8.0,
     'L0_xattn_q_down': 8.0,
     'L0_xattn_q_up': 8.0,
     'L0_xattn_k_down': 8.0,
     'L0_xattn_k_up': 8.0,
     'L0_xattn_v_down': 5.777,
     'L0_xattn_v_up': 6.413,
     'L0_xattn_o_down': 3.678,
     'L0_xattn_o_up': 3.821,
     'L0_xattn_Wk_ipa': 8.0,
     'L1_attn_bq': 35.526,
     'L1_attn_bk': 55.841,
     'L1_attn_bv': 5.017,
     'L1_attn_bp': 5.115}
    for name, (base, spread) in spreads.items():
        noise = np.random.default_rng([zlib.crc32(name.encode()), seed]).standard_normal(out[name].shape)
        drawn = base * np.exp(spread * noise) if base else spread * noise
        out[name] = jnp.asarray(drawn.astype(out[name].dtype))
    for name, factor in factors.items():
        out[name] = (out[name] * factor).astype(out[name].dtype)
    return out
```

```python
from contextlib import ExitStack

import concourse.bass as bass
from concourse import mybir

F32 = mybir.dt.float32
BF16 = mybir.dt.bfloat16
I32 = mybir.dt.int32
U32 = mybir.dt.uint32
ALU = mybir.AluOpType
ACT = mybir.ActivationFunctionType
AX = mybir.AxisListType

B, T, C = 8, 128, 128
H, D = 16, 8
G, R = 4, 4
BR = 4
L, CC = 77, 96
LO, LI = 73, 4
PR, DX = 8, 64
E = 32
CAP0 = 40
CAP1 = 512
HID = 64
TOPK = 4
BANK = 512
LN_EPS = 1e-5
RMS_EPS = 1.1920928955078125e-07
BIG = 1.0e6

CI, CM, CCOS, CSIN, CHM, CIOTA, CONE = 0, 128, 512, 520, 528, 532, 564
NCF = 692
BI, BNEG, BTRI, BONE = 0, 128, 256, 384
NCB = 512


def cols(b, n):
    return bass.ds(b * n, n)


class Net:
    pass


def buffers(nc, ctx, tag):
    def sb(name, shape, dt=F32):
        return ctx.enter_context(nc.sbuf_tensor(tag + name, shape, dt))

    own = []

    def sem(name):
        own.append(nc.alloc_semaphore(tag + name))
        return own[-1]

    def clear():
        if own:
            nc.clear_and_free_semaphores(own)
            nc.all_engine_barrier()

    ctx.callback(clear)
    return sb, sem


def peel(b, k, lag):
    return type(b) is int and b == 0 and k < lag


def batches(eng, a_then_b, first, last):
    first()
    a_then_b(0, 0)
    with eng.Fori(0, (B - 2) // 2) as i:
        a_then_b(2 * i + 1, 1)
        a_then_b(2 * i + 2, 0)
    last()


def load_phase(nc, w, n):
    with ExitStack() as ctx:
        sb, sem = buffers(nc, ctx, "ld_")
        small_loaded, x_loaded, lora_loaded = sem("small_loaded"), sem("x_loaded"), sem("lora_loaded")
        folded_ps, folded, psum_used = sem("folded_ps"), sem("folded"), sem("psum_used")
        tanh_done, sink_done, scaled = sem("tanh_done"), sem("sink_done"), sem("scaled")
        kvi_ps, kvi_sb, kvi_stored = sem("kvi_ps"), sem("kvi_sb"), sem("kvi_stored")
        sinks, v_nulls, esink = sb("sinks", [128, 64]), sb("v_nulls", [128, 512]), sb("esink", [128, 64])
        down = [sb(f"down{i}", [32, k]) for i, k in enumerate((C, CC, CC, 1024))]
        up = [sb(f"up{i}", [32, k]) for i, k in enumerate((1024, 1024, 1024, C))]
        alpha = sb("alpha", [128, 4])
        ctx_i = sb("ctx_i", [CC, B * LI])
        wvi = sb("wvi", [CC, 1024])
        vi = sb("vi", [B * LI, 1024])
        half = sb("half", [128, NCB])
        ps = ctx.enter_context(nc.psum_tensor("ld_ps", [128, 8 * BANK], F32))

        @nc_block(nc, ctx).sync
        def _(sp):
            sp.dma_start(n.X[:].rearrange("p (b c) -> p b c", b=B), w["x"].rearrange("b t c -> t b c")).then_inc(x_loaded, 16)
            sp.dma_start(n.CF[:], w["const_f32"]).then_inc(small_loaded, 16)
            sp.dma_start(half[:], w["const_half"]).then_inc(small_loaded, 16)
            sp.dma_start(sinks[:], w["L0_attn_sink_scalars"].rearrange("(o n) -> o n", o=1).to_broadcast([128, 64])).then_inc(small_loaded, 16)
            sp.dma_start(v_nulls[:], w["L0_attn_v_nulls"].rearrange("h d -> (h d)").rearrange("(o n) -> o n", o=1).to_broadcast([128, 512])).then_inc(small_loaded, 16)
            sp.dma_start(n.WQX[:], w["L0_xattn_Wq"]).then_inc(lora_loaded, 16)
            sp.dma_start(n.WKX[:], w["L0_xattn_Wk"]).then_inc(lora_loaded, 16)
            sp.dma_start(n.WVX[:], w["L0_xattn_Wv"]).then_inc(lora_loaded, 16)
            sp.dma_start(n.WOX[:].rearrange("p (j n) -> p j n", j=PR), w["L0_xattn_Wo"].rearrange("(j p) n -> p j n", p=128)).then_inc(lora_loaded, 16)
            sp.wait_ge(kvi_sb, 1)
            sp.dma_start(n.vi_dram, vi[:]).then_inc(kvi_stored, 16)
            sp.wait_ge(kvi_stored, 16)

        @n.block.scalar
        def _(act):
            for i, t in enumerate("qkvo"):
                act.dma_start(down[i][:], w[f"L0_xattn_{t}_down_T"]).then_inc(lora_loaded, 16)
                act.dma_start(up[i][:], w[f"L0_xattn_{t}_up"]).then_inc(lora_loaded, 16)
                act.dma_start(alpha[:, i:i + 1], w[f"L0_xattn_{t}_alpha"].rearrange("(o n) -> o n", o=1).to_broadcast([128, 1])).then_inc(lora_loaded, 16)
            act.dma_start(ctx_i[:], w["ctx_img_T"]).then_inc(lora_loaded, 16)
            act.dma_start(wvi[:], w["L0_xattn_Wv_ipa"]).then_inc(lora_loaded, 16)
            act.wait_ge(small_loaded, 64)
            act.activation(esink[:], sinks[:], ACT.Tanh).then_inc(tanh_done, 1)
            act.wait_ge(tanh_done, 1)
            act.activation(esink[:], esink[:], ACT.Exp).then_inc(sink_done, 1)
            act.wait_ge(kvi_ps, 1)
            act.activation(vi[:], ps[0:B * LI, 6 * BANK:8 * BANK], ACT.Copy).then_inc(kvi_sb, 1)

        @n.block.tensor
        def _(pe):
            pe.wait_ge(lora_loaded, 16 * 18)
            for i in range(3):
                for half in range(2):
                    last = pe.matmul(ps[0:down[i].shape[1], (2 * i + half) * BANK:(2 * i + half + 1) * BANK],
                                     down[i][:], up[i][:, half * BANK:(half + 1) * BANK], start=True, stop=True)
                last.then_inc(folded_ps, 1)
            for half in range(2):
                last = pe.matmul(ps[0:B * LI, (6 + half) * BANK:(7 + half) * BANK], ctx_i[:],
                                 wvi[:, half * BANK:(half + 1) * BANK], start=True, stop=True)
            last.then_inc(kvi_ps, 1)
            pe.wait_ge(folded, 1)
            for j in range(PR):
                last = pe.matmul(ps[:, j * 128:(j + 1) * 128], down[3][:, j * 128:(j + 1) * 128], up[3][:],
                                 start=True, stop=True)
            last.then_inc(folded_ps, 1)

        @n.block.vector
        def _(dve):
            dve.wait_ge(lora_loaded, 16 * 18)
            dve.tensor_scalar(alpha[:], alpha[:], 1.0 / 32, None, ALU.mult).then_inc(scaled, 1)
            dve.wait_ge(scaled, 1)
            for i, (dst, rows) in enumerate(((n.WQX, C), (n.WKX, CC), (n.WVX, CC), (n.WOX, 128))):
                dve.wait_ge(folded_ps, i + 1)
                src = ps[0:rows, 2 * (i % 3) * BANK:2 * (i % 3) * BANK + 1024]
                dve.scalar_tensor_tensor(dst[:], src, alpha[0:rows, i:i + 1], dst[:], ALU.mult, ALU.add).then_inc(folded, 1)
            dve.wait_ge(sink_done, 1)
            row = n.SINK[:].rearrange("p (h k) -> p h k", k=D + 1)
            dve.tensor_tensor(row[:, :, 0:D], v_nulls[:].rearrange("p (h d) -> p h d", d=D),
                              esink[:].unsqueeze(2).to_broadcast([128, 64, D]), ALU.mult).then_inc(folded, 1)
            dve.tensor_copy(row[:, :, D:D + 1], esink[:].unsqueeze(2)).then_inc(folded, 1)
            dve.wait_ge(x_loaded, 16)
            dve.tensor_copy(n.CB[:], half[:]).then_inc(folded, 1)
            dve.wait_ge(folded, 7)
            dve.memset(n.NHALF[:], -0.5).then_inc(tanh_done, 1)
            dve.memset(n.EPS[:], LN_EPS).then_inc(tanh_done, 1)
            dve.wait_ge(tanh_done, 3)


def nc_block(nc, ctx):
    Net.block = ctx.enter_context(nc.Block())
    return Net.block


def norm_stats(dve, n, b, stats, s):
    dve.bn_stats(stats[:, 0:6], n.X[:, cols(b, C)]).then_inc(s["stats"], 1)
    dve.wait_ge(s["stats"], b + 1)
    dve.tensor_copy(stats[:, 10:11], n.EPS[:])
    dve.bn_aggr(stats[:, 6:8], stats[:, 0:6]).then_inc(s["aggr"], 1)


def norm_apply(dve, n, b, dst, stats, s):
    dve.wait_ge(s["rstd"], b + 1)
    dve.tensor_scalar(dst, n.X[:, cols(b, C)], stats[:, 6:7], stats[:, 9:10], ALU.subtract, ALU.mult).then_inc(s["xn"], 1)


def norm_vector(dve, n, b, dst, stats, s):
    norm_stats(dve, n, b, stats, s)
    norm_apply(dve, n, b, dst, stats, s)


def norm_pool(pool, n, b, stats, s):
    pool.wait_ge(s["aggr"], b + 1)
    pool.tensor_tensor(stats[:, 8:9], stats[:, 7:8], n.EPS[:], ALU.add).then_inc(s["var_eps"], 1)
    pool.wait_ge(s["var_eps"], b + 1)
    pool.tensor_tensor(stats[:, 9:10], stats[:, 8:9], n.NHALF[:], ALU.pow).then_inc(s["rstd"], 1)


NORM_SEMS = ("stats", "aggr", "rstd", "xn", "var_eps")


def rope(dve, src, a, c, dst, nh, n, done, base):
    v = src.rearrange("p (h d) -> p h d", d=D)
    cos = n.CF[:, CCOS:CCOS + D].unsqueeze(1).to_broadcast([128, nh, D])
    sin = n.CF[:, CSIN:CSIN + D].unsqueeze(1).to_broadcast([128, nh, D])
    av = a.rearrange("p (h d) -> p h d", d=D)
    cv = c.rearrange("p (h d) -> p h d", d=D)
    dve.tensor_tensor(av, v, cos, ALU.mult).then_inc(done, 1)
    dve.tensor_tensor(cv, v, sin, ALU.mult).then_inc(done, 1)
    dve.wait_ge(done, base + 2)
    a2 = a.rearrange("p (h t two) -> p h t two", t=D // 2, two=2)
    c2 = c.rearrange("p (h t two) -> p h t two", t=D // 2, two=2)
    o = dst.rearrange("p (h d) -> p h d", d=D)
    dve.tensor_tensor(o[:, :, 0:4], a2[:, :, :, 0], c2[:, :, :, 1], ALU.subtract).then_inc(done, 1)
    dve.tensor_tensor(o[:, :, 4:8], c2[:, :, :, 0], a2[:, :, :, 1], ALU.add).then_inc(done, 1)


def self_attention0(nc, w, n):
    NQ = (BR - 1) * C
    VC = 32
    with ExitStack() as ctx:
        sb, sem = buffers(nc, ctx, "a0_")
        WQ, WK, WV, WO = sb("WQ", [128, NQ]), sb("WK", [128, C]), sb("WV", [128, 512]), sb("WO", [128, C])
        bqk, bv, bo = sb("bqk", [128, 512]), sb("bv", [128, 512]), sb("bo", [128, C])
        stats, XN, XT = sb("stats", [128, 11]), sb("XN", [128, C]), sb("XT", [128, T])
        QK, SQ, RA, RB, QR = (sb(k, [128, 512]) for k in ("QK", "SQ", "RA", "RB", "QR"))
        SS, Y, A1, A2 = (sb(k, [128, 64]) for k in ("SS", "Y", "A1", "A2"))
        SI = sb("SI", [128, 64], I32)
        QT, KZ, V = sb("QT", [128, 2, NQ]), sb("KZ", [128, 2, R, T]), sb("V", [128, 2, BR * H * VC])
        WS, P = sb("WS", [128, 2, 2 * NQ]), sb("P", [128, 2, 2 * NQ])
        OT = sb("OT", [128, 2, NQ])
        NUM, RD, CX, CS, CT = sb("NUM", [128, 2, BR * H * (D + 1)]), sb("RD", [128, 64]), sb("CX", [128, 512]), sb("CS", [128, C]), sb("CT", [128, T])
        ps = ctx.enter_context(nc.psum_tensor("a0_ps", [128, 8 * BANK], F32))
        bank = [ps[:, k * BANK:(k + 1) * BANK] for k in range(8)]
        s = {k: sem(k) for k in NORM_SEMS}
        loaded, v_ones = sem("loaded"), sem("v_ones")
        xT_ps, xT, qkv_ps, qk, v_rows, sq, rs = (sem(k) for k in ("xT_ps", "xT", "qkv_ps", "qk", "v_rows", "sq", "rs"))
        qr, qkT_ps, qT, kz = (sem(k) for k in ("qr", "qkT_ps", "qT", "kz"))
        s_ps, w_done, p_done, pv_done, oT, oR_ps = (sem(k) for k in ("s_ps", "w_done", "p_done", "pv_done", "oT", "oR_ps"))
        v_zero = sem("v_zero")
        num3 = sem("num3")
        num, cs, cT_ps, cT, y_ps, x_new = (sem(k) for k in ("num", "cs", "cT_ps", "cT", "y_ps", "x_new"))
        RS, QRN, CSN = 14, 4, 3

        @nc_block(nc, ctx).sync
        def _(sp):
            sp.dma_start(WQ[:], w["L0_attn_WQ"][:, 0:NQ]).then_inc(loaded, 16)
            sp.dma_start(WK[:], w["L0_attn_WK"]).then_inc(loaded, 16)
            sp.dma_start(WV[:], w["L0_attn_WV"]).then_inc(loaded, 16)
            sp.dma_start(WO[:], w["L0_attn_WO"]).then_inc(loaded, 16)
            row = lambda a: a.rearrange("(o n) -> o n", o=1)
            sp.dma_start(bqk[:, 0:NQ], row(w["L0_attn_bQ"])[:, 0:NQ].to_broadcast([128, NQ])).then_inc(loaded, 16)
            sp.dma_start(bqk[:, NQ:512], row(w["L0_attn_bK"]).to_broadcast([128, C])).then_inc(loaded, 16)
            sp.dma_start(bv[:], row(w["L0_attn_bV"]).to_broadcast([128, 512])).then_inc(loaded, 16)
            sp.dma_start(bo[:], row(w["L0_attn_bO"]).to_broadcast([128, C])).then_inc(loaded, 16)

        @n.block.gpsimd
        def _(pool):
            pool.memset(V[:], 0.0).then_inc(v_zero, 1)
            pool.wait_ge(v_zero, 1)
            pool.memset(V[:].rearrange("p t (h k) -> p (t h) k", k=VC)[:, :, D:D + 1], 1.0).then_inc(v_ones, 1)

            def a(b, p):
                norm_pool(pool, n, b, stats, s)

            batches(pool, lambda b, p: a(b + 1, 1 - p), lambda: a(0, 0), lambda: None)

        @n.block.scalar
        def _(act):
            def a_xt(b, p):
                act.wait_ge(xT_ps, b + 1)
                act.activation(XT[:], bank[4][:, 0:T], ACT.Copy).then_inc(xT, 1)

            def a_sq(b, p):
                act.wait_ge(qk, b + 1)
                act.activation(SQ[:], QK[:], ACT.Square).then_inc(sq, 1)

            def a_qt(b, p):
                act.wait_ge(qkT_ps, b + 1)
                act.activation(QT[:, p], bank[4][:, 0:NQ], ACT.Copy).then_inc(qT, 1)

            def b_pair(b, m):
                act.wait_ge(w_done, 16 * b + 2 * m + 2)
                if not (type(b) is int and b == 0 and m < 2):
                    act.wait_ge(pv_done, 8 * b + m - 1)
                act.activation(P[:, m % 2], WS[:, m % 2], ACT.Exp).then_inc(p_done, 1)

            def b_ctx(b):
                act.wait_ge(cT_ps, b + 1)
                act.activation(CT[:], bank[5][:, 0:T], ACT.Copy).then_inc(cT, 1)

            def b_ot(b, r):
                act.wait_ge(pv_done, 8 * b + 2 * r + 2)
                if not peel(b, r, 2):
                    act.wait_ge(oR_ps, 4 * b + r - 1)
                act.activation(OT[:, r % 2], bank[6 + r % 2][:, 0:NQ], ACT.Copy).then_inc(oT, 1)

            def pairs(b, p, more=True):
                for m in range(8):
                    b_pair(b, m)
                    if m == 0 and not peel(b, 0, 1):
                        b_ot(b - 1, 3)
                    if m in (2, 4, 6):
                        b_ot(b, m // 2 - 1)
                    if m == 1 and more:
                        a_xt(b + 1, 1 - p)
                    if m == 2 and more:
                        a_sq(b + 1, 1 - p)
                    if m == 4 and not peel(b, 0, 1):
                        b_ctx(b - 1)
                    if m == 6 and more:
                        a_qt(b + 1, 1 - p)

            batches(act, pairs, lambda: (a_xt(0, 0), a_sq(0, 0), a_qt(0, 0)),
                    lambda: (pairs(B - 1, 1, False), b_ot(B - 1, 3), b_ctx(B - 1)))

        @n.block.tensor
        def _(pe):
            pe.wait_ge(loaded, 16 * 8)
            ident = n.CF[:, CI:CI + 128]

            def a_xt(b, p):
                pe.wait_ge(s["xn"], b + 1)
                if not (type(b) is int and b == 0):
                    pe.wait_ge(qT, b)
                    pe.wait_ge(kz, b)
                pe.transpose(bank[4][:, 0:T], XN[:], ident).then_inc(xT_ps, 1)

            def a_proj(b, p):
                pe.wait_ge(xT, b + 1)
                pe.matmul(bank[4][:, 0:NQ], XT[:], WQ[:], start=True, stop=True)
                pe.matmul(bank[4][:, NQ:512], XT[:], WK[:], start=True, stop=True)
                pe.matmul(bank[5], XT[:], WV[:], start=True, stop=True).then_inc(qkv_ps, 1)

            def a_qkt(b, p):
                pe.wait_ge(qr, QRN * (b + 1))
                if not (type(b) is int and b < 2):
                    pe.wait_ge(x_new, 2 * (b - 1))
                for j in range(3):
                    pe.transpose(bank[4][:, j * 128:(j + 1) * 128], QR[:, j * 128:(j + 1) * 128], ident)
                pe.transpose(bank[5][:, 0:128], QR[:, NQ:512], ident)
                v3 = V[:, p, 3 * H * VC:].rearrange("p (h k) -> p h k", k=VC)[:, :, 0:D + 1]
                pe.matmul(bank[5][:, 128:272].rearrange("p (h k) -> p h k", k=D + 1), n.CF[:, CONE:CONE + 128], v3, start=True, stop=True).then_inc(qkT_ps, 1)

            def score(b, p, k):
                g, r = k % G, k // G
                if k == 0:
                    pe.wait_ge(qT, b + 1)
                    pe.wait_ge(kz, b + 1)
                if not (type(b) is int and b == 0 and k < 4):
                    pe.wait_ge(w_done, 16 * b + k - 3)
                rows = slice(32 * g, 32 * g + 32)
                pe.matmul(bank[k % 4][:, 0:NQ], KZ[rows, p, r], QT[rows, p], start=True, stop=True).then_inc(s_ps, 1)

            def values(b, p, m):
                r = m // 2
                pe.wait_ge(p_done, 8 * b + m + 1)
                if m == 0:
                    pe.wait_ge(v_rows, b + 1)
                if m % 2 == 0 and not peel(b, r, 2):
                    pe.wait_ge(num, 4 * b + r - 1)
                for k in (2 * m, 2 * m + 1):
                    g = k % G
                    for br in range(3):
                        at = (k % 2) * NQ + br * T
                        v = (br * H + G * g + r) * VC
                        last = pe.matmul(bank[6 + r % 2][32 * g:32 * g + 32, br * T:(br + 1) * T], V[:, p, v:v + VC],
                                         P[:, m % 2, at:at + T], start=True, stop=True)
                last.then_inc(pv_done, 1)

            def turn_back(b, r):
                pe.wait_ge(oT, 4 * b + r + 1)
                for br in range(3):
                    last = pe.transpose(bank[6 + r % 2][:, br * T:(br + 1) * T], OT[:, r % 2, br * T:(br + 1) * T], ident)
                last.then_inc(oR_ps, 1)

            def b_transpose(b):
                pe.wait_ge(cs, CSN * (b + 1))
                pe.transpose(bank[5][:, 0:T], CS[:], ident).then_inc(cT_ps, 1)

            def b_project(b):
                pe.wait_ge(cT, b + 1)
                pe.matmul(bank[5][:, 128:128 + C], CT[:], WO[:], start=True, stop=True).then_inc(y_ps, 1)

            def pairs(b, p, more=True):
                for m in range(8):
                    if m < 6:
                        score(b, p, 2 * m + 4), score(b, p, 2 * m + 5)
                    elif more:
                        score(b + 1, 1 - p, 2 * m - 12), score(b + 1, 1 - p, 2 * m - 11)
                    if m == 1 and more:
                        a_xt(b + 1, 1 - p)
                    if m == 2 and more:
                        a_proj(b + 1, 1 - p)
                    if m == 3 and not peel(b, 0, 1):
                        if more:
                            pe.wait_ge(v_rows, b + 2)
                        b_transpose(b - 1)
                    if m == 4 and not peel(b, 0, 1):
                        b_project(b - 1)
                    if m == 5 and more:
                        a_qkt(b + 1, 1 - p)
                    values(b, p, m)
                    if m == 0 and not peel(b, 0, 1):
                        turn_back(b - 1, 3)
                    if m in (2, 4, 6):
                        turn_back(b, m // 2 - 1)

            def first():
                a_xt(0, 0), a_proj(0, 0), a_qkt(0, 0)
                for k in range(4):
                    score(0, 0, k)

            def last():
                pairs(B - 1, 1, False)
                turn_back(B - 1, 3)
                pe.wait_ge(x_new, 2 * (B - 1))
                b_transpose(B - 1), b_project(B - 1)

            batches(pe, pairs, first, last)

        @n.block.vector
        def _(dve):
            dve.wait_ge(loaded, 16 * 8)
            dve.wait_ge(v_ones, 1)

            def a_bias(b, p):
                dve.wait_ge(qkv_ps, b + 1)
                dve.tensor_tensor(QK[:], bank[4], bqk[:], ALU.add).then_inc(qk, 1)
                out = V[:, p].rearrange("p (h k) -> p h k", k=VC)[:, :, 0:D]
                dve.tensor_tensor(out, bank[5].rearrange("p (h d) -> p h d", d=D), bv[:].rearrange("p (h d) -> p h d", d=D), ALU.add).then_inc(v_rows, 1)

            def a_rms(b, part):
                step = RS * b
                if part == 0:
                    dve.wait_ge(sq, b + 1)
                    dve.tensor_reduce(SS[:], SQ[:].rearrange("p (h d) -> p h d", d=D), AX.X, ALU.add).then_inc(rs, 1)
                    dve.wait_ge(rs, step + 1)
                    dve.tensor_scalar(SS[:, 0:48], SS[:, 0:48], 1.0 / D, RMS_EPS, ALU.mult, ALU.add).then_inc(rs, 1)
                    dve.wait_ge(rs, step + 2)
                    dve.tensor_scalar(SI[:], SS[:].bitcast(I32), 1, None, ALU.arith_shift_right).then_inc(rs, 1)
                    dve.wait_ge(rs, step + 3)
                    dve.tensor_scalar(Y[:].bitcast(I32), SI[:], -1.0, 1597463007.0, ALU.mult, ALU.add).then_inc(rs, 1)
                elif part < 4:
                    k = part - 1
                    dve.wait_ge(rs, step + 4 + 3 * k)
                    dve.tensor_tensor(A1[:], Y[:], Y[:], ALU.mult).then_inc(rs, 1)
                    dve.wait_ge(rs, step + 5 + 3 * k)
                    dve.scalar_tensor_tensor(A2[:], A1[:], -0.5, SS[:], ALU.mult, ALU.mult).then_inc(rs, 1)
                    dve.wait_ge(rs, step + 6 + 3 * k)
                    dve.scalar_tensor_tensor(Y[:], A2[:], 1.5, Y[:], ALU.add, ALU.mult).then_inc(rs, 1)
                else:
                    dve.wait_ge(rs, step + 13)
                    q3 = QK[:].rearrange("p (h d) -> p h d", d=D)
                    dve.tensor_tensor(q3, q3, Y[:].unsqueeze(2).to_broadcast([128, 64, D]), ALU.mult).then_inc(rs, 1)
                    dve.wait_ge(rs, step + 14)

            def a_rope(b, p):
                rope(dve, QK[:], RA[:], RB[:], QR[:], 64, n, qr, QRN * b)

            def a_kz(b, p):
                dve.wait_ge(qkT_ps, b + 1)
                dve.tensor_tensor(NUM[:, p, 432:576], bank[5][:, 128:272], n.SINK[:, 432:576], ALU.add).then_inc(num3, 1)
                dve.tensor_tensor(KZ[:, p], bank[5][:, 0:T].unsqueeze(1).to_broadcast([128, R, T]),
                                  n.CF[:, CHM:CHM + R].unsqueeze(2).to_broadcast([128, R, T]), ALU.mult).then_inc(kz, 1)

            def b_mask(b, k):
                m = k // 2
                dve.wait_ge(s_ps, 16 * b + k + 1)
                if not (type(b) is int and b == 0 and m < 2):
                    dve.wait_ge(p_done, 8 * b + m - 1)
                dve.tensor_tensor(WS[:, m % 2, (k % 2) * NQ:(k % 2 + 1) * NQ], bank[k % 4][:, 0:NQ],
                                  n.CF[:, CM:CM + NQ], ALU.mult).then_inc(w_done, 1)

            def b_num(b, p, r):
                def of_round(a):
                    return a.rearrange("p (br g r k) -> p br g r k", br=BR, g=G, r=R)[:, 0:3, :, r, :]

                dve.wait_ge(oR_ps, 4 * b + r + 1)
                rows = bank[6 + r % 2][:, 0:NQ].rearrange("p (br g k) -> p br g k", br=3, g=G)[:, :, :, 0:D + 1]
                dve.tensor_tensor(of_round(NUM[:, p]), rows, of_round(n.SINK[:]), ALU.add).then_inc(num, 1)

            def b_sums(b, p):
                dve.wait_ge(num, 4 * (b + 1))
                dve.wait_ge(num3, b + 1)
                n3 = NUM[:, p].rearrange("p (h k) -> p h k", k=D + 1)
                dve.reciprocal(RD[:].unsqueeze(2), n3[:, :, D:D + 1]).then_inc(cs, 1)
                dve.wait_ge(cs, CSN * b + 1)
                dve.tensor_tensor(CX[:].rearrange("p (h d) -> p h d", d=D), n3[:, :, 0:D],
                                  RD[:].unsqueeze(2).to_broadcast([128, 64, D]), ALU.mult).then_inc(cs, 1)
                dve.wait_ge(cs, CSN * b + 2)
                dve.tensor_reduce(CS[:], CX[:].rearrange("p (r c) -> p c r", r=BR), AX.X, ALU.add).then_inc(cs, 1)

            def b_out(b):
                dve.wait_ge(y_ps, b + 1)
                x = n.X[:, cols(b, C)]
                dve.scalar_tensor_tensor(x, bank[5][:, 128:128 + C], 1.0 / BR, x, ALU.mult, ALU.add).then_inc(x_new, 1)
                dve.wait_ge(x_new, 2 * b + 1)
                dve.tensor_tensor(x, x, bo[:], ALU.add).then_inc(x_new, 1)

            def masks(b, p, more=True):
                for k in range(16):
                    b_mask(b, k)
                    if k == 3 and not peel(b, 0, 1):
                        b_num(b - 1, 1 - p, 3)
                        b_sums(b - 1, 1 - p)
                    if k in (7, 11, 15):
                        b_num(b, p, k // 4 - 1)
                    if k == 12 and not peel(b, 0, 1):
                        b_out(b - 1)
                    if more:
                        if k == 2:
                            norm_stats(dve, n, b + 1, stats, s)
                        if k == 3:
                            norm_apply(dve, n, b + 1, XN[:], stats, s)
                        if k == 6:
                            a_bias(b + 1, 1 - p)
                        if 7 <= k < 12:
                            a_rms(b + 1, k - 7)
                        if k == 11:
                            a_rope(b + 1, 1 - p)
                        if k == 14:
                            a_kz(b + 1, 1 - p)

            def first():
                norm_vector(dve, n, 0, XN[:], stats, s)
                a_bias(0, 0)
                for part in range(5):
                    a_rms(0, part)
                a_rope(0, 0), a_kz(0, 0)

            def last():
                masks(B - 1, 1, False)
                b_num(B - 1, 1, 3)
                b_sums(B - 1, 1)
                b_out(B - 1)
                dve.wait_ge(x_new, 2 * B)

            batches(dve, masks, first, last)


def cross_attention0(nc, w, n):
    SCALE = DX ** -0.5
    with ExitStack() as ctx:
        sb, sem = buffers(nc, ctx, "x0_")
        WKI, bo = sb("WKI", [CC, 1024]), sb("bo", [128, C])
        stats, XN, XT = sb("stats", [128, 11]), sb("XN", [128, C]), sb("XT", [128, T])
        CT = sb("CT", [CC, 2, L])
        QT, KT, V = sb("QT", [128, PR * T]), sb("KT", [128, PR * L]), sb("V", [L, 2, 1024])
        MX, SM, RD = sb("MX", [128, 2 * H]), sb("SM", [128, 2 * H]), sb("RD", [128, 2 * H])
        P = sb("P", [128, 2, H * L])
        PT, OT = sb("PT", [L, 2, 4 * T]), sb("OT", [128, PR * T])
        ps = ctx.enter_context(nc.psum_tensor("x0_ps", [128, 8 * BANK], F32))
        bank = [ps[:, k * BANK:(k + 1) * BANK] for k in range(8)]
        s = {k: sem(k) for k in NORM_SEMS}
        loaded = sem("loaded")
        ctx_in = [sem("ctx_even"), sem("ctx_odd")]
        vi_in = [sem("vi_even"), sem("vi_odd")]
        xT_ps, xT, q_ps, qT, k_ps, kT, v_ps, v_rows = (sem(k) for k in ("xT_ps", "xT", "q_ps", "qT", "k_ps", "kT", "v_ps", "v_rows"))
        s_ps, mx, sub, p_exp, sm, p_norm = (sem(k) for k in ("s_ps", "mx", "sub", "p_exp", "sm", "p_norm"))
        pT_ps, pT, o_ps, oT, y_ps, x_new = (sem(k) for k in ("pT_ps", "pT", "o_ps", "oT", "y_ps", "x_new"))

        scores = ps[:, 0:4 * BANK].rearrange("p (k n) -> p k n", k=4)[:, :, 0:4 * L].rearrange("p k (h l) -> p k h l", h=4)

        def place(h):
            return 8 * (h % 2) + h // 2

        def spread(a):
            return a.rearrange("p (h t) -> p h t", t=2)

        @nc_block(nc, ctx).sync
        def _(sp):
            sp.dma_start(WKI[:], w["L0_xattn_Wk_ipa"]).then_inc(loaded, 16)
            sp.dma_start(bo[:], w["L0_xattn_bo"].rearrange("(o n) -> o n", o=1).to_broadcast([128, C])).then_inc(loaded, 16)

            def a(b, p, turn):
                if not peel(b, p, 2):
                    sp.wait_ge(o_ps, 4 * (b - 1))
                sp.dma_start(CT[:, p, :], w["ctx_T"][bass.ds(b, 1)].rearrange("o c l -> c (o l)")).then_inc(ctx_in[p], 16)
                sp.dma_start(V[LO:L, p, :], n.vi_dram[cols(b, LI), :]).then_inc(vi_in[p], 16)

            a(0, 0, 0)
            a(1, 1, 0)
            with sp.Fori(1, B // 2) as i:
                a(2 * i, 0, i)
                a(2 * i + 1, 1, i)

        @n.block.gpsimd
        def _(pool):
            batches(pool, lambda b, p: norm_pool(pool, n, b + 1, stats, s), lambda: norm_pool(pool, n, 0, stats, s), lambda: None)

        @n.block.scalar
        def _(act):
            def a_xt(b, p):
                act.wait_ge(xT_ps, b + 1)
                act.activation(XT[:], bank[4][:, 0:T], ACT.Copy).then_inc(xT, 1)

            def a_q(b, p):
                act.wait_ge(q_ps, b + 1)
                act.activation(QT[:], ps[:, 4 * BANK:6 * BANK], ACT.Copy).then_inc(qT, 1)

            def a_k(b, p):
                act.wait_ge(k_ps, b + 1)
                src = ps[:, 4 * BANK:6 * BANK].rearrange("p (k n) -> p k n", k=2)[:, :, 0:4 * L]
                act.activation(KT[:].rearrange("p (k n) -> p k n", k=2), src, ACT.Copy).then_inc(kT, 1)

            def a_v(b, p):
                act.wait_ge(v_ps, b + 1)
                act.activation(V[0:LO, p, :], ps[0:LO, 4 * BANK:6 * BANK], ACT.Copy).then_inc(v_rows, 1)

            def a_exp(b, p):
                act.wait_ge(sub, 2 * (b + 1))
                act.activation(P[:, p, :], P[:, p, :], ACT.Exp, scale=SCALE).then_inc(p_exp, 1)

            def b_pt(b, p, g):
                act.wait_ge(pT_ps, 4 * b + g + 1)
                if not peel(b, g, 2):
                    act.wait_ge(o_ps, 4 * b + g - 1)
                act.activation(PT[:, g % 2, :], bank[6][0:L, :], ACT.Copy).then_inc(pT, 1)

            def a_then_b(b, p):
                b_pt(b, p, 0)
                a_xt(b + 1, 1 - p)
                b_pt(b, p, 1)
                a_q(b + 1, 1 - p)
                b_pt(b, p, 2)
                a_k(b + 1, 1 - p)
                b_pt(b, p, 3)
                a_v(b + 1, 1 - p)
                a_exp(b + 1, 1 - p)

            def first():
                a_xt(0, 0), a_q(0, 0), a_k(0, 0), a_v(0, 0), a_exp(0, 0)

            def last():
                for g in range(4):
                    b_pt(B - 1, 1, g)

            batches(act, a_then_b, first, last)

        @n.block.tensor
        def _(pe):
            ident = n.CF[:, CI:CI + 128]

            def a_xt(b, p):
                pe.wait_ge(s["xn"], b + 1)
                if not peel(b, 0, 1):
                    pe.wait_ge(v_rows, b)
                pe.transpose(bank[4][:, 0:T], XN[:], ident).then_inc(xT_ps, 1)

            def a_q(b, p):
                pe.wait_ge(xT, b + 1)
                for j in range(PR):
                    last = pe.matmul(ps[:, 4 * BANK + j * T:4 * BANK + (j + 1) * T], n.WQX[:, j * 128:(j + 1) * 128], XT[:],
                                     start=True, stop=True)
                last.then_inc(q_ps, 1)

            def a_k(b, p, turn):
                pe.wait_ge(qT, b + 1)
                pe.wait_ge(ctx_in[p], 16 * (turn + 1))
                for j in range(PR):
                    at = (4 + j // 4) * BANK + (j % 4) * L
                    pe.matmul(ps[:, at:at + LO], n.WKX[:, j * 128:(j + 1) * 128], CT[:, p, 0:LO], start=True, stop=True)
                    last = pe.matmul(ps[:, at + LO:at + L], WKI[:, j * 128:(j + 1) * 128], CT[:, p, LO:L], start=True, stop=True)
                last.then_inc(k_ps, 1)

            def a_v(b, p):
                pe.wait_ge(kT, b + 1)
                for half in range(2):
                    last = pe.matmul(ps[0:LO, (4 + half) * BANK:(5 + half) * BANK], CT[:, p, 0:LO],
                                     n.WVX[:, half * BANK:(half + 1) * BANK], start=True, stop=True)
                last.then_inc(v_ps, 1)

            def a_scores(b, p):
                if not peel(b, 0, 1):
                    pe.wait_ge(sub, 2 * b)
                for h in range(H):
                    rows = slice(DX * (h % 2), DX * (h % 2) + DX)
                    j = h // 2
                    at = place(h) // 4 * BANK + place(h) % 4 * L
                    last = pe.matmul(ps[:, at:at + L], QT[rows, j * T:(j + 1) * T], KT[rows, j * L:(j + 1) * L], start=True, stop=True)
                last.then_inc(s_ps, 1)

            def b_pt(b, p, g):
                if g == 0:
                    pe.wait_ge(p_norm, 2 * (b + 1))
                if not peel(b, g, 1):
                    pe.wait_ge(pT, 4 * b + g)
                if g == 0 and not peel(b, 0, 1):
                    pe.wait_ge(x_new, 2 * b)
                for k in range(4):
                    h = 4 * g + k
                    last = pe.transpose(bank[6][0:L, k * T:(k + 1) * T], P[:, p, place(h) * L:(place(h) + 1) * L], ident)
                last.then_inc(pT_ps, 1)

            def b_pv(b, p, g, turn):
                pe.wait_ge(pT, 4 * b + g + 1)
                if g == 0:
                    pe.wait_ge(vi_in[p], 16 * (turn + 1))
                    pe.wait_ge(v_rows, b + 1)
                if not peel(b, g, 1):
                    pe.wait_ge(oT, 4 * b + g)
                for k in range(4):
                    h = 4 * g + k
                    last = pe.matmul(bank[7][DX * (h % 2):DX * (h % 2) + DX, (k // 2) * T:(k // 2 + 1) * T],
                                     V[:, p, h * DX:(h + 1) * DX], PT[:, g % 2, k * T:(k + 1) * T], start=True, stop=True)
                last.then_inc(o_ps, 1)

            def b_out(b):
                pe.wait_ge(oT, 4 * (b + 1))
                for j in range(PR):
                    last = pe.matmul(bank[6][:, 0:C], OT[:, j * T:(j + 1) * T], n.WOX[:, j * C:(j + 1) * C],
                                     start=(j == 0), stop=(j == PR - 1))
                last.then_inc(y_ps, 1)

            pe.wait_ge(loaded, 32)

            def a_then_b(b, p, turn=0, next_turn=0):
                b_pt(b, p, 0)
                a_xt(b + 1, 1 - p)
                b_pv(b, p, 0, turn)
                b_pt(b, p, 1)
                a_q(b + 1, 1 - p)
                b_pv(b, p, 1, turn)
                b_pt(b, p, 2)
                a_k(b + 1, 1 - p, next_turn)
                b_pv(b, p, 2, turn)
                b_pt(b, p, 3)
                a_v(b + 1, 1 - p)
                b_pv(b, p, 3, turn)
                a_scores(b + 1, 1 - p)
                b_out(b)

            a_xt(0, 0), a_q(0, 0), a_k(0, 0, 0), a_v(0, 0), a_scores(0, 0)
            a_then_b(0, 0, 0, 0)
            with pe.Fori(0, (B - 2) // 2) as i:
                a_then_b(2 * i + 1, 1, i, i + 1)
                a_then_b(2 * i + 2, 0, i + 1, i + 1)
            for g in range(4):
                b_pt(B - 1, 1, g)
                b_pv(B - 1, 1, g, B // 2 - 1)
            b_out(B - 1)

        @n.block.vector
        def _(dve):
            def a_norm(b, p):
                norm_vector(dve, n, b, XN[:], stats, s)

            def a_softmax1(b, p):
                dve.wait_ge(s_ps, b + 1)
                m4 = MX[:].rearrange("p (k h t) -> p k h t", k=4, t=2)
                p4 = P[:, p, :].rearrange("p (k h l) -> p k h l", k=4, l=L)
                dve.tensor_reduce(m4[:, :, :, 0], scores[:, :, :, 0:LO], AX.X, ALU.max).then_inc(mx, 1)
                dve.tensor_reduce(m4[:, :, :, 1], scores[:, :, :, LO:L], AX.X, ALU.max).then_inc(mx, 1)
                dve.wait_ge(mx, 2 * (b + 1))
                for t, (lo, hi) in enumerate(((0, LO), (LO, L))):
                    dve.tensor_tensor(p4[:, :, :, lo:hi], scores[:, :, :, lo:hi],
                                      m4[:, :, :, t:t + 1].to_broadcast([128, 4, 4, hi - lo]), ALU.subtract).then_inc(sub, 1)

            def a_softmax2(b, p):
                dve.wait_ge(p_exp, b + 1)
                p3 = P[:, p, :].rearrange("p (h l) -> p h l", l=L)
                sums = spread(SM[:])
                dve.tensor_reduce(sums[:, :, 0], p3[:, :, 0:LO], AX.X, ALU.add).then_inc(sm, 1)
                dve.tensor_reduce(sums[:, :, 1], p3[:, :, LO:L], AX.X, ALU.add).then_inc(sm, 1)
                dve.wait_ge(sm, 3 * b + 2)
                dve.reciprocal(RD[:], SM[:]).then_inc(sm, 1)
                dve.wait_ge(sm, 3 * b + 3)
                rd = spread(RD[:])
                for t, (lo, hi) in enumerate(((0, LO), (LO, L))):
                    dve.tensor_tensor(p3[:, :, lo:hi], p3[:, :, lo:hi], rd[:, :, t:t + 1].to_broadcast([128, H, hi - lo]), ALU.mult).then_inc(p_norm, 1)

            def b_ot(b, g):
                dve.wait_ge(o_ps, 4 * b + g + 1)
                if g == 0 and not peel(b, 0, 1):
                    dve.wait_ge(y_ps, b)
                dve.tensor_copy(OT[:, 2 * g * T:2 * (g + 1) * T], bank[7][:, 0:2 * T]).then_inc(oT, 1)

            def b_out(b):
                dve.wait_ge(y_ps, b + 1)
                x = n.X[:, cols(b, C)]
                dve.tensor_tensor(x, bank[6][:, 0:C], x, ALU.add).then_inc(x_new, 1)
                dve.wait_ge(x_new, 2 * b + 1)
                dve.tensor_tensor(x, x, bo[:], ALU.add).then_inc(x_new, 1)

            dve.wait_ge(loaded, 32)

            def a_then_b(b, p):
                a_norm(b + 1, 1 - p)
                for g in range(4):
                    b_ot(b, g)
                a_softmax1(b + 1, 1 - p)
                b_out(b)
                a_softmax2(b + 1, 1 - p)

            def first():
                a_norm(0, 0), a_softmax1(0, 0), a_softmax2(0, 0)

            def last():
                for g in range(4):
                    b_ot(B - 1, g)
                b_out(B - 1)
                dve.wait_ge(x_new, 2 * B)

            batches(dve, a_then_b, first, last)


def each_batch(eng, f):
    f(0, 0, 0)
    f(1, 1, 0)
    with eng.Fori(1, B // 2) as i:
        f(2 * i, 0, i)
        f(2 * i + 1, 1, i)


def carry_wait(dve, n, sem, value, spare):
    dve.wait_ge(sem, value)
    dve.tensor_copy(spare, n.EPS[:])


def route0(nc, w, n):
    with ExitStack() as ctx:
        sb, sem = buffers(nc, ctx, "r0_")
        WR, ZERO = sb("WR", [128, E]), sb("ZERO", [128, 1280])
        stats, XN, XT = sb("stats", [128, 11]), sb("XN", [128, 2, C]), sb("XT", [128, 2, T])
        LG, TOP, IDX, NEG = sb("LG", [128, 2, E]), sb("TOP", [128, 8]), sb("IDX", [128, 8], U32), sb("NEG", [128, 2, 1])
        EX, SE, IDF, PC, CNT, OV, SL = sb("EX", [128, E]), sb("SE", [128, 2, 1]), sb("IDF", [128, 1]), sb("PC", [128, E]), sb("CNT", [128, 1]), sb("OV", [128, 1]), sb("SL", [128, 1])
        SLI, SPARE = sb("SLI", [128, 2, 1], I32), sb("SPARE", [128, 1])
        OH, OHS = sb("OH", [128, 2, E], BF16), sb("OHS", [128, 2, E], BF16)
        ps = ctx.enter_context(nc.psum_tensor("r0_ps", [128, 8 * BANK], F32))
        bank = [ps[:, k * BANK:(k + 1) * BANK] for k in range(8)]
        s = {k: sem(k) for k in NORM_SEMS}
        loaded, zeroed, cleared, ohs0 = sem("loaded"), sem("zeroed"), sem("cleared"), sem("ohs0")
        xT_ps, xT, l_ps, lg, top, idx, neg, se, oh, pos_ps, slot, steps = (
            sem(k) for k in ("xT_ps", "xT", "l_ps", "lg", "top", "idx", "neg", "se", "oh", "pos_ps", "slot", "steps"))
        scattered = [sem("scattered_even"), sem("scattered_odd")]
        NS = 9

        @nc_block(nc, ctx).sync
        def _(sp):
            sp.dma_start(WR[:], w["L0_ffn_w_router"]).then_inc(loaded, 16)
            sp.wait_ge(zeroed, 1)
            sp.dma_start(n.buf_dram.rearrange("(p k) c -> p (k c)", p=128), ZERO[:]).then_inc(cleared, 16)
            for p in range(2):
                sp.wait_ge(scattered[p], 16 * 4)

        @n.block.gpsimd
        def _(pool):
            pool.memset(ZERO[:], 0.0).then_inc(zeroed, 1)
            pool.memset(OHS[:], 0.0).then_inc(ohs0, 1)
            last_slot = pool.to_reg(E * CAP0 - 1)

            def f(b, p, turn):
                norm_pool(pool, n, b, stats, s)
                if type(b) is int and b == 0:
                    pool.wait_ge(cleared, 16)
                pool.wait_ge(slot, b + 1)
                pool.tensor_tensor(SPARE[:], n.EPS[:], n.EPS[:], ALU.add)
                pool.indirect_dma_start(out=n.buf_dram, out_offset=bass.IndirectOffsetOnAxis(ap=SLI[:, p, :].bitcast(U32), axis=0),
                                        in_=XN[:, p, :], in_offset=None, bounds_check=last_slot,
                                        oob_is_err=False).then_inc(scattered[p], 16)

            each_batch(pool, f)

        @n.block.scalar
        def _(act):
            def f(b, p, turn):
                act.wait_ge(xT_ps, b + 1)
                act.activation(XT[:, p], bank[p][:, 0:T], ACT.Copy).then_inc(xT, 1)
                act.wait_ge(neg, b + 1)
                act.activation(EX[:], LG[:, p], ACT.Exp, bias=NEG[:, p], accum_out=SE[:, p]).then_inc(se, 1)
                act.wait_ge(se, b + 1)

            each_batch(act, f)

        @n.block.tensor
        def _(pe):
            pe.wait_ge(loaded, 16)
            pe.wait_ge(ohs0, 1)

            def f(b, p, turn):
                pe.wait_ge(s["xn"], b + 1)
                pe.transpose(bank[p][:, 0:T], XN[:, p], n.CF[:, CI:CI + 128]).then_inc(xT_ps, 1)
                pe.wait_ge(xT, b + 1)
                if not (type(b) is int and b < 2):
                    pe.wait_ge(lg, b - 1)
                pe.matmul(bank[2 + p][:, 0:E], XT[:, p], WR[:], start=True, stop=True).then_inc(l_ps, 1)
                pe.wait_ge(oh, 2 * b + 1)
                pe.matmul(bank[4 + p][:, 0:E], n.CB[:, BTRI:BTRI + 128], OH[:, p], start=True, stop=False)
                pe.matmul(bank[4 + p][:, 0:E], n.CB[:, BONE:BONE + 128], OHS[:, p], start=False, stop=True).then_inc(pos_ps, 1)

            each_batch(pe, f)

        @n.block.vector
        def _(dve):
            dve.wait_ge(ohs0, 1)

            def f(b, p, turn):
                if not (type(b) is int and b < 2):
                    dve.wait_ge(scattered[p], 16 * turn)
                norm_vector(dve, n, b, XN[:, p], stats, s)
                x = n.X[:, cols(b, C)]
                dve.wait_ge(s["xn"], b + 1)
                dve.tensor_tensor(x, x, XN[:, p], ALU.add).then_inc(steps, 1)
                dve.wait_ge(l_ps, b + 1)
                dve.tensor_copy(LG[:, p], bank[2 + p][:, 0:E]).then_inc(lg, 1)
                carry_wait(dve, n, lg, b + 1, stats[:, 10:11])
                dve.max(TOP[:], LG[:, p]).then_inc(top, 1)
                carry_wait(dve, n, top, b + 1, stats[:, 10:11])
                dve.max_index(IDX[:], TOP[:], LG[:, p]).then_inc(idx, 1)
                dve.tensor_scalar(NEG[:, p], TOP[:, 0:1], -1.0, None, ALU.mult).then_inc(neg, 1)
                dve.wait_ge(idx, b + 1)
                dve.tensor_copy(IDF[:], IDX[:, 0:1]).then_inc(steps, 1)
                dve.wait_ge(steps, NS * b + 2)
                dve.tensor_scalar(OH[:, p], n.CF[:, CIOTA:CIOTA + E], IDF[:], None, ALU.is_equal).then_inc(oh, 1)
                dve.wait_ge(pos_ps, b + 1)
                dve.wait_ge(oh, 2 * b + 1)
                dve.tensor_tensor(OHS[:, 1 - p], OHS[:, p], OH[:, p], ALU.add).then_inc(oh, 1)
                dve.tensor_tensor(PC[:], bank[4 + p][:, 0:E], OH[:, p], ALU.mult).then_inc(steps, 1)
                dve.wait_ge(steps, NS * b + 3)
                dve.tensor_reduce(CNT[:], PC[:], AX.X, ALU.add).then_inc(steps, 1)
                dve.wait_ge(steps, NS * b + 4)
                dve.tensor_scalar(OV[:], CNT[:], CAP0 + 0.5, BIG, ALU.is_gt, ALU.mult).then_inc(steps, 1)
                dve.scalar_tensor_tensor(SL[:], IDF[:], float(CAP0), CNT[:], ALU.mult, ALU.add).then_inc(steps, 1)
                dve.wait_ge(steps, NS * b + 6)
                dve.scalar_tensor_tensor(SLI[:, p], SL[:], -1.0, OV[:], ALU.add, ALU.add).then_inc(slot, 1)
                dve.wait_ge(slot, b + 1)
                dve.tensor_copy(n.SLOT[:, cols(b, 1)], SLI[:, p]).then_inc(steps, 1)
                dve.wait_ge(se, b + 1)
                dve.reciprocal(n.GATE[:, cols(b, 1)], SE[:, p]).then_inc(steps, 1)
                dve.wait_ge(oh, 2 * b + 2)
                dve.tensor_copy(OHS[:, p], OHS[:, 1 - p]).then_inc(steps, 1)
                dve.wait_ge(steps, NS * b + 9)

            each_batch(dve, f)


def experts0(nc, w, n):
    NG, K = E // 4, 4
    with ExitStack() as ctx:
        sb, sem = buffers(nc, ctx, "e0_")
        ROWS, BT = sb("ROWS", [128, 10 * C]), sb("BT", [128, E * CAP0])
        WG, WU, WD = (sb(k, [128, 2, K * 128]) for k in ("WG", "WU", "WD"))
        SG, HT, Y = sb("SG", [128, 2, K * CAP0]), sb("HT", [128, 2, K * CAP0]), sb("Y", [CAP0, 2, K * C])
        ps = ctx.enter_context(nc.psum_tensor("e0_ps", [128, 8 * BANK], F32))
        bank = [ps[:, k * BANK:(k + 1) * BANK] for k in range(8)]
        rows, rT_ps, bT = sem("rows"), sem("rT_ps"), sem("bT")
        w_in = [sem("w_even"), sem("w_odd")]
        y_out = [sem("y_even"), sem("y_odd")]
        gu_ps, silu, h, y_ps, y = (sem(k) for k in ("gu_ps", "silu", "h", "y_ps", "y"))

        def each_group(eng, f, ahead=None):
            if ahead:
                ahead(0, 0, 0)
                both = lambda g, p, t, gn, tn: (ahead(gn, 1 - p, tn), f(g, p, t))
                both(0, 0, 0, 1, 0)
                with eng.Fori(1, NG // 2) as i:
                    both(2 * i - 1, 1, i - 1, 2 * i, i)
                    both(2 * i, 0, i, 2 * i + 1, i)
                f(NG - 1, 1, NG // 2 - 1)
            else:
                f(0, 0, 0)
                f(1, 1, 0)
                with eng.Fori(1, NG // 2) as i:
                    f(2 * i, 0, i)
                    f(2 * i + 1, 1, i)

        @nc_block(nc, ctx).sync
        def _(sp):
            sp.dma_start(ROWS[:].rearrange("p (k c) -> p k c", c=C), n.buf_dram.rearrange("(k p) c -> p k c", p=128)).then_inc(rows, 16)

            def f(g, p, turn):
                if not (type(g) is int and g < 2):
                    sp.wait_ge(y_ps, g - 1)
                for dst, name in ((WG, "gate"), (WU, "up"), (WD, "down")):
                    sp.dma_start(dst[:, p].rearrange("h (e f) -> h e f", e=K),
                                 w["L0_ffn_w_" + name][bass.ds(g * K, K)].rearrange("e h f -> h e f")).then_inc(w_in[p], 16)

            each_group(sp, f)

        @n.block.gpsimd
        def _(pool):
            def f(g, p, turn):
                pool.wait_ge(y, g + 1)
                pool.dma_start(n.y_dram[cols(g, K * CAP0), :].rearrange("(e c) d -> c e d", e=K),
                               Y[:, p].rearrange("c (e d) -> c e d", e=K)).then_inc(y_out[p], 16)

            each_group(pool, f)
            for p in range(2):
                pool.wait_ge(y_out[p], 16 * NG // 2)

        @n.block.scalar
        def _(act):
            for k in range(3):
                act.wait_ge(rT_ps, k + 1)
                m = min(4, 10 - 4 * k) * 128
                act.activation(BT[:, k * 512:k * 512 + m], bank[6 + k % 2][:, 0:m], ACT.Copy).then_inc(bT, 1)

            def f(g, p, turn):
                act.wait_ge(gu_ps, g + 1)
                act.activation(SG[:, p], bank[2 * p][:, 0:K * CAP0], ACT.Silu).then_inc(silu, 1)
                act.wait_ge(y_ps, g + 1)
                if not (type(g) is int and g < 2):
                    act.wait_ge(y_out[p], 16 * turn)
                act.activation(Y[:, p], bank[4 + p][0:CAP0, :], ACT.Copy).then_inc(y, 1)

            each_group(act, f)

        @n.block.tensor
        def _(pe):
            pe.wait_ge(rows, 16)
            for k in range(3):
                if k == 2:
                    pe.wait_ge(bT, 1)
                for j in range(min(4, 10 - 4 * k)):
                    last = pe.transpose(bank[6 + k % 2][:, j * 128:(j + 1) * 128], ROWS[:, (4 * k + j) * C:(4 * k + j + 1) * C], n.CF[:, CI:CI + 128])
                last.then_inc(rT_ps, 1)
            pe.wait_ge(bT, 3)

            def gate_up(g, p, turn):
                pe.wait_ge(w_in[p], 48 * (turn + 1))
                if not (type(g) is int and g < 2):
                    pe.wait_ge(h, g - 1)
                for j in range(K):
                    x = BT[:, bass.ds(g * (K * CAP0) + j * CAP0, CAP0)]
                    pe.matmul(bank[2 * p][:, j * CAP0:(j + 1) * CAP0], WG[:, p, j * 128:(j + 1) * 128], x, start=True, stop=True)
                    last = pe.matmul(bank[2 * p + 1][:, j * CAP0:(j + 1) * CAP0], WU[:, p, j * 128:(j + 1) * 128], x, start=True, stop=True)
                last.then_inc(gu_ps, 1)

            def down(g, p, turn):
                pe.wait_ge(h, g + 1)
                if not (type(g) is int and g < 2):
                    pe.wait_ge(y, g - 1)
                for j in range(K):
                    last = pe.matmul(bank[4 + p][0:CAP0, j * C:(j + 1) * C], HT[:, p, j * CAP0:(j + 1) * CAP0],
                                     WD[:, p, j * 128:(j + 1) * 128], start=True, stop=True)
                last.then_inc(y_ps, 1)

            each_group(pe, down, gate_up)

        @n.block.vector
        def _(dve):
            def f(g, p, turn):
                dve.wait_ge(silu, g + 1)
                if not (type(g) is int and g < 2):
                    dve.wait_ge(y_ps, g - 1)
                dve.tensor_tensor(HT[:, p], bank[2 * p + 1][:, 0:K * CAP0], SG[:, p], ALU.mult).then_inc(h, 1)

            each_group(dve, f)


def combine0(nc, w, n):
    with ExitStack() as ctx:
        sb, sem = buffers(nc, ctx, "c0_")
        GY = sb("GY", [128, B * C])
        cleared, summed = sem("cleared"), sem("summed")
        got = [sem(f"got{b}") for b in range(B)]

        @nc_block(nc, ctx).gpsimd
        def _(pool):
            pool.wait_ge(cleared, 1)
            for b in range(B):
                pool.indirect_dma_start(out=GY[:, b * C:(b + 1) * C], out_offset=None, in_=n.y_dram,
                                        in_offset=bass.IndirectOffsetOnAxis(ap=n.SLOT[:, b:b + 1].bitcast(U32), axis=0),
                                        bounds_check=E * CAP0 - 1, oob_is_err=False).then_inc(got[b], 16)

        @n.block.vector
        def _(dve):
            dve.memset(GY[:], 0.0).then_inc(cleared, 1)
            for b in range(B):
                dve.wait_ge(got[b], 16)
                x = n.X[:, b * C:(b + 1) * C]
                dve.scalar_tensor_tensor(x, GY[:, b * C:(b + 1) * C], n.GATE[:, b:b + 1], x, ALU.mult, ALU.add).then_inc(summed, 1)
            dve.wait_ge(summed, B)


def experts_layer0(nc, w, n):
    route0(nc, w, n)
    experts0(nc, w, n)
    combine0(nc, w, n)


def attention1(nc, w, n, cross):
    SCALE = D ** -0.5
    LK = L if cross else T
    NV = H * (D + 1)
    tag = "x1_" if cross else "a1_"
    with ExitStack() as ctx:
        sb, sem = buffers(nc, ctx, tag)
        stats, XN, XT = sb("stats", [128, 11]), sb("XN", [128, C]), sb("XT", [128, T])
        WO, bo = sb("WO", [128, C]), sb("bo", [128, C])
        if cross:
            WQ, WK, WV = sb("WQ", [128, C]), sb("WK", [CC, C]), sb("WV", [CC, C])
            bq, bk, bv = sb("bq", [128, 1]), sb("bk", [128, 1]), sb("bv", [L, C])
            CT = sb("CT", [CC, 2, L])
        else:
            WQKV, bqkv = sb("WQKV", [128, 3 * C]), sb("bqkv", [128, 3 * C])
            QK, RA, RB, QR = (sb(k, [128, 2 * C]) for k in ("QK", "RA", "RB", "QR"))
        QT, KZ, V = sb("QT", [128, T]), sb("KZ", [128, R * LK]), sb("V", [LK, 2, NV])
        MX, P = sb("MX", [128, H]), sb("P", [128, 2, H * LK])
        PT = sb("PT", [LK, 2, 4 * T])
        RD, CX, CTX = sb("RD", [128, H]), sb("CX", [128, C]), sb("CTX", [128, T])
        ps = ctx.enter_context(nc.psum_tensor(tag + "ps", [128, 8 * BANK], F32))
        bank = [ps[:, k * BANK:(k + 1) * BANK] for k in range(8)]
        s = {k: sem(k) for k in NORM_SEMS}
        loaded, v_ones = sem("loaded"), sem("v_ones")
        ctx_in = [sem("ctx_even"), sem("ctx_odd")]
        xT_ps, xT, proj_ps, v_rows, qk, qr, qkT_ps, qT, kz = (sem(k) for k in ("xT_ps", "xT", "proj_ps", "v_rows", "qk", "qr", "qkT_ps", "qT", "kz"))
        s_ps, mx, sub, p_exp = (sem(k) for k in ("s_ps", "mx", "sub", "p_exp"))
        pT_ps, pT, o_ps, cx, cT_ps, cT, y_ps, x_new = (sem(k) for k in ("pT_ps", "pT", "o_ps", "cx", "cT_ps", "cT", "y_ps", "x_new"))
        scores = ps[:, 0:4 * BANK].rearrange("p (g n) -> p g n", g=4)[:, :, 0:R * LK].rearrange("p g (r l) -> p g r l", r=R)
        NL = 8 if cross else 4
        NSUB = 2 if cross else 1

        @nc_block(nc, ctx).sync
        def _(sp):
            row = lambda a: a.rearrange("(o n) -> o n", o=1)
            if cross:
                for dst, name in ((WQ, "Wq"), (WK, "Wk"), (WV, "Wv"), (WO, "Wo")):
                    sp.dma_start(dst[:], w["L1_xattn_" + name]).then_inc(loaded, 16)
                sp.dma_start(bq[:], w["L1_xattn_bq"].rearrange("(n o) -> n o", o=1)).then_inc(loaded, 16)
                sp.dma_start(bk[:], w["L1_xattn_bk"].rearrange("(n o) -> n o", o=1)).then_inc(loaded, 16)
                sp.dma_start(bv[:], row(w["L1_xattn_bv"]).to_broadcast([L, C])).then_inc(loaded, 16)
                sp.dma_start(bo[:], row(w["L1_xattn_bo"]).to_broadcast([128, C])).then_inc(loaded, 16)

                def a(b, p, turn):
                    if not peel(b, p, 2):
                        sp.wait_ge(proj_ps, b - 1)
                    sp.dma_start(CT[:, p, :], w["ctx_T"][bass.ds(b, 1)].rearrange("o c l -> c (o l)")).then_inc(ctx_in[p], 16)

                each_batch(sp, a)
            else:
                sp.dma_start(WQKV[:], w["L1_attn_wqkv_T"]).then_inc(loaded, 16)
                sp.dma_start(WO[:], w["L1_attn_wp_T"]).then_inc(loaded, 16)
                sp.dma_start(bqkv[:], row(w["L1_attn_bqkv"]).to_broadcast([128, 3 * C])).then_inc(loaded, 16)
                sp.dma_start(bo[:], row(w["L1_attn_bp"]).to_broadcast([128, C])).then_inc(loaded, 16)

        @n.block.gpsimd
        def _(pool):
            pool.memset(V[:], 1.0).then_inc(v_ones, 1)
            batches(pool, lambda b, p: norm_pool(pool, n, b + 1, stats, s), lambda: norm_pool(pool, n, 0, stats, s), lambda: None)

        @n.block.scalar
        def _(act):
            def a_xt(b, p):
                act.wait_ge(xT_ps, b + 1)
                act.activation(XT[:], bank[4][:, 0:T], ACT.Copy).then_inc(xT, 1)

            def a_q(b, p):
                if cross:
                    act.wait_ge(proj_ps, b + 1)
                    act.activation(QT[:], bank[4][:, 0:T], ACT.Identity, bias=bq[:]).then_inc(qT, 1)
                else:
                    act.wait_ge(qkT_ps, b + 1)
                    act.activation(QT[:], bank[4][:, 0:T], ACT.Copy).then_inc(qT, 1)

            def a_exp(b, p):
                act.wait_ge(sub, NSUB * (b + 1))
                act.activation(P[:, p, :], P[:, p, :], ACT.Exp, scale=SCALE).then_inc(p_exp, 1)

            def b_pt(b, p, g):
                act.wait_ge(pT_ps, 4 * b + g + 1)
                if not peel(b, g, 2):
                    act.wait_ge(o_ps, 4 * b + g - 1)
                act.activation(PT[:, g % 2, :], bank[6][0:LK, :], ACT.Copy).then_inc(pT, 1)

            def b_ctx(b):
                act.wait_ge(cT_ps, b + 1)
                act.activation(CTX[:], bank[6][:, 0:T], ACT.Copy).then_inc(cT, 1)

            def a_then_b(b, p):
                b_pt(b, p, 0)
                a_xt(b + 1, 1 - p)
                b_pt(b, p, 1)
                b_pt(b, p, 2)
                b_pt(b, p, 3)
                a_q(b + 1, 1 - p)
                b_ctx(b)
                a_exp(b + 1, 1 - p)

            def last():
                for g in range(4):
                    b_pt(B - 1, 1, g)
                b_ctx(B - 1)

            batches(act, a_then_b, lambda: (a_xt(0, 0), a_q(0, 0), a_exp(0, 0)), last)

        @n.block.tensor
        def _(pe):
            ident = n.CF[:, CI:CI + 128]

            def a_xt(b, p):
                pe.wait_ge(s["xn"], b + 1)
                if not peel(b, 0, 1):
                    pe.wait_ge(qT, b)
                    pe.wait_ge(kz, b)
                pe.transpose(bank[4][:, 0:T], XN[:], ident).then_inc(xT_ps, 1)

            def a_proj(b, p, turn):
                pe.wait_ge(xT, b + 1)
                if cross:
                    pe.wait_ge(ctx_in[p], 16 * (turn + 1))
                    pe.matmul(bank[4][:, 0:T], WQ[:], XT[:], start=True, stop=True)
                    pe.matmul(bank[5][:, 0:L], WK[:], CT[:, p, :], start=True, stop=True)
                    pe.matmul(bank[5][0:L, 128:128 + C], CT[:, p, :], WV[:], start=True, stop=True).then_inc(proj_ps, 1)
                else:
                    pe.matmul(bank[5][:, 0:3 * C], XT[:], WQKV[:], start=True, stop=True).then_inc(proj_ps, 1)

            def a_qkt(b, p):
                if not cross:
                    pe.wait_ge(qr, 4 * (b + 1))
                    pe.transpose(bank[4][:, 0:T], QR[:, 0:C], ident)
                    pe.transpose(bank[5][:, 0:T], QR[:, C:2 * C], ident).then_inc(qkT_ps, 1)

            def a_scores(b, p):
                pe.wait_ge(qT, b + 1)
                pe.wait_ge(kz, b + 1)
                if not peel(b, 0, 1):
                    pe.wait_ge(sub, NSUB * b)
                for g in range(G):
                    rows = slice(32 * g, 32 * g + 32)
                    last = pe.matmul(bank[g][:, 0:R * LK], QT[rows, :], KZ[rows, :], start=True, stop=cross)
                if not cross:
                    for g in range(G):
                        last = pe.matmul(bank[g].rearrange("p (r l) -> p r l", r=R), n.CB[:, BI:BI + 128],
                                         n.CB[:, BNEG:BNEG + 128].unsqueeze(1).to_broadcast([128, R, T]), start=False, stop=True)
                last.then_inc(s_ps, 1)

            def b_pt(b, p, g):
                if g == 0:
                    pe.wait_ge(p_exp, b + 1)
                    if not peel(b, 0, 1):
                        pe.wait_ge(cT, b)
                        pe.wait_ge(x_new, 2 * b)
                else:
                    pe.wait_ge(pT, 4 * b + g)
                for r in range(R):
                    h = R * g + r
                    last = pe.transpose(bank[6][0:LK, r * T:(r + 1) * T], P[:, p, h * LK:(h + 1) * LK], ident)
                last.then_inc(pT_ps, 1)

            def b_pv(b, p, g):
                pe.wait_ge(pT, 4 * b + g + 1)
                if g == 0:
                    pe.wait_ge(v_rows, b + 1)
                for r in range(R):
                    h = R * g + r
                    last = pe.matmul(bank[7][:, h * (D + 1):(h + 1) * (D + 1)], PT[:, g % 2, r * T:(r + 1) * T],
                                     V[:, p, h * (D + 1):(h + 1) * (D + 1)], start=True, stop=True)
                last.then_inc(o_ps, 1)

            def b_out(b):
                pe.wait_ge(cx, 2 * (b + 1))
                pe.transpose(bank[6][:, 0:T], CX[:], ident).then_inc(cT_ps, 1)
                pe.wait_ge(cT, b + 1)
                pe.matmul(bank[7][:, 256:256 + C], CTX[:], WO[:], start=True, stop=True).then_inc(y_ps, 1)

            pe.wait_ge(loaded, 16 * NL)
            pe.wait_ge(v_ones, 1)

            def a_then_b(b, p, next_turn):
                b_pt(b, p, 0)
                a_xt(b + 1, 1 - p)
                b_pv(b, p, 0)
                b_pt(b, p, 1)
                a_proj(b + 1, 1 - p, next_turn)
                b_pv(b, p, 1)
                b_pt(b, p, 2)
                b_pv(b, p, 2)
                b_pt(b, p, 3)
                b_pv(b, p, 3)
                a_qkt(b + 1, 1 - p)
                a_scores(b + 1, 1 - p)
                b_out(b)

            a_xt(0, 0), a_proj(0, 0, 0), a_qkt(0, 0), a_scores(0, 0)
            a_then_b(0, 0, 0)
            with pe.Fori(0, (B - 2) // 2) as i:
                a_then_b(2 * i + 1, 1, i + 1)
                a_then_b(2 * i + 2, 0, i + 1)
            for g in range(4):
                b_pt(B - 1, 1, g)
                b_pv(B - 1, 1, g)
            b_out(B - 1)

        @n.block.vector
        def _(dve):
            def a_norm(b, p):
                norm_vector(dve, n, b, XN[:], stats, s)

            def a_proj(b, p):
                dve.wait_ge(proj_ps, b + 1)
                v = V[:, p].rearrange("p (h k) -> p h k", k=D + 1)[:, :, 0:D]
                if cross:
                    kz4 = KZ[:].rearrange("p (r l) -> p r l", r=R)
                    dve.scalar_tensor_tensor(kz4, bank[5][:, 0:L].unsqueeze(1).to_broadcast([128, R, L]), bk[:],
                                             n.CF[:, CHM:CHM + R].unsqueeze(2).to_broadcast([128, R, L]), ALU.add, ALU.mult).then_inc(kz, 1)
                    dve.tensor_tensor(v, bank[5][0:L, 128:128 + C].rearrange("p (h d) -> p h d", d=D),
                                      bv[:].rearrange("p (h d) -> p h d", d=D), ALU.add).then_inc(v_rows, 1)
                else:
                    dve.tensor_tensor(QK[:], bank[5][:, 0:2 * C], bqkv[:, 0:2 * C], ALU.add).then_inc(qk, 1)
                    dve.tensor_tensor(v, bank[5][:, 2 * C:3 * C].rearrange("p (h d) -> p h d", d=D),
                                      bqkv[:, 2 * C:3 * C].rearrange("p (h d) -> p h d", d=D), ALU.add).then_inc(v_rows, 1)
                    dve.wait_ge(qk, b + 1)
                    rope(dve, QK[:], RA[:], RB[:], QR[:], 2 * H, n, qr, 4 * b)

            def a_kz(b, p):
                if not cross:
                    dve.wait_ge(qkT_ps, b + 1)
                    dve.tensor_tensor(KZ[:].rearrange("p (r l) -> p r l", r=R), bank[5][:, 0:T].unsqueeze(1).to_broadcast([128, R, T]),
                                      n.CF[:, CHM:CHM + R].unsqueeze(2).to_broadcast([128, R, T]), ALU.mult).then_inc(kz, 1)

            def a_softmax(b, p):
                dve.wait_ge(s_ps, b + 1)
                p4 = P[:, p, :].rearrange("p (g r l) -> p g r l", g=4, l=LK)
                m3 = MX[:].rearrange("p (g r) -> p g r", g=4)
                dve.tensor_reduce(m3, scores, AX.X, ALU.max).then_inc(mx, 1)
                top = m3.unsqueeze(3).to_broadcast([128, 4, R, LK])
                if cross:
                    lim = 10000.0 / SCALE
                    dve.tensor_scalar(p4, scores, lim, -lim, ALU.min, ALU.max).then_inc(sub, 1)
                    dve.wait_ge(mx, 2 * b + 1)
                    dve.tensor_scalar(MX[:], MX[:], lim, -lim, ALU.min, ALU.max).then_inc(mx, 1)
                    dve.wait_ge(mx, 2 * b + 2)
                    dve.wait_ge(sub, 2 * b + 1)
                    dve.tensor_tensor(p4, p4, top, ALU.subtract).then_inc(sub, 1)
                else:
                    dve.wait_ge(mx, b + 1)
                    dve.tensor_tensor(p4, scores, top, ALU.subtract).then_inc(sub, 1)

            def b_cx(b):
                dve.wait_ge(o_ps, 4 * (b + 1))
                o = bank[7][:, 0:NV].rearrange("p (h k) -> p h k", k=D + 1)
                dve.reciprocal(RD[:].unsqueeze(2), o[:, :, D:D + 1]).then_inc(cx, 1)
                dve.wait_ge(cx, 2 * b + 1)
                dve.tensor_tensor(CX[:].rearrange("p (h d) -> p h d", d=D), o[:, :, 0:D],
                                  RD[:].unsqueeze(2).to_broadcast([128, H, D]), ALU.mult).then_inc(cx, 1)

            def b_out(b):
                dve.wait_ge(y_ps, b + 1)
                x = n.X[:, cols(b, C)]
                dve.tensor_tensor(x, bank[7][:, 256:256 + C], x, ALU.add).then_inc(x_new, 1)
                dve.wait_ge(x_new, 2 * b + 1)
                dve.tensor_tensor(x, x, bo[:], ALU.add).then_inc(x_new, 1)

            dve.wait_ge(loaded, 16 * NL)
            dve.wait_ge(v_ones, 1)

            def a_then_b(b, p):
                a_norm(b + 1, 1 - p)
                a_proj(b + 1, 1 - p)
                b_cx(b)
                a_kz(b + 1, 1 - p)
                a_softmax(b + 1, 1 - p)
                b_out(b)

            def last():
                b_cx(B - 1)
                b_out(B - 1)
                dve.wait_ge(x_new, 2 * B)

            batches(dve, a_then_b, lambda: (a_norm(0, 0), a_proj(0, 0), a_kz(0, 0), a_softmax(0, 0)), last)


def self_attention1(nc, w, n):
    attention1(nc, w, n, cross=False)


def cross_attention1(nc, w, n):
    attention1(nc, w, n, cross=True)


def route1(nc, w, n):
    with ExitStack() as ctx:
        sb, sem = buffers(nc, ctx, "r1_")
        WR = sb("WR", [128, E])
        stats, XN, XT = sb("stats", [128, 11]), sb("XN", [128, C]), sb("XT", [128, 2, T])
        LG, TOP, IDX, NEG, IDF = sb("LG", [128, 2, E]), sb("TOP", [128, 8]), sb("IDX", [128, 8], U32), sb("NEG", [128, 2, 1]), sb("IDF", [128, 8])
        EX, SE, RS, W, A, R1, R2 = sb("EX", [128, 2, E]), sb("SE", [128, 2, 1]), sb("RS", [128, 1]), sb("W", [128, E]), sb("A", [128, E]), sb("R1", [128, E]), sb("R2", [128, E])
        SEL, SELS = sb("SEL", [128, 2, E], BF16), sb("SELS", [128, 2, E], BF16)
        S4 = sb("S4", [128, E])
        WS = sb("WS", [128, 2, 3 * E], BF16)
        ps = ctx.enter_context(nc.psum_tensor("r1_ps", [128, 7 * BANK], F32))
        psb = ctx.enter_context(nc.psum_tensor("r1_psb", [128, 2 * BANK], BF16))
        bank = [ps[:, k * BANK:(k + 1) * BANK] for k in range(7)]
        s = {k: sem(k) for k in NORM_SEMS}
        loaded, sels0 = sem("loaded"), sem("sels0")
        xT_ps, xT, xta, l_ps, lg, top, idx, neg, se, selected, pos_ps, parts, steps, wT_ps, wT = (
            sem(k) for k in ("xT_ps", "xT", "xta", "l_ps", "lg", "top", "idx", "neg", "se", "selected", "pos_ps", "parts", "steps", "wT_ps", "wT"))
        NS, NP = 7, 5

        @nc_block(nc, ctx).sync
        def _(sp):
            sp.dma_start(WR[:], w["L1_ffn_Wg"]).then_inc(loaded, 16)

        @n.block.gpsimd
        def _(pool):
            pool.memset(SELS[:], 0.0).then_inc(sels0, 1)

            def f(b, p, turn):
                norm_pool(pool, n, b, stats, s)

            each_batch(pool, f)

        @n.block.scalar
        def _(act):
            def f(b, p, turn):
                act.wait_ge(xT_ps, b + 1)
                act.activation(XT[:, p], bank[p][:, 0:T], ACT.Copy).then_inc(xT, 1)
                act.activation(n.XTA[:, cols(b, T)], bank[p][:, 0:T], ACT.Copy).then_inc(xta, 1)
                act.wait_ge(neg, b + 1)
                act.activation(EX[:, p], LG[:, p], ACT.Exp, bias=NEG[:, p], accum_out=SE[:, p]).then_inc(se, 1)
                act.wait_ge(wT_ps, b + 1)
                act.activation(n.WT[:, cols(b, T)], psb[0:96, 0:T], ACT.Copy).then_inc(wT, 1)
                act.wait_ge(se, b + 1)

            each_batch(act, f)
            act.wait_ge(wT, B)
            act.wait_ge(xta, B)

        @n.block.tensor
        def _(pe):
            pe.wait_ge(loaded, 16)
            pe.wait_ge(sels0, 1)

            def f(b, p, turn):
                pe.wait_ge(s["xn"], b + 1)
                if not (type(b) is int and b < 2):
                    pe.wait_ge(xta, b - 1)
                pe.transpose(bank[p][:, 0:T], XN[:], n.CF[:, CI:CI + 128]).then_inc(xT_ps, 1)
                pe.wait_ge(xT, b + 1)
                if not (type(b) is int and b < 2):
                    pe.wait_ge(lg, b - 1)
                pe.matmul(bank[2 + p][:, 0:E], XT[:, p], WR[:], start=True, stop=True).then_inc(l_ps, 1)
                pe.wait_ge(selected, 2 * b + 1)
                pe.matmul(bank[4 + p][:, 0:E], n.CB[:, BTRI:BTRI + 128], SEL[:, p], start=True, stop=False)
                pe.matmul(bank[4 + p][:, 0:E], n.CB[:, BONE:BONE + 128], SELS[:, p], start=False, stop=True).then_inc(pos_ps, 1)
                pe.wait_ge(parts, NP * (b + 1))
                if not (type(b) is int and b == 0):
                    pe.wait_ge(wT, b)
                pe.transpose(psb[0:96, 0:T], WS[:, p], n.CB[:, BI:BI + 128]).then_inc(wT_ps, 1)

            each_batch(pe, f)

        @n.block.vector
        def _(dve):
            dve.wait_ge(sels0, 1)

            def f(b, p, turn):
                if not (type(b) is int and b == 0):
                    dve.wait_ge(xT_ps, b)
                norm_vector(dve, n, b, XN[:], stats, s)
                dve.wait_ge(l_ps, b + 1)
                dve.tensor_copy(LG[:, p], bank[2 + p][:, 0:E]).then_inc(lg, 1)
                carry_wait(dve, n, lg, b + 1, stats[:, 10:11])
                dve.max(TOP[:], LG[:, p]).then_inc(top, 1)
                carry_wait(dve, n, top, b + 1, stats[:, 10:11])
                dve.max_index(IDX[:], TOP[:], LG[:, p]).then_inc(idx, 1)
                dve.tensor_scalar(NEG[:, p], TOP[:, 0:1], -1.0, None, ALU.mult).then_inc(neg, 1)
                dve.wait_ge(idx, b + 1)
                dve.tensor_copy(IDF[:], IDX[:]).then_inc(steps, 1)
                dve.wait_ge(steps, NS * b + 1)
                dve.tensor_scalar(S4[:], n.CF[:, CIOTA:CIOTA + E], IDF[:, 0:1], None, ALU.is_equal).then_inc(steps, 1)
                for k in range(1, TOPK):
                    dve.wait_ge(steps, NS * b + 1 + k)
                    dve.scalar_tensor_tensor(S4[:], n.CF[:, CIOTA:CIOTA + E], IDF[:, k:k + 1], S4[:], ALU.is_equal, ALU.add).then_inc(steps, 1)
                dve.wait_ge(steps, NS * b + 5)
                dve.tensor_copy(SEL[:, p], S4[:]).then_inc(selected, 1)
                dve.wait_ge(se, b + 1)
                dve.reciprocal(RS[:], SE[:, p]).then_inc(steps, 1)
                dve.wait_ge(pos_ps, b + 1)
                dve.scalar_tensor_tensor(A[:], bank[4 + p][:, 0:E], CAP1 + 0.5, S4[:], ALU.is_lt, ALU.mult).then_inc(steps, 1)
                dve.tensor_tensor(SELS[:, 1 - p], SELS[:, p], SEL[:, p], ALU.add).then_inc(selected, 1)
                dve.wait_ge(steps, NS * b + 7)
                dve.scalar_tensor_tensor(W[:], EX[:, p], RS[:], A[:], ALU.mult, ALU.mult).then_inc(parts, 1)
                dve.wait_ge(parts, NP * b + 1)
                dve.tensor_copy(WS[:, p, 0:E], W[:]).then_inc(parts, 1)
                dve.wait_ge(parts, NP * b + 2)
                dve.tensor_tensor(R1[:], W[:], WS[:, p, 0:E], ALU.subtract).then_inc(parts, 1)
                dve.wait_ge(parts, NP * b + 3)
                dve.tensor_copy(WS[:, p, E:2 * E], R1[:]).then_inc(parts, 1)
                dve.wait_ge(parts, NP * b + 4)
                dve.tensor_tensor(WS[:, p, 2 * E:3 * E], R1[:], WS[:, p, E:2 * E], ALU.subtract).then_inc(parts, 1)
                dve.wait_ge(selected, 2 * b + 2)

            each_batch(dve, f)


def experts1(nc, w, n, out):
    NP = E // 2
    with ExitStack() as ctx:
        sb, sem = buffers(nc, ctx, "e1_")
        W1, W3, W2 = (sb(k, [128, 2, 128]) for k in ("W1", "W3", "W2"))
        S1, S3, S2 = (sb(k, [128, 128]) for k in ("S1", "S3", "S2"))
        SELF, SELB = sb("SELF", [96, NP * 128]), sb("SELB", [96, NP * 128], BF16)
        SG, HU, HW = (sb(k, [128, 2, BANK]) for k in ("SG", "HU", "HW"))
        YT = sb("YT", [128, B * T])
        ps = ctx.enter_context(nc.psum_tensor("e1_ps", [128, 8 * BANK], F32))
        bank = [ps[:, k * BANK:(k + 1) * BANK] for k in range(8)]
        shared_in, sel_ready = sem("shared_in"), sem("sel_ready")
        w_in = [sem("w_even"), sem("w_odd")]
        gu_ps, wb_ps, silu, hu, hw, y_ps = (sem(k) for k in ("gu_ps", "wb_ps", "silu", "hu", "hw", "y_ps"))
        yT, yr_ps, x_new, stored = sem("yT"), sem("yr_ps"), sem("x_new"), sem("stored")

        @nc_block(nc, ctx).sync
        def _(sp):
            for dst, name in ((S1, "Ws1"), (S3, "Ws3"), (S2, "Ws2")):
                sp.dma_start(dst[:], w["L1_ffn_" + name]).then_inc(shared_in, 16)
            sp.dma_start(SELF[:], w["const_sel"]).then_inc(shared_in, 16)

            def f(i, p, turn):
                if not (type(i) is int and i < 2):
                    sp.wait_ge(y_ps, 2 * i - 1 + 1)
                sp.dma_start(W1[:, p].rearrange("c (e f) -> c e f", e=2), w["L1_ffn_W1"][bass.ds(2 * i, 2)].rearrange("e c f -> c e f")).then_inc(w_in[p], 16)
                sp.dma_start(W3[:, p].rearrange("c (e f) -> c e f", e=2), w["L1_ffn_W3"][bass.ds(2 * i, 2)].rearrange("e c f -> c e f")).then_inc(w_in[p], 16)
                sp.dma_start(W2[:, p], w["L1_ffn_W2"].rearrange("e f d -> (e f) d")[bass.ds(128 * i, 128), :]).then_inc(w_in[p], 16)

            f(0, 0, 0)
            f(1, 1, 0)
            with sp.Fori(1, NP // 2) as i:
                f(2 * i, 0, i)
                f(2 * i + 1, 1, i)
            for b in range(B):
                sp.wait_ge(x_new, b + 1)
                sp.dma_start(out[b], n.X[:, b * C:(b + 1) * C]).then_inc(stored, 16)
            sp.wait_ge(stored, 16 * B)

        def each_pair(eng, shared, f):
            shared()
            with eng.Fori(0, NP) as i:
                f(i)

        @n.block.scalar
        def _(act):
            def half(u, q):
                act.wait_ge(gu_ps, u + 1)
                if not (type(u) is int and u < 2):
                    act.wait_ge(hu, u - 1)
                act.activation(SG[:, q], bank[q], ACT.Silu).then_inc(silu, 1)

            each_pair(act, lambda: (half(0, 0), half(1, 1)), lambda i: (half(2 * i + 2, 0), half(2 * i + 3, 1)))
            for q in range(2):
                act.wait_ge(y_ps, 2 * NP + 1 + q)
                act.activation(YT[:, q * BANK:(q + 1) * BANK], bank[6 + q], ACT.Copy).then_inc(yT, 1)

        @n.block.tensor
        def _(pe):
            def half(u, q, w1, w3, sel):
                x = n.XTA[:, q * BANK:(q + 1) * BANK]
                if not (type(u) is int and u < 2):
                    pe.wait_ge(hu, u - 1)
                pe.matmul(bank[q], w1, x, start=True, stop=True)
                pe.matmul(bank[2 + q], w3, x, start=True, stop=True).then_inc(gu_ps, 1)
                if sel is not None:
                    if not (type(u) is int and u < 4):
                        pe.wait_ge(hw, u - 3)
                    pe.matmul(bank[4 + q], sel, n.WT[:, q * BANK:(q + 1) * BANK], start=True, stop=True).then_inc(wb_ps, 1)

            def down(u, q, w2, start, stop):
                if type(u) is int and u < 2:
                    pe.wait_ge(hu, u + 1)
                else:
                    pe.wait_ge(hw, u - 1)
                pe.matmul(bank[6 + q], w2, HU[:, q] if type(u) is int and u < 2 else HW[:, q], start=start, stop=stop).then_inc(y_ps, 1)

            def pair(i, p, turn, down_w, start):
                pe.wait_ge(w_in[p], 48 * (turn + 1))
                for q in range(2):
                    half(2 * i + 2 + q, q, W1[:, p], W3[:, p], SELB[:, bass.ds(i * 128, 128)])
                    down(2 * i + q, q, down_w, start, False)

            pe.wait_ge(shared_in, 64)
            pe.wait_ge(sel_ready, 1)
            half(0, 0, S1[:], S3[:], None)
            half(1, 1, S1[:], S3[:], None)
            pair(0, 0, 0, S2[:], True)
            with pe.Fori(0, NP // 2 - 1) as t:
                pair(2 * t + 1, 1, t, W2[:, 0], False)
                pair(2 * t + 2, 0, t + 1, W2[:, 1], False)
            pair(NP - 1, 1, NP // 2 - 1, W2[:, 0], False)
            for q in range(2):
                down(2 * NP + q, q, W2[:, 1], False, True)
            pe.wait_ge(hu, 2 * NP + 2)
            for b in range(B):
                pe.wait_ge(yT, b // 4 + 1)
                pe.transpose(bank[b // 4][:, (b % 4) * T:(b % 4 + 1) * T], YT[:, b * T:(b + 1) * T], n.CF[:, CI:CI + 128])\
                    .then_inc(yr_ps, 1)

        @n.block.vector
        def _(dve):
            def shared(u, q):
                dve.wait_ge(silu, u + 1)
                dve.tensor_tensor(HU[:, q], bank[2 + q], SG[:, q], ALU.mult).then_inc(hu, 1)

            def half(u, q):
                dve.wait_ge(silu, u + 1)
                dve.wait_ge(y_ps, u - 1)
                dve.tensor_tensor(HU[:, q], bank[2 + q], SG[:, q], ALU.mult).then_inc(hu, 1)
                dve.wait_ge(wb_ps, u - 1)
                dve.wait_ge(hu, u + 1)
                dve.tensor_tensor(HW[:, q], bank[4 + q], HU[:, q], ALU.mult).then_inc(hw, 1)

            dve.wait_ge(shared_in, 64)
            dve.tensor_copy(SELB[:], SELF[:]).then_inc(sel_ready, 1)
            each_pair(dve, lambda: (shared(0, 0), shared(1, 1)), lambda i: (half(2 * i + 2, 0), half(2 * i + 3, 1)))
            for b in range(B):
                dve.wait_ge(yr_ps, 4 * (b // 4) + 4)
                x = n.X[:, b * C:(b + 1) * C]
                dve.tensor_tensor(x, bank[b // 4][:, (b % 4) * T:(b % 4 + 1) * T], x, ALU.add).then_inc(x_new, 1)


def program(nc, w, out, upto=99, only=0):
    n = Net()
    with ExitStack() as ctx:
        sb, sem = buffers(nc, ctx, "")
        n.X = sb("X", [128, B * C])
        n.CF, n.CB = sb("CF", [128, NCF]), sb("CB", [128, NCB], BF16)
        n.NHALF, n.EPS = sb("NHALF", [128, 1]), sb("EPS", [128, 1])
        n.SINK = sb("SINK", [128, 64 * (D + 1)])
        n.WQX, n.WKX, n.WVX, n.WOX = sb("WQX", [128, 1024]), sb("WKX", [CC, 1024]), sb("WVX", [CC, 1024]), sb("WOX", [128, 1024])
        n.vi_dram = nc.dram_tensor("vi_scratch", (B * LI, 1024), F32, kind="Internal").ap()
        n.buf_dram = nc.dram_tensor("slots_scratch", (E * CAP0, C), F32, kind="Internal").ap()
        n.y_dram = nc.dram_tensor("rows_scratch", (E * CAP0, C), F32, kind="Internal").ap()
        n.SLOT, n.GATE = sb("SLOT", [128, B], I32), sb("GATE", [128, B])
        load_phase(nc, w, n)
        phases = [self_attention0, cross_attention0, experts_layer0, self_attention1, cross_attention1]
        for phase in phases[only:upto]:
            phase(nc, w, n)
        if upto == 99:
            n.XTA, n.WT = sb("XTA", [128, B * T]), sb("WT", [96, B * T], BF16)
            route1(nc, w, n)
            experts1(nc, w, n, out)
        else:
            store_phase(nc, w, n, out)


def constants():
    import numpy as np

    f = np.zeros((128, NCF), np.float32)
    p = np.arange(128)[:, None]
    q = np.arange(128)[None, :]
    f[:, CI:CI + 128] = p == q
    for br, (h, g) in enumerate(((16, 0), (128, 16), (128, 0))):
        f[:, CM + br * 128:CM + (br + 1) * 128] = (q - p >= g) & (q - p < h)
    angle = np.arange(T, dtype=np.float32)[:, None] * (1.0 / np.float32(10000.0) ** (np.arange(0, D, 2, dtype=np.float32) / D))[None, :]
    angle = np.repeat(angle.astype(np.float32), 2, axis=1)
    f[:, CCOS:CCOS + D] = np.cos(angle)
    f[:, CSIN:CSIN + D] = np.sin(angle)
    f[:, CHM:CHM + R] = (p % 32) // D == np.arange(R)[None, :]
    f[:, CIOTA:CIOTA + E] = np.arange(E)[None, :]
    f[:, CONE:CONE + 128] = 1.0
    h = np.zeros((128, NCB), np.float32)
    h[:, BI:BI + 128] = p == q
    h[:, BNEG:BNEG + 128] = np.where(q <= p, 0.0, -1e30)
    h[:, BTRI:BTRI + 128] = p <= q
    h[:, BONE:BONE + 128] = 1.0
    sel = np.zeros((96, 16, 128), np.float32)
    k, i, m = np.arange(96)[:, None, None], np.arange(16)[None, :, None], np.arange(128)[None, None, :]
    sel[:] = k % 32 == 2 * i + m // 64
    return {"const_f32": f, "const_half": h, "const_sel": sel.reshape(96, 2048)}


def layout(inputs):
    import numpy as np

    a = {k: np.asarray(v) for k, v in inputs.items()}
    out = {k: a[k] for k in a if k != "ctx_768"}
    for t in "qkvo":
        out[f"L0_xattn_{t}_down_T"] = a[f"L0_xattn_{t}_down"].T
        del out[f"L0_xattn_{t}_down"]
    out["ctx_T"] = a["ctx_768"].transpose(0, 2, 1)
    out["ctx_img_T"] = a["ctx_768"][:, LO:, :].reshape(B * LI, CC).T
    out["L1_attn_wqkv_T"] = np.concatenate([out.pop(f"L1_attn_w{t}").T for t in "qkv"], axis=1)
    out["L1_attn_bqkv"] = np.concatenate([out.pop(f"L1_attn_b{t}") for t in "qkv"])
    out["L1_attn_wp_T"] = out.pop("L1_attn_wp").T
    out.update(constants())
    return {k: np.ascontiguousarray(v) for k, v in out.items()}


def kernel(**inputs):
    import numpy as np
    import concourse.bacc as bacc
    from concourse.bass_utils import run_bass_kernel_spmd

    nc = bacc.Bacc("TRN2", target_bir_lowering=False, num_devices=1)
    arrays = {f"in_{k}": v for k, v in layout(inputs).items()}
    w = {k[3:]: nc.dram_tensor(k, v.shape, mybir.dt.from_np(v.dtype), kind="ExternalInput").ap() for k, v in arrays.items()}
    out = nc.dram_tensor("out_x", (B, T, C), F32, kind="ExternalOutput").ap()
    program(nc, w, out)
    r = run_bass_kernel_spmd(nc, [arrays], core_ids=[0])
    return r.results[0]["out_x"]
```

```python
from contextlib import ExitStack

import concourse.bass as bass
from concourse import mybir

F32 = mybir.dt.float32
BF16 = mybir.dt.bfloat16
I32 = mybir.dt.int32
U32 = mybir.dt.uint32
ALU = mybir.AluOpType
ACT = mybir.ActivationFunctionType
AX = mybir.AxisListType

B, T, C = 8, 128, 128
H, D = 16, 8
G, R = 4, 4
BR = 4
L, CC = 77, 96
LO, LI = 73, 4
PR, DX = 8, 64
E = 32
NG0 = 8
CAP0 = 40
CAP1 = 512
HID = 64
TOPK = 4
BANK = 512
LN_EPS = 1e-5
RMS_EPS = 1.1920928955078125e-07
BIG = 1.0e6

CI, CM, CCOS, CSIN, CHM, CIOTA, CONE = 0, 128, 512, 520, 528, 532, 564
NCF = 692
BI, BNEG, BTRI, BONE = 0, 128, 256, 384
NCB = 512


def cols(b, n):
    return bass.ds(b * n, n)


class Net:
    pass


def buffers(nc, ctx, tag):
    def sb(name, shape, dt=F32):
        return ctx.enter_context(nc.sbuf_tensor(tag + name, shape, dt))

    own = []

    def sem(name):
        own.append(nc.alloc_semaphore(tag + name))
        return own[-1]

    def clear():
        if own:
            nc.clear_and_free_semaphores(own)
            nc.all_engine_barrier()

    ctx.callback(clear)
    return sb, sem


def peel(b, k, lag):
    return type(b) is int and b == 0 and k < lag


def batches(eng, a_then_b, first, last):
    first()
    a_then_b(0, 0)
    with eng.Fori(0, (B - 2) // 2) as i:
        a_then_b(2 * i + 1, 1)
        a_then_b(2 * i + 2, 0)
    last()


def load_phase(nc, w, n):
    with ExitStack() as ctx:
        sb, sem = buffers(nc, ctx, "ld_")
        small_loaded, x_loaded, lora_loaded = sem("small_loaded"), sem("x_loaded"), sem("lora_loaded")
        folded_ps, folded, psum_used = sem("folded_ps"), sem("folded"), sem("psum_used")
        tanh_done, sink_done, scaled = sem("tanh_done"), sem("sink_done"), sem("scaled")
        kvi_ps, kvi_sb, kvi_stored = sem("kvi_ps"), sem("kvi_sb"), sem("kvi_stored")
        sinks, v_nulls, esink = sb("sinks", [128, 64]), sb("v_nulls", [128, 512]), sb("esink", [128, 64])
        down = [sb(f"down{i}", [32, k]) for i, k in enumerate((C, CC, CC, 1024))]
        up = [sb(f"up{i}", [32, k]) for i, k in enumerate((1024, 1024, 1024, C))]
        alpha = sb("alpha", [128, 4])
        ctx_i = sb("ctx_i", [CC, B * LI])
        wvi = sb("wvi", [CC, 1024])
        vi = sb("vi", [B * LI, 1024])
        half = sb("half", [128, NCB])
        ps = ctx.enter_context(nc.psum_tensor("ld_ps", [128, 8 * BANK], F32))

        @nc_block(nc, ctx).sync
        def _(sp):
            sp.dma_start(n.X[:].rearrange("p (b c) -> p b c", b=B), w["x"].rearrange("b t c -> t b c")).then_inc(x_loaded, 16)
            sp.dma_start(n.CF[:], w["const_f32"]).then_inc(small_loaded, 16)
            sp.dma_start(half[:], w["const_half"]).then_inc(small_loaded, 16)
            sp.dma_start(sinks[:], w["L0_attn_sink_scalars"].rearrange("(o n) -> o n", o=1).to_broadcast([128, 64])).then_inc(small_loaded, 16)
            sp.dma_start(v_nulls[:], w["L0_attn_v_nulls"].rearrange("h d -> (h d)").rearrange("(o n) -> o n", o=1).to_broadcast([128, 512])).then_inc(small_loaded, 16)
            sp.dma_start(n.WQX[:], w["L0_xattn_Wq"]).then_inc(lora_loaded, 16)
            sp.dma_start(n.WKX[:], w["L0_xattn_Wk"]).then_inc(lora_loaded, 16)
            sp.dma_start(n.WVX[:], w["L0_xattn_Wv"]).then_inc(lora_loaded, 16)
            sp.dma_start(n.WOX[:].rearrange("p (j n) -> p j n", j=PR), w["L0_xattn_Wo"].rearrange("(j p) n -> p j n", p=128)).then_inc(lora_loaded, 16)
            sp.wait_ge(kvi_sb, 1)
            sp.dma_start(n.vi_dram, vi[:]).then_inc(kvi_stored, 16)
            sp.wait_ge(kvi_stored, 16)

        @n.block.scalar
        def _(act):
            for i, t in enumerate("qkvo"):
                act.dma_start(down[i][:], w[f"L0_xattn_{t}_down_T"]).then_inc(lora_loaded, 16)
                act.dma_start(up[i][:], w[f"L0_xattn_{t}_up"]).then_inc(lora_loaded, 16)
                act.dma_start(alpha[:, i:i + 1], w[f"L0_xattn_{t}_alpha"].rearrange("(o n) -> o n", o=1).to_broadcast([128, 1])).then_inc(lora_loaded, 16)
            act.dma_start(ctx_i[:], w["ctx_img_T"]).then_inc(lora_loaded, 16)
            act.dma_start(wvi[:], w["L0_xattn_Wv_ipa"]).then_inc(lora_loaded, 16)
            act.wait_ge(small_loaded, 64)
            act.activation(esink[:], sinks[:], ACT.Tanh).then_inc(tanh_done, 1)
            act.wait_ge(tanh_done, 1)
            act.activation(esink[:], esink[:], ACT.Exp).then_inc(sink_done, 1)
            act.wait_ge(kvi_ps, 1)
            act.activation(vi[:], ps[0:B * LI, 6 * BANK:8 * BANK], ACT.Copy).then_inc(kvi_sb, 1)

        @n.block.tensor
        def _(pe):
            pe.wait_ge(lora_loaded, 16 * 18)
            for i in range(3):
                for half in range(2):
                    last = pe.matmul(ps[0:down[i].shape[1], (2 * i + half) * BANK:(2 * i + half + 1) * BANK],
                                     down[i][:], up[i][:, half * BANK:(half + 1) * BANK], start=True, stop=True)
                last.then_inc(folded_ps, 1)
            for half in range(2):
                last = pe.matmul(ps[0:B * LI, (6 + half) * BANK:(7 + half) * BANK], ctx_i[:],
                                 wvi[:, half * BANK:(half + 1) * BANK], start=True, stop=True)
            last.then_inc(kvi_ps, 1)
            pe.wait_ge(folded, 1)
            for j in range(PR):
                last = pe.matmul(ps[:, j * 128:(j + 1) * 128], down[3][:, j * 128:(j + 1) * 128], up[3][:],
                                 start=True, stop=True)
            last.then_inc(folded_ps, 1)

        @n.block.vector
        def _(dve):
            dve.wait_ge(lora_loaded, 16 * 18)
            dve.tensor_scalar(alpha[:], alpha[:], 1.0 / 32, None, ALU.mult).then_inc(scaled, 1)
            dve.wait_ge(scaled, 1)
            for i, (dst, rows) in enumerate(((n.WQX, C), (n.WKX, CC), (n.WVX, CC), (n.WOX, 128))):
                dve.wait_ge(folded_ps, i + 1)
                src = ps[0:rows, 2 * (i % 3) * BANK:2 * (i % 3) * BANK + 1024]
                dve.scalar_tensor_tensor(dst[:], src, alpha[0:rows, i:i + 1], dst[:], ALU.mult, ALU.add).then_inc(folded, 1)
            dve.wait_ge(sink_done, 1)
            row = n.SINK[:].rearrange("p (h k) -> p h k", k=D + 1)
            dve.tensor_tensor(row[:, :, 0:D], v_nulls[:].rearrange("p (h d) -> p h d", d=D),
                              esink[:].unsqueeze(2).to_broadcast([128, 64, D]), ALU.mult).then_inc(folded, 1)
            dve.tensor_copy(row[:, :, D:D + 1], esink[:].unsqueeze(2)).then_inc(folded, 1)
            dve.wait_ge(x_loaded, 16)
            dve.tensor_copy(n.CB[:], half[:]).then_inc(folded, 1)
            dve.wait_ge(folded, 7)
            dve.memset(n.NHALF[:], -0.5).then_inc(tanh_done, 1)
            dve.memset(n.EPS[:], LN_EPS).then_inc(tanh_done, 1)
            dve.wait_ge(tanh_done, 3)


def nc_block(nc, ctx):
    Net.block = ctx.enter_context(nc.Block())
    return Net.block


def norm_stats(dve, n, b, stats, s):
    dve.bn_stats(stats[:, 0:6], n.X[:, cols(b, C)]).then_inc(s["stats"], 1)
    dve.wait_ge(s["stats"], b + 1)
    dve.tensor_copy(stats[:, 10:11], n.EPS[:])
    dve.bn_aggr(stats[:, 6:8], stats[:, 0:6]).then_inc(s["aggr"], 1)


def norm_apply(dve, n, b, dst, stats, s):
    dve.wait_ge(s["rstd"], b + 1)
    dve.tensor_scalar(dst, n.X[:, cols(b, C)], stats[:, 6:7], stats[:, 9:10], ALU.subtract, ALU.mult).then_inc(s["xn"], 1)


def norm_vector(dve, n, b, dst, stats, s):
    norm_stats(dve, n, b, stats, s)
    norm_apply(dve, n, b, dst, stats, s)


def norm_pool(pool, n, b, stats, s):
    pool.wait_ge(s["aggr"], b + 1)
    pool.tensor_tensor(stats[:, 8:9], stats[:, 7:8], n.EPS[:], ALU.add).then_inc(s["var_eps"], 1)
    pool.wait_ge(s["var_eps"], b + 1)
    pool.tensor_tensor(stats[:, 9:10], stats[:, 8:9], n.NHALF[:], ALU.pow).then_inc(s["rstd"], 1)


def norm_all_vector(dve, n, dst, stats, s):
    for b in range(B):
        dve.bn_stats(stats[:, b, 0:6], n.X[:, cols(b, C)]).then_inc(s["stats"], 1)
    dve.wait_ge(s["stats"], B)
    for b in range(B):
        dve.bn_aggr(stats[:, b, 6:8], stats[:, b, 0:6]).then_inc(s["aggr"], 1)
    dve.wait_ge(s["rstd"], 1)
    for b in range(B):
        dve.tensor_scalar(dst[:, b], n.X[:, cols(b, C)], stats[:, b, 6:7], stats[:, b, 9:10], ALU.subtract, ALU.mult).then_inc(s["xn"], 1)


def norm_all_pool(pool, n, stats, s):
    pool.wait_ge(s["aggr"], B)
    pool.tensor_tensor(stats[:, :, 8:9], stats[:, :, 7:8], n.EPS[:].unsqueeze(1).to_broadcast([128, B, 1]), ALU.add).then_inc(s["var_eps"], 1)
    pool.wait_ge(s["var_eps"], 1)
    pool.tensor_tensor(stats[:, :, 9:10], stats[:, :, 8:9], n.NHALF[:].unsqueeze(1).to_broadcast([128, B, 1]), ALU.pow).then_inc(s["rstd"], 1)


NORM_SEMS = ("stats", "aggr", "rstd", "xn", "var_eps")


def rope(dve, src, a, c, dst, nh, n, done, base):
    v = src.rearrange("p (h d) -> p h d", d=D)
    cos = n.CF[:, CCOS:CCOS + D].unsqueeze(1).to_broadcast([128, nh, D])
    sin = n.CF[:, CSIN:CSIN + D].unsqueeze(1).to_broadcast([128, nh, D])
    av = a.rearrange("p (h d) -> p h d", d=D)
    cv = c.rearrange("p (h d) -> p h d", d=D)
    dve.tensor_tensor(av, v, cos, ALU.mult).then_inc(done, 1)
    dve.tensor_tensor(cv, v, sin, ALU.mult).then_inc(done, 1)
    dve.wait_ge(done, base + 2)
    a2 = a.rearrange("p (h t two) -> p h t two", t=D // 2, two=2)
    c2 = c.rearrange("p (h t two) -> p h t two", t=D // 2, two=2)
    o = dst.rearrange("p (h d) -> p h d", d=D)
    dve.tensor_tensor(o[:, :, 0:4], a2[:, :, :, 0], c2[:, :, :, 1], ALU.subtract).then_inc(done, 1)
    dve.tensor_tensor(o[:, :, 4:8], c2[:, :, :, 0], a2[:, :, :, 1], ALU.add).then_inc(done, 1)


def self_attention0(nc, w, n):
    NQ = (BR - 1) * C
    VC = 32
    with ExitStack() as ctx:
        sb, sem = buffers(nc, ctx, "a0_")
        WQ, WK, WV, WO = sb("WQ", [128, NQ]), sb("WK", [128, C]), sb("WV", [128, 512]), sb("WO", [128, C])
        bqk, bv, bo = sb("bqk", [128, 512]), sb("bv", [128, 512]), sb("bo", [128, C])
        stats, XN, XT = sb("stats", [128, 11]), sb("XN", [128, C]), sb("XT", [128, T])
        QK, SQ, RA, RB, QR = (sb(k, [128, 512]) for k in ("QK", "SQ", "RA", "RB", "QR"))
        SS, Y, A1, A2 = (sb(k, [128, 64]) for k in ("SS", "Y", "A1", "A2"))
        SI = sb("SI", [128, 64], I32)
        QT, KZ, V = sb("QT", [128, 2, NQ]), sb("KZ", [128, 2, R, T]), sb("V", [128, 2, BR * H * VC])
        WS, P = sb("WS", [128, 2, 2 * NQ]), sb("P", [128, 2, 2 * NQ])
        OT = sb("OT", [128, 2, NQ])
        NUM, RD, CX, CS, CT = sb("NUM", [128, 2, BR * H * (D + 1)]), sb("RD", [128, 64]), sb("CX", [128, 512]), sb("CS", [128, C]), sb("CT", [128, T])
        ps = ctx.enter_context(nc.psum_tensor("a0_ps", [128, 8 * BANK], F32))
        bank = [ps[:, k * BANK:(k + 1) * BANK] for k in range(8)]
        s = {k: sem(k) for k in NORM_SEMS}
        loaded, v_ones = sem("loaded"), sem("v_ones")
        xT_ps, xT, qkv_ps, qk, v_rows, sq, rs = (sem(k) for k in ("xT_ps", "xT", "qkv_ps", "qk", "v_rows", "sq", "rs"))
        qr, qkT_ps, qT, kz = (sem(k) for k in ("qr", "qkT_ps", "qT", "kz"))
        s_ps, w_done, p_done, pv_done, oT, oR_ps = (sem(k) for k in ("s_ps", "w_done", "p_done", "pv_done", "oT", "oR_ps"))
        v_zero = sem("v_zero")
        num3 = sem("num3")
        num, cs, cT_ps, cT, y_ps, x_new = (sem(k) for k in ("num", "cs", "cT_ps", "cT", "y_ps", "x_new"))
        RS, QRN, CSN = 14, 4, 3

        @nc_block(nc, ctx).sync
        def _(sp):
            sp.dma_start(WQ[:], w["L0_attn_WQ"][:, 0:NQ]).then_inc(loaded, 16)
            sp.dma_start(WK[:], w["L0_attn_WK"]).then_inc(loaded, 16)
            sp.dma_start(WV[:], w["L0_attn_WV"]).then_inc(loaded, 16)
            sp.dma_start(WO[:], w["L0_attn_WO"]).then_inc(loaded, 16)
            row = lambda a: a.rearrange("(o n) -> o n", o=1)
            sp.dma_start(bqk[:, 0:NQ], row(w["L0_attn_bQ"])[:, 0:NQ].to_broadcast([128, NQ])).then_inc(loaded, 16)
            sp.dma_start(bqk[:, NQ:512], row(w["L0_attn_bK"]).to_broadcast([128, C])).then_inc(loaded, 16)
            sp.dma_start(bv[:], row(w["L0_attn_bV"]).to_broadcast([128, 512])).then_inc(loaded, 16)
            sp.dma_start(bo[:], row(w["L0_attn_bO"]).to_broadcast([128, C])).then_inc(loaded, 16)

        @n.block.gpsimd
        def _(pool):
            pool.memset(V[:], 0.0).then_inc(v_zero, 1)
            pool.wait_ge(v_zero, 1)
            pool.memset(V[:].rearrange("p t (h k) -> p (t h) k", k=VC)[:, :, D:D + 1], 1.0).then_inc(v_ones, 1)

            def a(b, p):
                norm_pool(pool, n, b, stats, s)

            batches(pool, lambda b, p: a(b + 1, 1 - p), lambda: a(0, 0), lambda: None)

        @n.block.scalar
        def _(act):
            def a_xt(b, p):
                act.wait_ge(xT_ps, b + 1)
                act.activation(XT[:], bank[4][:, 0:T], ACT.Copy).then_inc(xT, 1)

            def a_sq(b, p):
                act.wait_ge(qk, b + 1)
                act.activation(SQ[:], QK[:], ACT.Square).then_inc(sq, 1)

            def a_qt(b, p):
                act.wait_ge(qkT_ps, b + 1)
                act.activation(QT[:, p], bank[4][:, 0:NQ], ACT.Copy).then_inc(qT, 1)

            def b_pair(b, m):
                act.wait_ge(w_done, 16 * b + 2 * m + 2)
                if not (type(b) is int and b == 0 and m < 2):
                    act.wait_ge(pv_done, 8 * b + m - 1)
                act.activation(P[:, m % 2], WS[:, m % 2], ACT.Exp).then_inc(p_done, 1)

            def b_ctx(b):
                act.wait_ge(cT_ps, b + 1)
                act.activation(CT[:], bank[5][:, 0:T], ACT.Copy).then_inc(cT, 1)

            def b_ot(b, r):
                act.wait_ge(pv_done, 8 * b + 2 * r + 2)
                if not peel(b, r, 2):
                    act.wait_ge(oR_ps, 4 * b + r - 1)
                act.activation(OT[:, r % 2], bank[6 + r % 2][:, 0:NQ], ACT.Copy).then_inc(oT, 1)

            def pairs(b, p, more=True):
                for m in range(8):
                    b_pair(b, m)
                    if m == 0 and not peel(b, 0, 1):
                        b_ot(b - 1, 3)
                    if m in (2, 4, 6):
                        b_ot(b, m // 2 - 1)
                    if m == 1 and more:
                        a_xt(b + 1, 1 - p)
                    if m == 2 and more:
                        a_sq(b + 1, 1 - p)
                    if m == 4 and not peel(b, 0, 1):
                        b_ctx(b - 1)
                    if m == 6 and more:
                        a_qt(b + 1, 1 - p)

            batches(act, pairs, lambda: (a_xt(0, 0), a_sq(0, 0), a_qt(0, 0)),
                    lambda: (pairs(B - 1, 1, False), b_ot(B - 1, 3), b_ctx(B - 1)))

        @n.block.tensor
        def _(pe):
            pe.wait_ge(loaded, 16 * 8)
            ident = n.CF[:, CI:CI + 128]

            def a_xt(b, p):
                pe.wait_ge(s["xn"], b + 1)
                if not (type(b) is int and b == 0):
                    pe.wait_ge(qT, b)
                    pe.wait_ge(kz, b)
                pe.transpose(bank[4][:, 0:T], XN[:], ident).then_inc(xT_ps, 1)

            def a_proj(b, p):
                pe.wait_ge(xT, b + 1)
                pe.matmul(bank[4][:, 0:NQ], XT[:], WQ[:], start=True, stop=True)
                pe.matmul(bank[4][:, NQ:512], XT[:], WK[:], start=True, stop=True)
                pe.matmul(bank[5], XT[:], WV[:], start=True, stop=True).then_inc(qkv_ps, 1)

            def a_qkt(b, p):
                pe.wait_ge(qr, QRN * (b + 1))
                if not (type(b) is int and b < 2):
                    pe.wait_ge(x_new, 2 * (b - 1))
                for j in range(3):
                    pe.transpose(bank[4][:, j * 128:(j + 1) * 128], QR[:, j * 128:(j + 1) * 128], ident)
                pe.transpose(bank[5][:, 0:128], QR[:, NQ:512], ident)
                v3 = V[:, p, 3 * H * VC:].rearrange("p (h k) -> p h k", k=VC)[:, :, 0:D + 1]
                pe.matmul(bank[5][:, 128:272].rearrange("p (h k) -> p h k", k=D + 1), n.CF[:, CONE:CONE + 128], v3, start=True, stop=True).then_inc(qkT_ps, 1)

            def score(b, p, k):
                g, r = k % G, k // G
                if k == 0:
                    pe.wait_ge(qT, b + 1)
                    pe.wait_ge(kz, b + 1)
                if not (type(b) is int and b == 0 and k < 4):
                    pe.wait_ge(w_done, 16 * b + k - 3)
                rows = slice(32 * g, 32 * g + 32)
                pe.matmul(bank[k % 4][:, 0:NQ], KZ[rows, p, r], QT[rows, p], start=True, stop=True).then_inc(s_ps, 1)

            def values(b, p, m):
                r = m // 2
                pe.wait_ge(p_done, 8 * b + m + 1)
                if m == 0:
                    pe.wait_ge(v_rows, b + 1)
                if m % 2 == 0 and not peel(b, r, 2):
                    pe.wait_ge(num, 4 * b + r - 1)
                for k in (2 * m, 2 * m + 1):
                    g = k % G
                    for br in range(3):
                        at = (k % 2) * NQ + br * T
                        v = (br * H + G * g + r) * VC
                        last = pe.matmul(bank[6 + r % 2][32 * g:32 * g + 32, br * T:(br + 1) * T], V[:, p, v:v + VC],
                                         P[:, m % 2, at:at + T], start=True, stop=True)
                last.then_inc(pv_done, 1)

            def turn_back(b, r):
                pe.wait_ge(oT, 4 * b + r + 1)
                for br in range(3):
                    last = pe.transpose(bank[6 + r % 2][:, br * T:(br + 1) * T], OT[:, r % 2, br * T:(br + 1) * T], ident)
                last.then_inc(oR_ps, 1)

            def b_transpose(b):
                pe.wait_ge(cs, CSN * (b + 1))
                pe.transpose(bank[5][:, 0:T], CS[:], ident).then_inc(cT_ps, 1)

            def b_project(b):
                pe.wait_ge(cT, b + 1)
                pe.matmul(bank[5][:, 128:128 + C], CT[:], WO[:], start=True, stop=True).then_inc(y_ps, 1)

            def pairs(b, p, more=True):
                for m in range(8):
                    if m < 6:
                        score(b, p, 2 * m + 4), score(b, p, 2 * m + 5)
                    elif more:
                        score(b + 1, 1 - p, 2 * m - 12), score(b + 1, 1 - p, 2 * m - 11)
                    if m == 1 and more:
                        a_xt(b + 1, 1 - p)
                    if m == 2 and more:
                        a_proj(b + 1, 1 - p)
                    if m == 3 and not peel(b, 0, 1):
                        if more:
                            pe.wait_ge(v_rows, b + 2)
                        b_transpose(b - 1)
                    if m == 4 and not peel(b, 0, 1):
                        b_project(b - 1)
                    if m == 5 and more:
                        a_qkt(b + 1, 1 - p)
                    values(b, p, m)
                    if m == 0 and not peel(b, 0, 1):
                        turn_back(b - 1, 3)
                    if m in (2, 4, 6):
                        turn_back(b, m // 2 - 1)

            def first():
                a_xt(0, 0), a_proj(0, 0), a_qkt(0, 0)
                for k in range(4):
                    score(0, 0, k)

            def last():
                pairs(B - 1, 1, False)
                turn_back(B - 1, 3)
                pe.wait_ge(x_new, 2 * (B - 1))
                b_transpose(B - 1), b_project(B - 1)

            batches(pe, pairs, first, last)

        @n.block.vector
        def _(dve):
            dve.wait_ge(loaded, 16 * 8)
            dve.wait_ge(v_ones, 1)

            def a_bias(b, p):
                dve.wait_ge(qkv_ps, b + 1)
                dve.tensor_tensor(QK[:], bank[4], bqk[:], ALU.add).then_inc(qk, 1)
                out = V[:, p].rearrange("p (h k) -> p h k", k=VC)[:, :, 0:D]
                dve.tensor_tensor(out, bank[5].rearrange("p (h d) -> p h d", d=D), bv[:].rearrange("p (h d) -> p h d", d=D), ALU.add).then_inc(v_rows, 1)

            def a_rms(b, part):
                step = RS * b
                if part == 0:
                    dve.wait_ge(sq, b + 1)
                    dve.tensor_reduce(SS[:], SQ[:].rearrange("p (h d) -> p h d", d=D), AX.X, ALU.add).then_inc(rs, 1)
                    dve.wait_ge(rs, step + 1)
                    dve.tensor_scalar(SS[:, 0:48], SS[:, 0:48], 1.0 / D, RMS_EPS, ALU.mult, ALU.add).then_inc(rs, 1)
                    dve.wait_ge(rs, step + 2)
                    dve.tensor_scalar(SI[:], SS[:].bitcast(I32), 1, None, ALU.arith_shift_right).then_inc(rs, 1)
                    dve.wait_ge(rs, step + 3)
                    dve.tensor_scalar(Y[:].bitcast(I32), SI[:], -1.0, 1597463007.0, ALU.mult, ALU.add).then_inc(rs, 1)
                elif part < 4:
                    k = part - 1
                    dve.wait_ge(rs, step + 4 + 3 * k)
                    dve.tensor_tensor(A1[:], Y[:], Y[:], ALU.mult).then_inc(rs, 1)
                    dve.wait_ge(rs, step + 5 + 3 * k)
                    dve.scalar_tensor_tensor(A2[:], A1[:], -0.5, SS[:], ALU.mult, ALU.mult).then_inc(rs, 1)
                    dve.wait_ge(rs, step + 6 + 3 * k)
                    dve.scalar_tensor_tensor(Y[:], A2[:], 1.5, Y[:], ALU.add, ALU.mult).then_inc(rs, 1)
                else:
                    dve.wait_ge(rs, step + 13)
                    q3 = QK[:].rearrange("p (h d) -> p h d", d=D)
                    dve.tensor_tensor(q3, q3, Y[:].unsqueeze(2).to_broadcast([128, 64, D]), ALU.mult).then_inc(rs, 1)
                    dve.wait_ge(rs, step + 14)

            def a_rope(b, p):
                rope(dve, QK[:], RA[:], RB[:], QR[:], 64, n, qr, QRN * b)

            def a_kz(b, p):
                dve.wait_ge(qkT_ps, b + 1)
                dve.tensor_tensor(NUM[:, p, 432:576], bank[5][:, 128:272], n.SINK[:, 432:576], ALU.add).then_inc(num3, 1)
                dve.tensor_tensor(KZ[:, p], bank[5][:, 0:T].unsqueeze(1).to_broadcast([128, R, T]),
                                  n.CF[:, CHM:CHM + R].unsqueeze(2).to_broadcast([128, R, T]), ALU.mult).then_inc(kz, 1)

            def b_mask(b, k):
                m = k // 2
                dve.wait_ge(s_ps, 16 * b + k + 1)
                if not (type(b) is int and b == 0 and m < 2):
                    dve.wait_ge(p_done, 8 * b + m - 1)
                dve.tensor_tensor(WS[:, m % 2, (k % 2) * NQ:(k % 2 + 1) * NQ], bank[k % 4][:, 0:NQ],
                                  n.CF[:, CM:CM + NQ], ALU.mult).then_inc(w_done, 1)

            def b_num(b, p, r):
                def of_round(a):
                    return a.rearrange("p (br g r k) -> p br g r k", br=BR, g=G, r=R)[:, 0:3, :, r, :]

                dve.wait_ge(oR_ps, 4 * b + r + 1)
                rows = bank[6 + r % 2][:, 0:NQ].rearrange("p (br g k) -> p br g k", br=3, g=G)[:, :, :, 0:D + 1]
                dve.tensor_tensor(of_round(NUM[:, p]), rows, of_round(n.SINK[:]), ALU.add).then_inc(num, 1)

            def b_sums(b, p):
                dve.wait_ge(num, 4 * (b + 1))
                dve.wait_ge(num3, b + 1)
                n3 = NUM[:, p].rearrange("p (h k) -> p h k", k=D + 1)
                dve.reciprocal(RD[:].unsqueeze(2), n3[:, :, D:D + 1]).then_inc(cs, 1)
                dve.wait_ge(cs, CSN * b + 1)
                dve.tensor_tensor(CX[:].rearrange("p (h d) -> p h d", d=D), n3[:, :, 0:D],
                                  RD[:].unsqueeze(2).to_broadcast([128, 64, D]), ALU.mult).then_inc(cs, 1)
                dve.wait_ge(cs, CSN * b + 2)
                dve.tensor_reduce(CS[:], CX[:].rearrange("p (r c) -> p c r", r=BR), AX.X, ALU.add).then_inc(cs, 1)

            def b_out(b):
                dve.wait_ge(y_ps, b + 1)
                x = n.X[:, cols(b, C)]
                dve.scalar_tensor_tensor(x, bank[5][:, 128:128 + C], 1.0 / BR, x, ALU.mult, ALU.add).then_inc(x_new, 1)
                dve.wait_ge(x_new, 2 * b + 1)
                dve.tensor_tensor(x, x, bo[:], ALU.add).then_inc(x_new, 1)

            def masks(b, p, more=True):
                for k in range(16):
                    b_mask(b, k)
                    if k == 3 and not peel(b, 0, 1):
                        b_num(b - 1, 1 - p, 3)
                        b_sums(b - 1, 1 - p)
                    if k in (7, 11, 15):
                        b_num(b, p, k // 4 - 1)
                    if k == 12 and not peel(b, 0, 1):
                        b_out(b - 1)
                    if more:
                        if k == 2:
                            norm_stats(dve, n, b + 1, stats, s)
                        if k == 3:
                            norm_apply(dve, n, b + 1, XN[:], stats, s)
                        if k == 6:
                            a_bias(b + 1, 1 - p)
                        if 7 <= k < 12:
                            a_rms(b + 1, k - 7)
                        if k == 11:
                            a_rope(b + 1, 1 - p)
                        if k == 14:
                            a_kz(b + 1, 1 - p)

            def first():
                norm_vector(dve, n, 0, XN[:], stats, s)
                a_bias(0, 0)
                for part in range(5):
                    a_rms(0, part)
                a_rope(0, 0), a_kz(0, 0)

            def last():
                masks(B - 1, 1, False)
                b_num(B - 1, 1, 3)
                b_sums(B - 1, 1)
                b_out(B - 1)
                dve.wait_ge(x_new, 2 * B)

            batches(dve, masks, first, last)


def cross_attention0(nc, w, n):
    SCALE = DX ** -0.5
    with ExitStack() as ctx:
        sb, sem = buffers(nc, ctx, "x0_")
        WKI, bo = sb("WKI", [CC, 1024]), sb("bo", [128, C])
        stats, XN, XT = sb("stats", [128, 11]), sb("XN", [128, C]), sb("XT", [128, T])
        CT = sb("CT", [CC, 2, L])
        QT, KT, V = sb("QT", [128, PR * T]), sb("KT", [128, PR * L]), sb("V", [L, 2, 1024])
        MX, SM, RD = sb("MX", [128, 2 * H]), sb("SM", [128, 2 * H]), sb("RD", [128, 2 * H])
        P = sb("P", [128, 2, H * L])
        PT, OT = sb("PT", [L, 2, 4 * T]), sb("OT", [128, PR * T])
        ps = ctx.enter_context(nc.psum_tensor("x0_ps", [128, 8 * BANK], F32))
        bank = [ps[:, k * BANK:(k + 1) * BANK] for k in range(8)]
        s = {k: sem(k) for k in NORM_SEMS}
        loaded = sem("loaded")
        ctx_in = [sem("ctx_even"), sem("ctx_odd")]
        vi_in = [sem("vi_even"), sem("vi_odd")]
        xT_ps, xT, q_ps, qT, k_ps, kT, v_ps, v_rows = (sem(k) for k in ("xT_ps", "xT", "q_ps", "qT", "k_ps", "kT", "v_ps", "v_rows"))
        s_ps, mx, sub, p_exp, sm, p_norm = (sem(k) for k in ("s_ps", "mx", "sub", "p_exp", "sm", "p_norm"))
        pT_ps, pT, o_ps, oT, y_ps, x_new = (sem(k) for k in ("pT_ps", "pT", "o_ps", "oT", "y_ps", "x_new"))

        scores = ps[:, 0:4 * BANK].rearrange("p (k n) -> p k n", k=4)[:, :, 0:4 * L].rearrange("p k (h l) -> p k h l", h=4)

        def place(h):
            return 8 * (h % 2) + h // 2

        def spread(a):
            return a.rearrange("p (h t) -> p h t", t=2)

        @nc_block(nc, ctx).sync
        def _(sp):
            sp.dma_start(WKI[:], w["L0_xattn_Wk_ipa"]).then_inc(loaded, 16)
            sp.dma_start(bo[:], w["L0_xattn_bo"].rearrange("(o n) -> o n", o=1).to_broadcast([128, C])).then_inc(loaded, 16)

            def a(b, p, turn):
                if not peel(b, p, 2):
                    sp.wait_ge(o_ps, 4 * (b - 1))
                sp.dma_start(CT[:, p, :], w["ctx_T"][bass.ds(b, 1)].rearrange("o c l -> c (o l)")).then_inc(ctx_in[p], 16)
                sp.dma_start(V[LO:L, p, :], n.vi_dram[cols(b, LI), :]).then_inc(vi_in[p], 16)

            a(0, 0, 0)
            a(1, 1, 0)
            with sp.Fori(1, B // 2) as i:
                a(2 * i, 0, i)
                a(2 * i + 1, 1, i)

        @n.block.gpsimd
        def _(pool):
            batches(pool, lambda b, p: norm_pool(pool, n, b + 1, stats, s), lambda: norm_pool(pool, n, 0, stats, s), lambda: None)

        @n.block.scalar
        def _(act):
            def a_xt(b, p):
                act.wait_ge(xT_ps, b + 1)
                act.activation(XT[:], bank[4][:, 0:T], ACT.Copy).then_inc(xT, 1)

            def a_q(b, p):
                act.wait_ge(q_ps, b + 1)
                act.activation(QT[:], ps[:, 4 * BANK:6 * BANK], ACT.Copy).then_inc(qT, 1)

            def a_k(b, p):
                act.wait_ge(k_ps, b + 1)
                src = ps[:, 4 * BANK:6 * BANK].rearrange("p (k n) -> p k n", k=2)[:, :, 0:4 * L]
                act.activation(KT[:].rearrange("p (k n) -> p k n", k=2), src, ACT.Copy).then_inc(kT, 1)

            def a_v(b, p):
                act.wait_ge(v_ps, b + 1)
                act.activation(V[0:LO, p, :], ps[0:LO, 4 * BANK:6 * BANK], ACT.Copy).then_inc(v_rows, 1)

            def a_exp(b, p):
                act.wait_ge(sub, 2 * (b + 1))
                act.activation(P[:, p, :], P[:, p, :], ACT.Exp, scale=SCALE).then_inc(p_exp, 1)

            def b_pt(b, p, g):
                act.wait_ge(pT_ps, 4 * b + g + 1)
                if not peel(b, g, 2):
                    act.wait_ge(o_ps, 4 * b + g - 1)
                act.activation(PT[:, g % 2, :], bank[6][0:L, :], ACT.Copy).then_inc(pT, 1)

            def a_then_b(b, p):
                b_pt(b, p, 0)
                a_xt(b + 1, 1 - p)
                b_pt(b, p, 1)
                a_q(b + 1, 1 - p)
                b_pt(b, p, 2)
                a_k(b + 1, 1 - p)
                b_pt(b, p, 3)
                a_v(b + 1, 1 - p)
                a_exp(b + 1, 1 - p)

            def first():
                a_xt(0, 0), a_q(0, 0), a_k(0, 0), a_v(0, 0), a_exp(0, 0)

            def last():
                for g in range(4):
                    b_pt(B - 1, 1, g)

            batches(act, a_then_b, first, last)

        @n.block.tensor
        def _(pe):
            ident = n.CF[:, CI:CI + 128]

            def a_xt(b, p):
                pe.wait_ge(s["xn"], b + 1)
                if not peel(b, 0, 1):
                    pe.wait_ge(v_rows, b)
                pe.transpose(bank[4][:, 0:T], XN[:], ident).then_inc(xT_ps, 1)

            def a_q(b, p):
                pe.wait_ge(xT, b + 1)
                for j in range(PR):
                    last = pe.matmul(ps[:, 4 * BANK + j * T:4 * BANK + (j + 1) * T], n.WQX[:, j * 128:(j + 1) * 128], XT[:],
                                     start=True, stop=True)
                last.then_inc(q_ps, 1)

            def a_k(b, p, turn):
                pe.wait_ge(qT, b + 1)
                pe.wait_ge(ctx_in[p], 16 * (turn + 1))
                for j in range(PR):
                    at = (4 + j // 4) * BANK + (j % 4) * L
                    pe.matmul(ps[:, at:at + LO], n.WKX[:, j * 128:(j + 1) * 128], CT[:, p, 0:LO], start=True, stop=True)
                    last = pe.matmul(ps[:, at + LO:at + L], WKI[:, j * 128:(j + 1) * 128], CT[:, p, LO:L], start=True, stop=True)
                last.then_inc(k_ps, 1)

            def a_v(b, p):
                pe.wait_ge(kT, b + 1)
                for half in range(2):
                    last = pe.matmul(ps[0:LO, (4 + half) * BANK:(5 + half) * BANK], CT[:, p, 0:LO],
                                     n.WVX[:, half * BANK:(half + 1) * BANK], start=True, stop=True)
                last.then_inc(v_ps, 1)

            def a_scores(b, p):
                if not peel(b, 0, 1):
                    pe.wait_ge(sub, 2 * b)
                for h in range(H):
                    rows = slice(DX * (h % 2), DX * (h % 2) + DX)
                    j = h // 2
                    at = place(h) // 4 * BANK + place(h) % 4 * L
                    last = pe.matmul(ps[:, at:at + L], QT[rows, j * T:(j + 1) * T], KT[rows, j * L:(j + 1) * L], start=True, stop=True)
                last.then_inc(s_ps, 1)

            def b_pt(b, p, g):
                if g == 0:
                    pe.wait_ge(p_norm, 2 * (b + 1))
                if not peel(b, g, 1):
                    pe.wait_ge(pT, 4 * b + g)
                if g == 0 and not peel(b, 0, 1):
                    pe.wait_ge(x_new, 2 * b)
                for k in range(4):
                    h = 4 * g + k
                    last = pe.transpose(bank[6][0:L, k * T:(k + 1) * T], P[:, p, place(h) * L:(place(h) + 1) * L], ident)
                last.then_inc(pT_ps, 1)

            def b_pv(b, p, g, turn):
                pe.wait_ge(pT, 4 * b + g + 1)
                if g == 0:
                    pe.wait_ge(vi_in[p], 16 * (turn + 1))
                    pe.wait_ge(v_rows, b + 1)
                if not peel(b, g, 1):
                    pe.wait_ge(oT, 4 * b + g)
                for k in range(4):
                    h = 4 * g + k
                    last = pe.matmul(bank[7][DX * (h % 2):DX * (h % 2) + DX, (k // 2) * T:(k // 2 + 1) * T],
                                     V[:, p, h * DX:(h + 1) * DX], PT[:, g % 2, k * T:(k + 1) * T], start=True, stop=True)
                last.then_inc(o_ps, 1)

            def b_out(b):
                pe.wait_ge(oT, 4 * (b + 1))
                for j in range(PR):
                    last = pe.matmul(bank[6][:, 0:C], OT[:, j * T:(j + 1) * T], n.WOX[:, j * C:(j + 1) * C],
                                     start=(j == 0), stop=(j == PR - 1))
                last.then_inc(y_ps, 1)

            pe.wait_ge(loaded, 32)

            def a_then_b(b, p, turn=0, next_turn=0):
                b_pt(b, p, 0)
                a_xt(b + 1, 1 - p)
                b_pv(b, p, 0, turn)
                b_pt(b, p, 1)
                a_q(b + 1, 1 - p)
                b_pv(b, p, 1, turn)
                b_pt(b, p, 2)
                a_k(b + 1, 1 - p, next_turn)
                b_pv(b, p, 2, turn)
                b_pt(b, p, 3)
                a_v(b + 1, 1 - p)
                b_pv(b, p, 3, turn)
                a_scores(b + 1, 1 - p)
                b_out(b)

            a_xt(0, 0), a_q(0, 0), a_k(0, 0, 0), a_v(0, 0), a_scores(0, 0)
            a_then_b(0, 0, 0, 0)
            with pe.Fori(0, (B - 2) // 2) as i:
                a_then_b(2 * i + 1, 1, i, i + 1)
                a_then_b(2 * i + 2, 0, i + 1, i + 1)
            for g in range(4):
                b_pt(B - 1, 1, g)
                b_pv(B - 1, 1, g, B // 2 - 1)
            b_out(B - 1)

        @n.block.vector
        def _(dve):
            def a_norm(b, p):
                norm_vector(dve, n, b, XN[:], stats, s)

            def a_softmax1(b, p):
                dve.wait_ge(s_ps, b + 1)
                m4 = MX[:].rearrange("p (k h t) -> p k h t", k=4, t=2)
                p4 = P[:, p, :].rearrange("p (k h l) -> p k h l", k=4, l=L)
                dve.tensor_reduce(m4[:, :, :, 0], scores[:, :, :, 0:LO], AX.X, ALU.max).then_inc(mx, 1)
                dve.tensor_reduce(m4[:, :, :, 1], scores[:, :, :, LO:L], AX.X, ALU.max).then_inc(mx, 1)
                dve.wait_ge(mx, 2 * (b + 1))
                for t, (lo, hi) in enumerate(((0, LO), (LO, L))):
                    dve.tensor_tensor(p4[:, :, :, lo:hi], scores[:, :, :, lo:hi],
                                      m4[:, :, :, t:t + 1].to_broadcast([128, 4, 4, hi - lo]), ALU.subtract).then_inc(sub, 1)

            def a_softmax2(b, p):
                dve.wait_ge(p_exp, b + 1)
                p3 = P[:, p, :].rearrange("p (h l) -> p h l", l=L)
                sums = spread(SM[:])
                dve.tensor_reduce(sums[:, :, 0], p3[:, :, 0:LO], AX.X, ALU.add).then_inc(sm, 1)
                dve.tensor_reduce(sums[:, :, 1], p3[:, :, LO:L], AX.X, ALU.add).then_inc(sm, 1)
                dve.wait_ge(sm, 3 * b + 2)
                dve.reciprocal(RD[:], SM[:]).then_inc(sm, 1)
                dve.wait_ge(sm, 3 * b + 3)
                rd = spread(RD[:])
                for t, (lo, hi) in enumerate(((0, LO), (LO, L))):
                    dve.tensor_tensor(p3[:, :, lo:hi], p3[:, :, lo:hi], rd[:, :, t:t + 1].to_broadcast([128, H, hi - lo]), ALU.mult).then_inc(p_norm, 1)

            def b_ot(b, g):
                dve.wait_ge(o_ps, 4 * b + g + 1)
                if g == 0 and not peel(b, 0, 1):
                    dve.wait_ge(y_ps, b)
                dve.tensor_copy(OT[:, 2 * g * T:2 * (g + 1) * T], bank[7][:, 0:2 * T]).then_inc(oT, 1)

            def b_out(b):
                dve.wait_ge(y_ps, b + 1)
                x = n.X[:, cols(b, C)]
                dve.tensor_tensor(x, bank[6][:, 0:C], x, ALU.add).then_inc(x_new, 1)
                dve.wait_ge(x_new, 2 * b + 1)
                dve.tensor_tensor(x, x, bo[:], ALU.add).then_inc(x_new, 1)

            dve.wait_ge(loaded, 32)

            def a_then_b(b, p):
                a_norm(b + 1, 1 - p)
                for g in range(4):
                    b_ot(b, g)
                a_softmax1(b + 1, 1 - p)
                b_out(b)
                a_softmax2(b + 1, 1 - p)

            def first():
                a_norm(0, 0), a_softmax1(0, 0), a_softmax2(0, 0)

            def last():
                for g in range(4):
                    b_ot(B - 1, g)
                b_out(B - 1)
                dve.wait_ge(x_new, 2 * B)

            batches(dve, a_then_b, first, last)


def each_batch(eng, f):
    f(0, 0, 0)
    f(1, 1, 0)
    with eng.Fori(1, B // 2) as i:
        f(2 * i, 0, i)
        f(2 * i + 1, 1, i)


def carry_wait(dve, n, sem, value, spare):
    dve.wait_ge(sem, value)
    dve.tensor_copy(spare, n.EPS[:])


def group_weights(w, n, g):
    k = E // NG0
    return [(dst[:, g * k:(g + 1) * k, :], w["L0_ffn_w_" + name][g * k:(g + 1) * k].rearrange("e h f -> h e f"))
            for dst, name in ((n.WG, "gate"), (n.WU, "up"), (n.WD, "down"))]


def route0(nc, w, n):
    with ExitStack() as ctx:
        sb, sem = buffers(nc, ctx, "r0_")
        WR, ZERO = sb("WR", [128, E]), sb("ZERO", [128, 1280])
        stats, XN, XT = sb("stats", [128, B, 10]), sb("XN", [128, B, C]), sb("XT", [128, B * T])
        LG, TOP, IDX, IDF = sb("LG", [128, B, E]), sb("TOP", [128, B, 8]), sb("IDX", [128, B, 8], U32), sb("IDF", [128, B, 1])
        EX, PC = sb("EX", [128, B, E]), sb("PC", [128, B, E])
        SE, CNT, OV, SL = (sb(k, [128, B]) for k in ("SE", "CNT", "OV", "SL"))
        OH = sb("OH", [128, B, E], BF16)
        ps = ctx.enter_context(nc.psum_tensor("r0_ps", [128, 4 * BANK], F32))
        bank = [ps[:, k * BANK:(k + 1) * BANK] for k in range(4)]
        s = {k: sem(k) for k in NORM_SEMS}
        loaded, zeroed, cleared, scattered = sem("loaded"), sem("zeroed"), sem("cleared"), sem("scattered")
        xT_ps, xT, l_ps, lg, top, idx, idf, less, ex, se = (sem(k) for k in ("xT_ps", "xT", "l_ps", "lg", "top", "idx", "idf", "less", "ex", "se"))
        one_hot, pos_ps, own, count, over, slot, x_sum = (sem(k) for k in ("one_hot", "pos_ps", "own", "count", "over", "slot", "x_sum"))
        logits = bank[2][:, 0:B * E].rearrange("p (b e) -> p b e", e=E)
        place = bank[3][:, 0:B * E].rearrange("p (b e) -> p b e", e=E)

        @nc_block(nc, ctx).sync
        def _(sp):
            sp.dma_start(WR[:], w["L0_ffn_w_router"]).then_inc(loaded, 16)
            sp.wait_ge(zeroed, 1)
            sp.dma_start(n.buf_dram.rearrange("(p k) c -> p (k c)", p=128), ZERO[:]).then_inc(cleared, 16)
            for g in range(NG0):
                for dma in group_weights(w, n, g):
                    sp.dma_start(*dma).then_inc(n.w_in[g], 16)
            sp.wait_ge(scattered, 16 * B)

        @n.block.gpsimd
        def _(pool):
            pool.memset(ZERO[:], 0.0).then_inc(zeroed, 1)
            norm_all_pool(pool, n, stats, s)
            pool.wait_ge(s["xn"], B)
            pool.tensor_tensor(n.X[:], n.X[:], XN[:].rearrange("p b c -> p (b c)"), ALU.add).then_inc(x_sum, 1)
            pool.wait_ge(cleared, 16)
            pool.wait_ge(slot, 1)
            for b in range(B):
                pool.indirect_dma_start(out=n.buf_dram, out_offset=bass.IndirectOffsetOnAxis(ap=n.SLOT[:, b:b + 1].bitcast(U32), axis=0),
                                        in_=XN[:, b, :], in_offset=None, bounds_check=E * CAP0 - 1,
                                        oob_is_err=False).then_inc(scattered, 16)
            pool.wait_ge(x_sum, 1)

        @n.block.scalar
        def _(act):
            for q in range(2):
                act.wait_ge(xT_ps, q + 1)
                act.activation(XT[:, q * BANK:(q + 1) * BANK], bank[q], ACT.Copy).then_inc(xT, 1)
            act.wait_ge(less, 1)
            act.activation(EX[:], EX[:], ACT.Exp).then_inc(ex, 1)

        @n.block.tensor
        def _(pe):
            for b in range(B):
                pe.wait_ge(s["xn"], b + 1)
                last = pe.transpose(bank[b // 4][:, (b % 4) * T:(b % 4 + 1) * T], XN[:, b], n.CF[:, CI:CI + 128])
                if b % 4 == 3:
                    last.then_inc(xT_ps, 1)
            pe.wait_ge(loaded, 16)
            for b in range(B):
                pe.wait_ge(xT, b // 4 + 1)
                last = pe.matmul(bank[2][:, b * E:(b + 1) * E], XT[:, b * T:(b + 1) * T], WR[:], start=True, stop=True)
            last.then_inc(l_ps, 1)
            count_places(pe, n, OH, bank[3], one_hot).then_inc(pos_ps, 1)

        @n.block.vector
        def _(dve):
            norm_all_vector(dve, n, XN, stats, s)
            dve.wait_ge(l_ps, 1)
            dve.tensor_copy(LG[:], logits).then_inc(lg, 1)
            dve.wait_ge(lg, 1)
            for b in range(B):
                dve.max(TOP[:, b], LG[:, b]).then_inc(top, 1)
            dve.wait_ge(top, B)
            for b in range(B):
                dve.max_index(IDX[:, b], TOP[:, b], LG[:, b]).then_inc(idx, 1)
            dve.tensor_tensor(EX[:], LG[:], TOP[:, :, 0:1].to_broadcast([128, B, E]), ALU.subtract).then_inc(less, 1)
            dve.wait_ge(idx, B)
            dve.tensor_copy(IDF[:], IDX[:, :, 0:1]).then_inc(idf, 1)
            dve.wait_ge(idf, 1)
            iota = n.CF[:, CIOTA:CIOTA + E].unsqueeze(1).to_broadcast([128, B, E])
            dve.tensor_tensor(OH[:], iota, IDF[:].to_broadcast([128, B, E]), ALU.is_equal).then_inc(one_hot, 1)
            dve.wait_ge(ex, 1)
            dve.tensor_reduce(SE[:], EX[:], AX.X, ALU.add).then_inc(se, 1)
            dve.wait_ge(se, 1)
            dve.reciprocal(n.GATE[:], SE[:]).then_inc(se, 1)
            dve.wait_ge(pos_ps, 1)
            dve.wait_ge(one_hot, 1)
            dve.tensor_tensor(PC[:], place, OH[:], ALU.mult).then_inc(own, 1)
            dve.wait_ge(own, 1)
            dve.tensor_reduce(CNT[:], PC[:], AX.X, ALU.add).then_inc(count, 1)
            dve.wait_ge(count, 1)
            dve.tensor_scalar(OV[:], CNT[:], CAP0 + 0.5, BIG, ALU.is_gt, ALU.mult).then_inc(over, 1)
            dve.scalar_tensor_tensor(SL[:], IDF[:].rearrange("p b o -> p (b o)"), float(CAP0), CNT[:], ALU.mult, ALU.add).then_inc(over, 1)
            dve.wait_ge(over, 2)
            dve.scalar_tensor_tensor(n.SLOT[:], SL[:], -1.0, OV[:], ALU.add, ALU.add).then_inc(slot, 1)
            dve.wait_ge(se, 2)
            dve.wait_ge(slot, 1)


def count_places(pe, n, chosen, bank, ready):
    pe.wait_ge(ready, 1)
    pe.matmul(bank[:, 0:B * E], n.CB[:, BTRI:BTRI + 128], chosen[:].rearrange("p b e -> p (b e)"), start=True, stop=False)
    for b in range(B - 1):
        rest = B - 1 - b
        last = pe.matmul(bank[:, (b + 1) * E:B * E].rearrange("p (b e) -> p b e", e=E), n.CB[:, BONE:BONE + 128],
                         chosen[:, b:b + 1].to_broadcast([128, rest, E]), start=False, stop=b == B - 2)
    return last


def experts0(nc, w, n):
    NG, K = NG0, E // NG0
    with ExitStack() as ctx:
        sb, sem = buffers(nc, ctx, "e0_")
        ROWS, BT = sb("ROWS", [128, 10 * C]), sb("BT", [128, E * CAP0])
        SG, HT, Y = sb("SG", [128, 2, K * CAP0]), sb("HT", [128, 2, K * CAP0]), sb("Y", [CAP0, 2, K * C])
        ps = ctx.enter_context(nc.psum_tensor("e0_ps", [128, 8 * BANK], F32))
        bank = [ps[:, k * BANK:(k + 1) * BANK] for k in range(8)]
        rows, rT_ps, bT = sem("rows"), sem("rT_ps"), sem("bT")
        y_out = [sem("y_even"), sem("y_odd")]
        gu_ps, silu, h, y_ps, y = (sem(k) for k in ("gu_ps", "silu", "h", "y_ps", "y"))

        def each_group(eng, f):
            f(0, 0, 0)
            f(1, 1, 0)
            with eng.Fori(1, NG // 2) as i:
                f(2 * i, 0, i)
                f(2 * i + 1, 1, i)

        @nc_block(nc, ctx).sync
        def _(sp):
            sp.dma_start(ROWS[:].rearrange("p (k c) -> p k c", c=C), n.buf_dram.rearrange("(k p) c -> p k c", p=128)).then_inc(rows, 16)

        @n.block.gpsimd
        def _(pool):
            def f(g, p, turn):
                pool.wait_ge(y, g + 1)
                pool.dma_start(n.y_dram[cols(g, K * CAP0), :].rearrange("(e c) d -> c e d", e=K),
                               Y[:, p].rearrange("c (e d) -> c e d", e=K)).then_inc(y_out[p], 16)

            each_group(pool, f)
            for p in range(2):
                pool.wait_ge(y_out[p], 16 * NG // 2)

        @n.block.scalar
        def _(act):
            for k in range(3):
                act.wait_ge(rT_ps, k + 1)
                m = min(4, 10 - 4 * k) * 128
                act.activation(BT[:, k * 512:k * 512 + m], bank[6 + k % 2][:, 0:m], ACT.Copy).then_inc(bT, 1)

            def f(g, p, turn):
                act.wait_ge(gu_ps, g + 1)
                act.activation(SG[:, p], bank[2 * p][:, 0:K * CAP0], ACT.Silu).then_inc(silu, 1)
                act.wait_ge(y_ps, g + 1)
                if not (type(g) is int and g < 2):
                    act.wait_ge(y_out[p], 16 * turn)
                act.activation(Y[:, p], bank[4 + p][0:CAP0, :], ACT.Copy).then_inc(y, 1)

            each_group(act, f)

        @n.block.tensor
        def _(pe):
            pe.wait_ge(rows, 16)
            for k in range(3):
                if k == 2:
                    pe.wait_ge(bT, 1)
                for j in range(min(4, 10 - 4 * k)):
                    last = pe.transpose(bank[6 + k % 2][:, j * 128:(j + 1) * 128], ROWS[:, (4 * k + j) * C:(4 * k + j + 1) * C], n.CF[:, CI:CI + 128])
                last.then_inc(rT_ps, 1)
            pe.wait_ge(bT, 3)

            def gate_up(g):
                p = g % 2
                pe.wait_ge(n.w_in[g], 48)
                if g >= 2:
                    pe.wait_ge(h, g - 1)
                for j in range(K):
                    e = g * K + j
                    x = BT[:, e * CAP0:(e + 1) * CAP0]
                    pe.matmul(bank[2 * p][:, j * CAP0:(j + 1) * CAP0], n.WG[:, e], x, start=True, stop=True)
                    last = pe.matmul(bank[2 * p + 1][:, j * CAP0:(j + 1) * CAP0], n.WU[:, e], x, start=True, stop=True)
                last.then_inc(gu_ps, 1)

            def down(g):
                p = g % 2
                pe.wait_ge(h, g + 1)
                if g >= 2:
                    pe.wait_ge(y, g - 1)
                for j in range(K):
                    last = pe.matmul(bank[4 + p][0:CAP0, j * C:(j + 1) * C], HT[:, p, j * CAP0:(j + 1) * CAP0],
                                     n.WD[:, g * K + j], start=True, stop=True)
                last.then_inc(y_ps, 1)

            gate_up(0)
            for g in range(NG):
                if g + 1 < NG:
                    gate_up(g + 1)
                down(g)

        @n.block.vector
        def _(dve):
            def f(g, p, turn):
                dve.wait_ge(silu, g + 1)
                if not (type(g) is int and g < 2):
                    dve.wait_ge(y_ps, g - 1)
                dve.tensor_tensor(HT[:, p], bank[2 * p + 1][:, 0:K * CAP0], SG[:, p], ALU.mult).then_inc(h, 1)

            each_group(dve, f)


def combine0(nc, w, n):
    with ExitStack() as ctx:
        sb, sem = buffers(nc, ctx, "c0_")
        GY = sb("GY", [128, B * C])
        cleared, summed = sem("cleared"), sem("summed")
        got = [sem(f"got{b}") for b in range(B)]

        @nc_block(nc, ctx).gpsimd
        def _(pool):
            pool.wait_ge(cleared, 1)
            for b in range(B):
                pool.indirect_dma_start(out=GY[:, b * C:(b + 1) * C], out_offset=None, in_=n.y_dram,
                                        in_offset=bass.IndirectOffsetOnAxis(ap=n.SLOT[:, b:b + 1].bitcast(U32), axis=0),
                                        bounds_check=E * CAP0 - 1, oob_is_err=False).then_inc(got[b], 16)

        @n.block.vector
        def _(dve):
            dve.memset(GY[:], 0.0).then_inc(cleared, 1)
            for b in range(B):
                dve.wait_ge(got[b], 16)
                x = n.X[:, b * C:(b + 1) * C]
                dve.scalar_tensor_tensor(x, GY[:, b * C:(b + 1) * C], n.GATE[:, b:b + 1], x, ALU.mult, ALU.add).then_inc(summed, 1)
            dve.wait_ge(summed, B)


def experts_layer0(nc, w, n):
    with ExitStack() as ctx:
        sb, sem = buffers(nc, ctx, "l0_")
        n.WG, n.WU, n.WD = (sb(k, [128, E, 128]) for k in ("WG", "WU", "WD"))
        n.w_in = [sem(f"w_in{g}") for g in range(NG0)]
        route0(nc, w, n)
        experts0(nc, w, n)
        combine0(nc, w, n)


def steps(eng, first, step, last):
    first()
    step(0, 0, 0, True, True)
    with eng.Fori(0, (B - 4) // 2) as i:
        step(2 * i + 1, 1, i, True, True)
        step(2 * i + 2, 0, i + 1, True, True)
    step(B - 3, 1, (B - 3) // 2, True, True)
    step(B - 2, 0, (B - 2) // 2, False, True)
    step(B - 1, 1, (B - 1) // 2, False, False)
    last()


def attention1(nc, w, n, cross):
    SCALE = D ** -0.5
    LK = L if cross else T
    VC = 32
    tag = "x1_" if cross else "a1_"
    with ExitStack() as ctx:
        sb, sem = buffers(nc, ctx, tag)
        stats, XN, XT = sb("stats", [128, 11]), sb("XN", [128, C]), sb("XT", [128, T])
        WO, bo = sb("WO", [128, C]), sb("bo", [128, C])
        if cross:
            WQ, WK, WV = sb("WQ", [128, C]), sb("WK", [CC, C]), sb("WV", [CC, C])
            bq, bk, bv = sb("bq", [128, 1]), sb("bk", [128, 1]), sb("bv", [L, C])
            CT = sb("CT", [CC, 2, L])
        else:
            WQKV, bqkv = sb("WQKV", [128, 3 * C]), sb("bqkv", [128, 3 * C])
            QK, RA, RB, QR = (sb(k, [128, 2 * C]) for k in ("QK", "RA", "RB", "QR"))
        VB = sb("VB", [LK, C])
        QT, KZ, V = sb("QT", [128, T]), sb("KZ", [128, R * LK]), sb("V", [LK, 2, H * VC])
        MX, P = sb("MX", [128, H]), sb("P", [128, 2, H * LK])
        PT, OT = sb("PT", [LK, 2, 4 * T]), sb("OT", [128, G * T])
        RD, CX, CTX = sb("RD", [128, H]), sb("CX", [128, C]), sb("CTX", [128, T])
        ps = ctx.enter_context(nc.psum_tensor(tag + "ps", [128, 8 * BANK], F32))
        bank = [ps[:, k * BANK:(k + 1) * BANK] for k in range(8)]
        s = {k: sem(k) for k in NORM_SEMS}
        loaded, v_zero, v_ones = sem("loaded"), sem("v_zero"), sem("v_ones")
        ctx_in = [sem("ctx_even"), sem("ctx_odd")]
        xT_ps, xT, proj_ps, v_copied, v_rows, qk, qr, qkT_ps, qT, kz = (sem(k) for k in ("xT_ps", "xT", "proj_ps", "v_copied", "v_rows", "qk", "qr", "qkT_ps", "qT", "kz"))
        s_ps, mx, sub, p_exp = (sem(k) for k in ("s_ps", "mx", "sub", "p_exp"))
        pT_ps, pT, o_ps, oT, oR_ps, cx, cT_ps, cT, y_ps, x_new = (sem(k) for k in ("pT_ps", "pT", "o_ps", "oT", "oR_ps", "cx", "cT_ps", "cT", "y_ps", "x_new"))
        scores = ps[:, 0:4 * BANK].rearrange("p (g n) -> p g n", g=4)[:, :, 0:R * LK].rearrange("p g (r l) -> p g r l", r=R)
        NL = 8 if cross else 4
        NSUB = 2 if cross else 1

        @nc_block(nc, ctx).sync
        def _(sp):
            row = lambda a: a.rearrange("(o n) -> o n", o=1)
            if cross:
                for dst, name in ((WQ, "Wq"), (WK, "Wk"), (WV, "Wv"), (WO, "Wo")):
                    sp.dma_start(dst[:], w["L1_xattn_" + name]).then_inc(loaded, 16)
                sp.dma_start(bq[:], w["L1_xattn_bq"].rearrange("(n o) -> n o", o=1)).then_inc(loaded, 16)
                sp.dma_start(bk[:], w["L1_xattn_bk"].rearrange("(n o) -> n o", o=1)).then_inc(loaded, 16)
                sp.dma_start(bv[:], row(w["L1_xattn_bv"]).to_broadcast([L, C])).then_inc(loaded, 16)
                sp.dma_start(bo[:], row(w["L1_xattn_bo"]).to_broadcast([128, C])).then_inc(loaded, 16)

                def a(b, p, turn):
                    if not peel(b, p, 2):
                        sp.wait_ge(proj_ps, b - 1)
                    sp.dma_start(CT[:, p, :], w["ctx_T"][bass.ds(b, 1)].rearrange("o c l -> c (o l)")).then_inc(ctx_in[p], 16)

                each_batch(sp, a)
            else:
                sp.dma_start(WQKV[:], w["L1_attn_wqkv_T"]).then_inc(loaded, 16)
                sp.dma_start(WO[:], w["L1_attn_wp_T"]).then_inc(loaded, 16)
                sp.dma_start(bqkv[:], row(w["L1_attn_bqkv"]).to_broadcast([128, 3 * C])).then_inc(loaded, 16)
                sp.dma_start(bo[:], row(w["L1_attn_bp"]).to_broadcast([128, C])).then_inc(loaded, 16)

        @n.block.gpsimd
        def _(pool):
            pool.memset(V[:], 0.0).then_inc(v_zero, 1)
            pool.wait_ge(v_zero, 1)
            pool.memset(V[:].rearrange("p t (h k) -> p (t h) k", k=VC)[:, :, D:D + 1], 1.0).then_inc(v_ones, 1)

            def f(b, p, turn):
                norm_pool(pool, n, b, stats, s)
                pool.wait_ge(v_copied, b + 1)
                if not (type(b) is int and b < 2):
                    pool.wait_ge(o_ps, 4 * (b - 1))
                bias = bv[:] if cross else bqkv[:, 2 * C:3 * C]
                pool.tensor_tensor(V[:, p].rearrange("p (h k) -> p h k", k=VC)[:, :, 0:D], VB[:].rearrange("p (h d) -> p h d", d=D),
                                   bias.rearrange("p (h d) -> p h d", d=D), ALU.add).then_inc(v_rows, 1)

            pool.wait_ge(v_ones, 1)
            pool.wait_ge(loaded, 16 * NL)
            each_batch(pool, f)

        @n.block.scalar
        def _(act):
            def a_xt(b, p):
                act.wait_ge(xT_ps, b + 1)
                act.activation(XT[:], bank[4][:, 0:T], ACT.Copy).then_inc(xT, 1)

            def a_q(b, p):
                if cross:
                    act.wait_ge(proj_ps, b + 1)
                    act.activation(QT[:], bank[4][:, 0:T], ACT.Identity, bias=bq[:]).then_inc(qT, 1)
                else:
                    act.wait_ge(qkT_ps, b + 1)
                    act.activation(QT[:], bank[4][:, 0:T], ACT.Copy).then_inc(qT, 1)

            def a_exp(b, p):
                act.wait_ge(sub, NSUB * (b + 1))
                act.activation(P[:, p, :], P[:, p, :], ACT.Exp, scale=SCALE).then_inc(p_exp, 1)

            def b_pt(b, p, g):
                act.wait_ge(pT_ps, 4 * b + g + 1)
                if not peel(b, g, 2):
                    act.wait_ge(o_ps, 4 * b + g - 1)
                act.activation(PT[:, g % 2, :], bank[6][0:LK, :], ACT.Copy).then_inc(pT, 1)

            def b_ot(b):
                act.wait_ge(o_ps, 4 * (b + 1))
                if not peel(b, 0, 1):
                    act.wait_ge(oR_ps, b)
                act.activation(OT[:], bank[7], ACT.Copy).then_inc(oT, 1)

            def b_ctx(b):
                act.wait_ge(cT_ps, b + 1)
                act.activation(CTX[:], bank[5][:, 0:T], ACT.Copy).then_inc(cT, 1)

            def step(b, p, turn, projections, scores):
                if projections:
                    a_xt(b + 2, p)
                b_pt(b, p, 0)
                if not peel(b, 0, 1):
                    b_ctx(b - 1)
                b_pt(b, p, 1)
                if projections and cross:
                    a_q(b + 2, p)
                b_pt(b, p, 2)
                b_pt(b, p, 3)
                if projections and not cross:
                    a_q(b + 2, p)
                b_ot(b)
                if scores:
                    a_exp(b + 1, 1 - p)

            steps(act, lambda: (a_xt(0, 0), a_q(0, 0), a_xt(1, 1), a_exp(0, 0), a_q(1, 1)), step, lambda: b_ctx(B - 1))

        @n.block.tensor
        def _(pe):
            ident = n.CF[:, CI:CI + 128]

            def a_xt(b, p):
                pe.wait_ge(s["xn"], b + 1)
                if not peel(b, 0, 1):
                    pe.wait_ge(qT, b)
                    pe.wait_ge(kz, b)
                pe.transpose(bank[4][:, 0:T], XN[:], ident).then_inc(xT_ps, 1)

            def a_proj(b, p, turn):
                pe.wait_ge(xT, b + 1)
                if not peel(b, 0, 1):
                    pe.wait_ge(v_copied, b)
                if not (type(b) is int and b < 3):
                    pe.wait_ge(cx, 2 * (b - 2))
                if cross:
                    pe.wait_ge(ctx_in[p], 16 * (turn + 1))
                    pe.matmul(bank[4][:, 0:T], WQ[:], XT[:], start=True, stop=True)
                    pe.matmul(bank[5][:, 0:L], WK[:], CT[:, p, :], start=True, stop=True)
                    pe.matmul(bank[5][0:L, 2 * C:3 * C], CT[:, p, :], WV[:], start=True, stop=True).then_inc(proj_ps, 1)
                else:
                    pe.matmul(bank[5][:, 0:3 * C], XT[:], WQKV[:], start=True, stop=True).then_inc(proj_ps, 1)

            def a_qkt(b, p):
                if not cross:
                    pe.wait_ge(qr, 4 * (b + 1))
                    pe.transpose(bank[4][:, 0:T], QR[:, 0:C], ident)
                    pe.transpose(bank[4][:, T:2 * T], QR[:, C:2 * C], ident).then_inc(qkT_ps, 1)

            def a_scores(b, g0):
                if g0 == 0:
                    pe.wait_ge(qT, b + 1)
                    pe.wait_ge(kz, b + 1)
                    if not peel(b, 0, 1):
                        pe.wait_ge(sub, NSUB * b)
                for g in (g0, g0 + 1):
                    rows = slice(32 * g, 32 * g + 32)
                    last = pe.matmul(bank[g][:, 0:R * LK], QT[rows, :], KZ[rows, :], start=True, stop=cross)
                if cross and g0 == 2:
                    last.then_inc(s_ps, 1)

            def a_causal(b):
                if not cross:
                    for g in range(G):
                        last = pe.matmul(bank[g].rearrange("p (r l) -> p r l", r=R), n.CB[:, BI:BI + 128],
                                         n.CB[:, BNEG:BNEG + 128].unsqueeze(1).to_broadcast([128, R, T]), start=False, stop=True)
                    last.then_inc(s_ps, 1)

            def b_pt(b, p, g):
                if g == 0:
                    pe.wait_ge(p_exp, b + 1)
                if not peel(b, g, 1):
                    pe.wait_ge(pT, 4 * b + g)
                for r in range(R):
                    h = R * g + r
                    last = pe.transpose(bank[6][0:LK, r * T:(r + 1) * T], P[:, p, h * LK:(h + 1) * LK], ident)
                last.then_inc(pT_ps, 1)

            def b_pv(b, p, g):
                pe.wait_ge(pT, 4 * b + g + 1)
                if g == 0:
                    pe.wait_ge(v_rows, b + 1)
                    if not peel(b, 0, 1):
                        pe.wait_ge(oT, b)
                for r in range(R):
                    h = R * g + r
                    last = pe.matmul(bank[7][32 * r:32 * r + 32, g * T:(g + 1) * T], V[:, p, h * VC:(h + 1) * VC],
                                     PT[:, g % 2, r * T:(r + 1) * T], start=True, stop=True)
                last.then_inc(o_ps, 1)

            def turn_back(b, projected):
                pe.wait_ge(oT, b + 1)
                if not peel(b, 0, 1):
                    pe.wait_ge(x_new, 2 * b)
                pe.wait_ge(v_copied, projected)
                for g in range(G):
                    last = pe.transpose(bank[5][:, g * T:(g + 1) * T], OT[:, g * T:(g + 1) * T], ident)
                last.then_inc(oR_ps, 1)

            def b_transpose(b, projected):
                pe.wait_ge(cx, 2 * (b + 1))
                pe.wait_ge(v_copied, projected)
                pe.transpose(bank[5][:, 0:T], CX[:], ident).then_inc(cT_ps, 1)

            def b_project(b):
                pe.wait_ge(cT, b + 1)
                pe.matmul(bank[5][:, T:T + C], CTX[:], WO[:], start=True, stop=True).then_inc(y_ps, 1)

            pe.wait_ge(loaded, 16 * NL)
            pe.wait_ge(v_ones, 1)

            def first():
                a_xt(0, 0), a_proj(0, 0, 0), a_qkt(0, 0)
                a_scores(0, 0), a_scores(0, 2), a_causal(0)
                a_xt(1, 1), a_proj(1, 1, 0), a_qkt(1, 1)

            def step(b, p, turn, projections, scores):
                tail = not peel(b, 0, 1)
                if tail:
                    turn_back(b - 1, b + 2 if scores else B)
                if scores:
                    a_scores(b + 1, 0)
                if projections:
                    a_xt(b + 2, p)
                if scores:
                    a_scores(b + 1, 2)
                if projections:
                    a_proj(b + 2, p, turn + 1)
                if scores:
                    a_causal(b + 1)
                b_pt(b, p, 0)
                if tail:
                    b_transpose(b - 1, b + 3 if projections else B)
                b_pt(b, p, 1)
                b_pv(b, p, 0)
                if tail:
                    b_project(b - 1)
                b_pt(b, p, 2)
                b_pv(b, p, 1)
                b_pt(b, p, 3)
                b_pv(b, p, 2)
                b_pv(b, p, 3)
                if projections:
                    a_qkt(b + 2, p)

            def last():
                turn_back(B - 1, B), b_transpose(B - 1, B), b_project(B - 1)

            steps(pe, first, step, last)

        @n.block.vector
        def _(dve):
            def a_norm(b, p):
                norm_vector(dve, n, b, XN[:], stats, s)

            def a_proj(b, p):
                dve.wait_ge(proj_ps, b + 1)
                if cross:
                    kz4 = KZ[:].rearrange("p (r l) -> p r l", r=R)
                    dve.scalar_tensor_tensor(kz4, bank[5][:, 0:L].unsqueeze(1).to_broadcast([128, R, L]), bk[:],
                                             n.CF[:, CHM:CHM + R].unsqueeze(2).to_broadcast([128, R, L]), ALU.add, ALU.mult).then_inc(kz, 1)
                else:
                    dve.tensor_tensor(QK[:], bank[5][:, 0:2 * C], bqkv[:, 0:2 * C], ALU.add).then_inc(qk, 1)
                if not peel(b, 0, 1):
                    dve.wait_ge(v_rows, b)
                dve.tensor_copy(VB[:], bank[5][0:LK, 2 * C:3 * C]).then_inc(v_copied, 1)
                if not cross:
                    dve.wait_ge(qk, b + 1)
                    rope(dve, QK[:], RA[:], RB[:], QR[:], 2 * H, n, qr, 4 * b)

            def a_kz(b, p):
                if not cross:
                    dve.wait_ge(qT, b + 1)
                    dve.tensor_tensor(KZ[:].rearrange("p (r l) -> p r l", r=R), bank[4][:, T:2 * T].unsqueeze(1).to_broadcast([128, R, T]),
                                      n.CF[:, CHM:CHM + R].unsqueeze(2).to_broadcast([128, R, T]), ALU.mult).then_inc(kz, 1)

            def a_softmax(b, p):
                dve.wait_ge(s_ps, b + 1)
                p4 = P[:, p, :].rearrange("p (g r l) -> p g r l", g=4, l=LK)
                m3 = MX[:].rearrange("p (g r) -> p g r", g=4)
                dve.tensor_reduce(m3, scores, AX.X, ALU.max).then_inc(mx, 1)
                top = m3.unsqueeze(3).to_broadcast([128, 4, R, LK])
                if cross:
                    lim = 10000.0 / SCALE
                    dve.tensor_scalar(p4, scores, lim, -lim, ALU.min, ALU.max).then_inc(sub, 1)
                    dve.wait_ge(mx, 2 * b + 1)
                    dve.tensor_scalar(MX[:], MX[:], lim, -lim, ALU.min, ALU.max).then_inc(mx, 1)
                    dve.wait_ge(mx, 2 * b + 2)
                    dve.wait_ge(sub, 2 * b + 1)
                    dve.tensor_tensor(p4, p4, top, ALU.subtract).then_inc(sub, 1)
                else:
                    dve.wait_ge(mx, b + 1)
                    dve.tensor_tensor(p4, scores, top, ALU.subtract).then_inc(sub, 1)

            def b_cx(b):
                dve.wait_ge(oR_ps, b + 1)
                o = bank[5].rearrange("p (h k) -> p h k", k=VC)
                dve.reciprocal(RD[:].unsqueeze(2), o[:, :, D:D + 1]).then_inc(cx, 1)
                dve.wait_ge(cx, 2 * b + 1)
                dve.tensor_tensor(CX[:].rearrange("p (h d) -> p h d", d=D), o[:, :, 0:D],
                                  RD[:].unsqueeze(2).to_broadcast([128, H, D]), ALU.mult).then_inc(cx, 1)

            def b_out(b):
                dve.wait_ge(y_ps, b + 1)
                x = n.X[:, cols(b, C)]
                dve.tensor_tensor(x, bank[5][:, T:T + C], x, ALU.add).then_inc(x_new, 1)
                dve.wait_ge(x_new, 2 * b + 1)
                dve.tensor_tensor(x, x, bo[:], ALU.add).then_inc(x_new, 1)

            dve.wait_ge(loaded, 16 * NL)
            dve.wait_ge(v_ones, 1)

            def first():
                a_norm(0, 0), a_proj(0, 0), a_norm(1, 1), a_kz(0, 0), a_softmax(0, 0)
                a_proj(1, 1), a_kz(1, 1)

            def step(b, p, turn, projections, scores):
                tail = not peel(b, 0, 1)
                if projections:
                    a_norm(b + 2, p)
                if tail:
                    b_cx(b - 1)
                if projections:
                    a_proj(b + 2, p)
                if scores:
                    a_softmax(b + 1, 1 - p)
                if tail:
                    b_out(b - 1)
                if projections:
                    a_kz(b + 2, p)

            def last():
                b_cx(B - 1), b_out(B - 1)
                dve.wait_ge(x_new, 2 * B)

            steps(dve, first, step, last)


def self_attention1(nc, w, n):
    attention1(nc, w, n, cross=False)


def cross_attention1(nc, w, n):
    attention1(nc, w, n, cross=True)


SLOTS = 4


def pair_weights(w, n, i, k):
    both = lambda name: w["L1_ffn_" + name][bass.ds(2 * i, 2)].rearrange("e c f -> c e f")
    return ((n.W1[:, k].rearrange("c (e f) -> c e f", e=2), both("W1")), (n.W3[:, k].rearrange("c (e f) -> c e f", e=2), both("W3")),
            (n.W2[:, k], w["L1_ffn_W2"].rearrange("e f d -> (e f) d")[bass.ds(128 * i, 128), :]))


def route1(nc, w, n):
    with ExitStack() as ctx:
        sb, sem = buffers(nc, ctx, "r1_")
        WR = sb("WR", [128, E])
        stats, XN = sb("stats", [128, B, 10]), sb("XN", [128, B, C])
        LG, TOP, IDX, IDF = sb("LG", [128, B, E]), sb("TOP", [128, B, 8]), sb("IDX", [128, B, 8], U32), sb("IDF", [128, B, 8])
        EX, SE, RS, W, R1, R2 = (sb(k, [128, B, m]) for k, m in (("EX", E), ("SE", 1), ("RS", 1), ("W", E), ("R1", E), ("R2", E)))
        EQ = [sb(f"EQ{k}", [128, B, E]) for k in range(TOPK)]
        SEL = sb("SEL", [128, B, E], BF16)
        WS = sb("WS", [128, B, 3 * E], BF16)
        ps = ctx.enter_context(nc.psum_tensor("r1_ps", [128, 5 * BANK], F32))
        psb = ctx.enter_context(nc.psum_tensor("r1_psb", [128, 2 * BANK], BF16))
        bank = [ps[:, k * BANK:(k + 1) * BANK] for k in range(5)]
        s = {k: sem(k) for k in NORM_SEMS}
        loaded, weights_in = sem("loaded"), sem("weights_in")
        xT_ps, xta, l_ps, lg, top, idx, idf, equal, selected = (sem(k) for k in ("xT_ps", "xta", "l_ps", "lg", "top", "idx", "idf", "equal", "selected"))
        less, ex, se, rs, pos_ps, kept, parts, wT_ps, wT = (sem(k) for k in ("less", "ex", "se", "rs", "pos_ps", "kept", "parts", "wT_ps", "wT"))
        logits = bank[2][:, 0:B * E].rearrange("p (b e) -> p b e", e=E)
        place = bank[3][:, 0:B * E].rearrange("p (b e) -> p b e", e=E)

        @nc_block(nc, ctx).sync
        def _(sp):
            sp.dma_start(WR[:], w["L1_ffn_Wg"]).then_inc(loaded, 16)
            for dst, name in ((n.S1, "Ws1"), (n.S3, "Ws3"), (n.S2, "Ws2")):
                sp.dma_start(dst[:], w["L1_ffn_" + name]).then_inc(weights_in, 16)
            sp.dma_start(n.SELF[:], w["const_sel"]).then_inc(weights_in, 16)
            for i in range(SLOTS):
                for dma in pair_weights(w, n, i, i):
                    sp.dma_start(*dma).then_inc(weights_in, 16)
            sp.wait_ge(weights_in, 16 * (4 + 3 * SLOTS))

        @n.block.gpsimd
        def _(pool):
            norm_all_pool(pool, n, stats, s)

        @n.block.scalar
        def _(act):
            for q in range(2):
                act.wait_ge(xT_ps, q + 1)
                act.activation(n.XTA[:, q * BANK:(q + 1) * BANK], bank[q], ACT.Copy).then_inc(xta, 1)
            act.wait_ge(less, 1)
            act.activation(EX[:], EX[:], ACT.Exp).then_inc(ex, 1)
            act.wait_ge(wT_ps, 1)
            act.activation(n.WT[:], psb[0:96, :], ACT.Copy).then_inc(wT, 1)
            act.wait_ge(wT, 1)

        @n.block.tensor
        def _(pe):
            for b in range(B):
                pe.wait_ge(s["xn"], b + 1)
                last = pe.transpose(bank[b // 4][:, (b % 4) * T:(b % 4 + 1) * T], XN[:, b], n.CF[:, CI:CI + 128])
                if b % 4 == 3:
                    last.then_inc(xT_ps, 1)
            pe.wait_ge(loaded, 16)
            for b in range(B):
                pe.wait_ge(xta, b // 4 + 1)
                last = pe.matmul(bank[2][:, b * E:(b + 1) * E], n.XTA[:, b * T:(b + 1) * T], WR[:], start=True, stop=True)
            last.then_inc(l_ps, 1)
            count_places(pe, n, SEL, bank[3], selected).then_inc(pos_ps, 1)
            pe.wait_ge(parts, 4)
            for b in range(B):
                last = pe.transpose(psb[0:96, b * T:(b + 1) * T], WS[:, b], n.CB[:, BI:BI + 128])
            last.then_inc(wT_ps, 1)

        @n.block.vector
        def _(dve):
            norm_all_vector(dve, n, XN, stats, s)
            dve.wait_ge(l_ps, 1)
            dve.tensor_copy(LG[:], logits).then_inc(lg, 1)
            dve.wait_ge(lg, 1)
            for b in range(B):
                dve.max(TOP[:, b], LG[:, b]).then_inc(top, 1)
            dve.wait_ge(top, B)
            dve.tensor_tensor(EX[:], LG[:], TOP[:, :, 0:1].to_broadcast([128, B, E]), ALU.subtract).then_inc(less, 1)
            for b in range(B):
                dve.max_index(IDX[:, b], TOP[:, b], LG[:, b]).then_inc(idx, 1)
            dve.wait_ge(idx, B)
            dve.tensor_copy(IDF[:], IDX[:]).then_inc(idf, 1)
            dve.wait_ge(idf, 1)
            iota = n.CF[:, CIOTA:CIOTA + E].unsqueeze(1).to_broadcast([128, B, E])
            for k in range(TOPK):
                dve.tensor_tensor(EQ[k][:], iota, IDF[:, :, k:k + 1].to_broadcast([128, B, E]), ALU.is_equal).then_inc(equal, 1)
            dve.wait_ge(equal, 4)
            dve.tensor_tensor(EQ[0][:], EQ[0][:], EQ[1][:], ALU.add).then_inc(equal, 1)
            dve.tensor_tensor(EQ[2][:], EQ[2][:], EQ[3][:], ALU.add).then_inc(equal, 1)
            dve.wait_ge(equal, 6)
            dve.tensor_tensor(SEL[:], EQ[0][:], EQ[2][:], ALU.add).then_inc(selected, 1)
            dve.wait_ge(ex, 1)
            dve.tensor_reduce(SE[:].rearrange("p b o -> p (b o)"), EX[:], AX.X, ALU.add).then_inc(se, 1)
            dve.wait_ge(se, 1)
            dve.reciprocal(RS[:], SE[:]).then_inc(rs, 1)
            dve.wait_ge(selected, 1)
            dve.tensor_tensor(R1[:], EX[:], SEL[:], ALU.mult).then_inc(rs, 1)
            dve.wait_ge(rs, 2)
            dve.tensor_tensor(R2[:], R1[:], RS[:].to_broadcast([128, B, E]), ALU.mult).then_inc(rs, 1)
            dve.wait_ge(pos_ps, 1)
            dve.wait_ge(rs, 3)
            dve.scalar_tensor_tensor(W[:], place, CAP1 + 0.5, R2[:], ALU.is_lt, ALU.mult).then_inc(kept, 1)
            dve.wait_ge(kept, 1)
            dve.tensor_copy(WS[:, :, 0:E], W[:]).then_inc(parts, 1)
            dve.wait_ge(parts, 1)
            dve.tensor_tensor(R1[:], W[:], WS[:, :, 0:E], ALU.subtract).then_inc(parts, 1)
            dve.wait_ge(parts, 2)
            dve.tensor_copy(WS[:, :, E:2 * E], R1[:]).then_inc(parts, 1)
            dve.wait_ge(parts, 3)
            dve.tensor_tensor(WS[:, :, 2 * E:3 * E], R1[:], WS[:, :, E:2 * E], ALU.subtract).then_inc(parts, 1)


def experts1(nc, w, n, out):
    NP = E // 2
    with ExitStack() as ctx:
        sb, sem = buffers(nc, ctx, "e1_")
        SELB = sb("SELB", [96, NP * 128], BF16)
        SG, HU, HW = (sb(k, [128, 2, BANK]) for k in ("SG", "HU", "HW"))
        YT = sb("YT", [128, B * T])
        ps = ctx.enter_context(nc.psum_tensor("e1_ps", [128, 8 * BANK], F32))
        bank = [ps[:, k * BANK:(k + 1) * BANK] for k in range(8)]
        sel_ready = sem("sel_ready")
        w_in = [sem(f"w_in{k}") for k in range(SLOTS)]
        gu_ps, wb_ps, silu, hu, hw, y_ps = (sem(k) for k in ("gu_ps", "wb_ps", "silu", "hu", "hw", "y_ps"))
        yT, yr_ps, x_new, stored = sem("yT"), sem("yr_ps"), sem("x_new"), sem("stored")

        @nc_block(nc, ctx).sync
        def _(sp):
            with sp.Fori(1, NP // SLOTS) as t:
                for k in range(SLOTS):
                    i = SLOTS * t + k
                    sp.wait_ge(y_ps, 2 * i + 4 - 2 * SLOTS)
                    for dma in pair_weights(w, n, i, k):
                        sp.dma_start(*dma).then_inc(w_in[k], 16)
            for b in range(B):
                sp.wait_ge(x_new, b + 1)
                sp.dma_start(out[b], n.X[:, b * C:(b + 1) * C]).then_inc(stored, 16)
            sp.wait_ge(stored, 16 * B)

        def each_pair(eng, shared, f):
            shared()
            with eng.Fori(0, NP) as i:
                f(i)

        @n.block.scalar
        def _(act):
            def half(u, q):
                act.wait_ge(gu_ps, u + 1)
                if not (type(u) is int and u < 2):
                    act.wait_ge(hu, u - 1)
                act.activation(SG[:, q], bank[q], ACT.Silu).then_inc(silu, 1)

            each_pair(act, lambda: (half(0, 0), half(1, 1)), lambda i: (half(2 * i + 2, 0), half(2 * i + 3, 1)))
            for q in range(2):
                act.wait_ge(y_ps, 2 * NP + 1 + q)
                act.activation(YT[:, q * BANK:(q + 1) * BANK], bank[6 + q], ACT.Copy).then_inc(yT, 1)

        @n.block.tensor
        def _(pe):
            def half(u, q, w1, w3, sel):
                x = n.XTA[:, q * BANK:(q + 1) * BANK]
                if not (type(u) is int and u < 2):
                    pe.wait_ge(hu, u - 1)
                pe.matmul(bank[q], w1, x, start=True, stop=True)
                pe.matmul(bank[2 + q], w3, x, start=True, stop=True).then_inc(gu_ps, 1)
                if sel is not None:
                    if not (type(u) is int and u < 4):
                        pe.wait_ge(hw, u - 3)
                    pe.matmul(bank[4 + q], sel, n.WT[:, q * BANK:(q + 1) * BANK], start=True, stop=True).then_inc(wb_ps, 1)

            def down(u, q, w2, start, stop):
                if type(u) is int and u < 2:
                    pe.wait_ge(hu, u + 1)
                else:
                    pe.wait_ge(hw, u - 1)
                pe.matmul(bank[6 + q], w2, HU[:, q] if type(u) is int and u < 2 else HW[:, q], start=start, stop=stop).then_inc(y_ps, 1)

            def pair(i, k, turn, down_w, start):
                if not type(turn) is int:
                    pe.wait_ge(w_in[k], 48 * turn)
                for q in range(2):
                    half(2 * i + 2 + q, q, n.W1[:, k], n.W3[:, k], SELB[:, cols(i, 128)])
                    down(2 * i + q, q, down_w, start, False)

            half(0, 0, n.S1[:], n.S3[:], None)
            half(1, 1, n.S1[:], n.S3[:], None)
            pe.wait_ge(sel_ready, 1)
            for k in range(SLOTS):
                pair(k, k, 0, n.W2[:, k - 1] if k else n.S2[:], k == 0)
            with pe.Fori(1, NP // SLOTS) as t:
                for k in range(SLOTS):
                    pair(SLOTS * t + k, k, t, n.W2[:, (k - 1) % SLOTS], False)
            for q in range(2):
                down(2 * NP + q, q, n.W2[:, SLOTS - 1], False, True)
            pe.wait_ge(hu, 2 * NP + 2)
            for b in range(B):
                pe.wait_ge(yT, b // 4 + 1)
                pe.transpose(bank[b // 4][:, (b % 4) * T:(b % 4 + 1) * T], YT[:, b * T:(b + 1) * T], n.CF[:, CI:CI + 128])\
                    .then_inc(yr_ps, 1)

        @n.block.vector
        def _(dve):
            def shared(u, q):
                dve.wait_ge(silu, u + 1)
                dve.tensor_tensor(HU[:, q], bank[2 + q], SG[:, q], ALU.mult).then_inc(hu, 1)

            def half(u, q):
                dve.wait_ge(silu, u + 1)
                dve.wait_ge(y_ps, u - 1)
                dve.tensor_tensor(HU[:, q], bank[2 + q], SG[:, q], ALU.mult).then_inc(hu, 1)
                dve.wait_ge(wb_ps, u - 1)
                dve.wait_ge(hu, u + 1)
                dve.tensor_tensor(HW[:, q], bank[4 + q], HU[:, q], ALU.mult).then_inc(hw, 1)

            dve.tensor_copy(SELB[:], n.SELF[:]).then_inc(sel_ready, 1)
            each_pair(dve, lambda: (shared(0, 0), shared(1, 1)), lambda i: (half(2 * i + 2, 0), half(2 * i + 3, 1)))
            for b in range(B):
                dve.wait_ge(yr_ps, 4 * (b // 4) + 4)
                x = n.X[:, b * C:(b + 1) * C]
                dve.tensor_tensor(x, bank[b // 4][:, (b % 4) * T:(b % 4 + 1) * T], x, ALU.add).then_inc(x_new, 1)


def program(nc, w, out, upto=99, only=0):
    n = Net()
    with ExitStack() as ctx:
        sb, sem = buffers(nc, ctx, "")
        n.X = sb("X", [128, B * C])
        n.CF, n.CB = sb("CF", [128, NCF]), sb("CB", [128, NCB], BF16)
        n.NHALF, n.EPS = sb("NHALF", [128, 1]), sb("EPS", [128, 1])
        n.SINK = sb("SINK", [128, 64 * (D + 1)])
        n.WQX, n.WKX, n.WVX, n.WOX = sb("WQX", [128, 1024]), sb("WKX", [CC, 1024]), sb("WVX", [CC, 1024]), sb("WOX", [128, 1024])
        n.vi_dram = nc.dram_tensor("vi_scratch", (B * LI, 1024), F32, kind="Internal").ap()
        n.buf_dram = nc.dram_tensor("slots_scratch", (E * CAP0, C), F32, kind="Internal").ap()
        n.y_dram = nc.dram_tensor("rows_scratch", (E * CAP0, C), F32, kind="Internal").ap()
        n.SLOT, n.GATE = sb("SLOT", [128, B], I32), sb("GATE", [128, B])
        load_phase(nc, w, n)
        phases = [self_attention0, cross_attention0, experts_layer0, self_attention1, cross_attention1]
        for phase in phases[only:upto]:
            phase(nc, w, n)
        if upto == 99:
            n.XTA, n.WT = sb("XTA", [128, B * T]), sb("WT", [96, B * T], BF16)
            n.W1, n.W3, n.W2 = (sb(k, [128, SLOTS, 128]) for k in ("W1", "W3", "W2"))
            n.S1, n.S3, n.S2, n.SELF = sb("S1", [128, 128]), sb("S3", [128, 128]), sb("S2", [128, 128]), sb("SELF", [96, E // 2 * 128])
            route1(nc, w, n)
            experts1(nc, w, n, out)
        else:
            store_phase(nc, w, n, out)


def constants():
    import numpy as np

    f = np.zeros((128, NCF), np.float32)
    p = np.arange(128)[:, None]
    q = np.arange(128)[None, :]
    f[:, CI:CI + 128] = p == q
    for br, (h, g) in enumerate(((16, 0), (128, 16), (128, 0))):
        f[:, CM + br * 128:CM + (br + 1) * 128] = (q - p >= g) & (q - p < h)
    angle = np.arange(T, dtype=np.float32)[:, None] * (1.0 / np.float32(10000.0) ** (np.arange(0, D, 2, dtype=np.float32) / D))[None, :]
    angle = np.repeat(angle.astype(np.float32), 2, axis=1)
    f[:, CCOS:CCOS + D] = np.cos(angle)
    f[:, CSIN:CSIN + D] = np.sin(angle)
    f[:, CHM:CHM + R] = (p % 32) // D == np.arange(R)[None, :]
    f[:, CIOTA:CIOTA + E] = np.arange(E)[None, :]
    f[:, CONE:CONE + 128] = 1.0
    h = np.zeros((128, NCB), np.float32)
    h[:, BI:BI + 128] = p == q
    h[:, BNEG:BNEG + 128] = np.where(q <= p, 0.0, -1e30)
    h[:, BTRI:BTRI + 128] = p <= q
    h[:, BONE:BONE + 128] = 1.0
    sel = np.zeros((96, 16, 128), np.float32)
    k, i, m = np.arange(96)[:, None, None], np.arange(16)[None, :, None], np.arange(128)[None, None, :]
    sel[:] = k % 32 == 2 * i + m // 64
    return {"const_f32": f, "const_half": h, "const_sel": sel.reshape(96, 2048)}


def layout(inputs):
    import numpy as np

    a = {k: np.asarray(v) for k, v in inputs.items()}
    out = {k: a[k] for k in a if k != "ctx_768"}
    for t in "qkvo":
        out[f"L0_xattn_{t}_down_T"] = a[f"L0_xattn_{t}_down"].T
        del out[f"L0_xattn_{t}_down"]
    out["ctx_T"] = a["ctx_768"].transpose(0, 2, 1)
    out["ctx_img_T"] = a["ctx_768"][:, LO:, :].reshape(B * LI, CC).T
    out["L1_attn_wqkv_T"] = np.concatenate([out.pop(f"L1_attn_w{t}").T for t in "qkv"], axis=1)
    out["L1_attn_bqkv"] = np.concatenate([out.pop(f"L1_attn_b{t}") for t in "qkv"])
    out["L1_attn_wp_T"] = out.pop("L1_attn_wp").T
    out.update(constants())
    return {k: np.ascontiguousarray(v) for k, v in out.items()}


def kernel(**inputs):
    import numpy as np
    import concourse.bacc as bacc
    from concourse.bass_utils import run_bass_kernel_spmd

    nc = bacc.Bacc("TRN2", target_bir_lowering=False, num_devices=1)
    arrays = {f"in_{k}": v for k, v in layout(inputs).items()}
    w = {k[3:]: nc.dram_tensor(k, v.shape, mybir.dt.from_np(v.dtype), kind="ExternalInput").ap() for k, v in arrays.items()}
    out = nc.dram_tensor("out_x", (B, T, C), F32, kind="ExternalOutput").ap()
    program(nc, w, out)
    r = run_bass_kernel_spmd(nc, [arrays], core_ids=[0])
    return r.results[0]["out_x"]
```

```python
from contextlib import ExitStack

import concourse.bass as bass
from concourse import mybir

F32 = mybir.dt.float32
BF16 = mybir.dt.bfloat16
I32 = mybir.dt.int32
U32 = mybir.dt.uint32
ALU = mybir.AluOpType
ACT = mybir.ActivationFunctionType
AX = mybir.AxisListType

B, T, C = 8, 128, 128
H, D = 16, 8
G, R = 4, 4
BR = 4
L, CC = 77, 96
LO, LI = 73, 4
PR, DX = 8, 64
E = 32
NG0 = 8
CAP0 = 40
CAP1 = 512
HID = 64
TOPK = 4
BANK = 512
LN_EPS = 1e-5
RMS_EPS = 1.1920928955078125e-07
BIG = 1.0e6

CI, CM, CCOS, CSIN, CHM, CIOTA, CONE = 0, 128, 512, 520, 528, 532, 564
NCF = 692
BI, BNEG, BTRI, BONE = 0, 128, 256, 384
NCB = 512


def cols(b, n):
    return bass.ds(b * n, n)


class Net:
    pass


def buffers(nc, ctx, tag):
    def sb(name, shape, dt=F32):
        return ctx.enter_context(nc.sbuf_tensor(tag + name, shape, dt))

    own = []

    def sem(name):
        own.append(nc.alloc_semaphore(tag + name))
        return own[-1]

    def clear():
        if own:
            nc.clear_and_free_semaphores(own)
            nc.all_engine_barrier()

    ctx.callback(clear)
    return sb, sem


def peel(b, k, lag):
    return type(b) is int and b == 0 and k < lag


def batches(eng, a_then_b, first, last):
    first()
    a_then_b(0, 0)
    with eng.Fori(0, (B - 2) // 2) as i:
        a_then_b(2 * i + 1, 1)
        a_then_b(2 * i + 2, 0)
    last()


def steps(eng, first, step, last):
    first()
    step(0, 0, 0, True, True)
    with eng.Fori(0, (B - 4) // 2) as i:
        step(2 * i + 1, 1, i, True, True)
        step(2 * i + 2, 0, i + 1, True, True)
    step(B - 3, 1, (B - 3) // 2, True, True)
    step(B - 2, 0, (B - 2) // 2, False, True)
    step(B - 1, 1, (B - 1) // 2, False, False)
    last()


def lora_buffers(nc, ctx, n):
    sb, sem = buffers(nc, ctx, "lo_")
    n.down = [sb(f"down{i}", [32, k]) for i, k in enumerate((C, CC, CC, 1024))]
    n.up = [sb(f"up{i}", [32, k]) for i, k in enumerate((1024, 1024, 1024, C))]
    n.alpha, n.ctx_i, n.wvi = sb("alpha", [128, 4]), sb("ctx_i", [CC, B * LI]), sb("wvi", [CC, 1024])
    n.lora_loaded = sem("lora_loaded")


def self0_buffers(nc, ctx, n):
    sb, sem = buffers(nc, ctx, "w0_")
    n.NQ = (BR - 1) * C
    n.WQ, n.WK, n.WV, n.WO = sb("WQ", [128, n.NQ]), sb("WK", [128, C]), sb("WV", [128, 512]), sb("WO", [128, C])
    n.bqk, n.bv, n.bo = sb("bqk", [128, 512]), sb("bv", [128, 512]), sb("bo", [128, C])
    n.self0_loaded = sem("self0_loaded")


def start_lora(sp, w, n):
    for dst, name in ((n.WQX, "Wq"), (n.WKX, "Wk"), (n.WVX, "Wv")):
        sp.dma_start(dst[:], w["L0_xattn_" + name]).then_inc(n.lora_loaded, 16)
    sp.dma_start(n.WOX[:].rearrange("p (j n) -> p j n", j=PR), w["L0_xattn_Wo"].rearrange("(j p) n -> p j n", p=128)).then_inc(n.lora_loaded, 16)
    for i, t in enumerate("qkvo"):
        sp.dma_start(n.down[i][:], w[f"L0_xattn_{t}_down_T"]).then_inc(n.lora_loaded, 16)
        sp.dma_start(n.up[i][:], w[f"L0_xattn_{t}_up"]).then_inc(n.lora_loaded, 16)
        sp.dma_start(n.alpha[:, i:i + 1], w[f"L0_xattn_{t}_alpha"].rearrange("(o n) -> o n", o=1).to_broadcast([128, 1])).then_inc(n.lora_loaded, 16)
    sp.dma_start(n.ctx_i[:], w["ctx_img_T"]).then_inc(n.lora_loaded, 16)
    sp.dma_start(n.wvi[:], w["L0_xattn_Wv_ipa"]).then_inc(n.lora_loaded, 16)


def load_phase(nc, w, n):
    with ExitStack() as ctx:
        sb, sem = buffers(nc, ctx, "ld_")
        small_loaded, x_loaded = sem("small_loaded"), sem("x_loaded")
        tanh_done, sink_done, made = sem("tanh_done"), sem("sink_done"), sem("made")
        sinks, v_nulls, esink = sb("sinks", [128, 64]), sb("v_nulls", [128, 512]), sb("esink", [128, 64])
        half = sb("half", [128, NCB])

        @nc_block(nc, ctx).sync
        def _(sp):
            sp.dma_start(sinks[:], w["L0_attn_sink_scalars"].rearrange("(o n) -> o n", o=1).to_broadcast([128, 64])).then_inc(small_loaded, 16)
            sp.dma_start(v_nulls[:], w["L0_attn_v_nulls"].rearrange("h d -> (h d)").rearrange("(o n) -> o n", o=1).to_broadcast([128, 512])).then_inc(small_loaded, 16)
            sp.dma_start(n.X[:].rearrange("p (b c) -> p b c", b=B), w["x"].rearrange("b t c -> t b c")).then_inc(x_loaded, 16)
            sp.dma_start(n.WQ[:], w["L0_attn_WQ"][:, 0:n.NQ]).then_inc(n.self0_loaded, 16)
            sp.dma_start(n.WK[:], w["L0_attn_WK"]).then_inc(n.self0_loaded, 16)
            sp.dma_start(n.WV[:], w["L0_attn_WV"]).then_inc(n.self0_loaded, 16)
            sp.dma_start(n.WO[:], w["L0_attn_WO"]).then_inc(n.self0_loaded, 16)
            row = lambda a: a.rearrange("(o n) -> o n", o=1)
            sp.dma_start(n.bqk[:, 0:n.NQ], row(w["L0_attn_bQ"])[:, 0:n.NQ].to_broadcast([128, n.NQ])).then_inc(n.self0_loaded, 16)
            sp.dma_start(n.bqk[:, n.NQ:512], row(w["L0_attn_bK"]).to_broadcast([128, C])).then_inc(n.self0_loaded, 16)
            sp.dma_start(n.bv[:], row(w["L0_attn_bV"]).to_broadcast([128, 512])).then_inc(n.self0_loaded, 16)
            sp.dma_start(n.bo[:], row(w["L0_attn_bO"]).to_broadcast([128, C])).then_inc(n.self0_loaded, 16)

        @n.block.scalar
        def _(act):
            act.dma_start(half[:], w["const_half"]).then_inc(small_loaded, 16)
            act.dma_start(n.CF[:], w["const_f32"]).then_inc(small_loaded, 16)
            act.wait_ge(small_loaded, 64)
            act.activation(esink[:], sinks[:], ACT.Tanh).then_inc(tanh_done, 1)
            act.wait_ge(tanh_done, 1)
            act.activation(esink[:], esink[:], ACT.Exp).then_inc(sink_done, 1)

        @n.block.vector
        def _(dve):
            dve.memset(n.NHALF[:], -0.5).then_inc(made, 1)
            dve.memset(n.EPS[:], LN_EPS).then_inc(made, 1)
            dve.wait_ge(small_loaded, 64)
            dve.tensor_copy(n.CB[:], half[:]).then_inc(made, 1)
            dve.wait_ge(sink_done, 1)
            row = n.SINK[:].rearrange("p (h k) -> p h k", k=D + 1)
            dve.tensor_tensor(row[:, :, 0:D], v_nulls[:].rearrange("p (h d) -> p h d", d=D),
                              esink[:].unsqueeze(2).to_broadcast([128, 64, D]), ALU.mult).then_inc(made, 1)
            dve.tensor_copy(row[:, :, D:D + 1], esink[:].unsqueeze(2)).then_inc(made, 1)
            dve.wait_ge(x_loaded, 16)
            dve.wait_ge(made, 5)


def fold_phase(nc, w, n):
    with ExitStack() as ctx:
        sb, sem = buffers(nc, ctx, "fo_")
        folded_ps, folded, scaled = sem("folded_ps"), sem("folded"), sem("scaled")
        kvi_ps, kvi_sb, kvi_stored = sem("kvi_ps"), sem("kvi_sb"), sem("kvi_stored")
        vi = sb("vi", [B * LI, 1024])
        ps = ctx.enter_context(nc.psum_tensor("fo_ps", [128, 8 * BANK], F32))

        @nc_block(nc, ctx).sync
        def _(sp):
            sp.wait_ge(kvi_sb, 1)
            sp.dma_start(n.vi_dram, vi[:]).then_inc(kvi_stored, 16)
            sp.wait_ge(kvi_stored, 16)

        @n.block.scalar
        def _(act):
            act.wait_ge(kvi_ps, 1)
            act.activation(vi[:], ps[0:B * LI, 6 * BANK:8 * BANK], ACT.Copy).then_inc(kvi_sb, 1)

        @n.block.tensor
        def _(pe):
            pe.wait_ge(n.lora_loaded, 16 * 18)
            for half in range(2):
                last = pe.matmul(ps[0:B * LI, (6 + half) * BANK:(7 + half) * BANK], n.ctx_i[:],
                                 n.wvi[:, half * BANK:(half + 1) * BANK], start=True, stop=True)
            last.then_inc(kvi_ps, 1)
            for i in range(3):
                for half in range(2):
                    last = pe.matmul(ps[0:n.down[i].shape[1], (2 * i + half) * BANK:(2 * i + half + 1) * BANK],
                                     n.down[i][:], n.up[i][:, half * BANK:(half + 1) * BANK], start=True, stop=True)
                last.then_inc(folded_ps, 1)
            pe.wait_ge(folded, 1)
            for j in range(PR):
                last = pe.matmul(ps[:, j * 128:(j + 1) * 128], n.down[3][:, j * 128:(j + 1) * 128], n.up[3][:],
                                 start=True, stop=True)
            last.then_inc(folded_ps, 1)

        @n.block.vector
        def _(dve):
            dve.wait_ge(n.lora_loaded, 16 * 18)
            dve.tensor_scalar(n.alpha[:], n.alpha[:], 1.0 / 32, None, ALU.mult).then_inc(scaled, 1)
            dve.wait_ge(scaled, 1)
            for i, (dst, rows) in enumerate(((n.WQX, C), (n.WKX, CC), (n.WVX, CC), (n.WOX, 128))):
                dve.wait_ge(folded_ps, i + 1)
                src = ps[0:rows, 2 * (i % 3) * BANK:2 * (i % 3) * BANK + 1024]
                dve.scalar_tensor_tensor(dst[:], src, n.alpha[0:rows, i:i + 1], dst[:], ALU.mult, ALU.add).then_inc(folded, 1)
            dve.wait_ge(folded, 4)


def nc_block(nc, ctx):
    Net.block = ctx.enter_context(nc.Block())
    return Net.block


def norm_stats(dve, n, b, stats, s):
    dve.bn_stats(stats[:, 0:6], n.X[:, cols(b, C)]).then_inc(s["stats"], 1)
    dve.wait_ge(s["stats"], b + 1)
    dve.tensor_copy(stats[:, 10:11], n.EPS[:])
    dve.bn_aggr(stats[:, 6:8], stats[:, 0:6]).then_inc(s["aggr"], 1)


def norm_apply(dve, n, b, dst, stats, s):
    dve.wait_ge(s["rstd"], b + 1)
    dve.tensor_scalar(dst, n.X[:, cols(b, C)], stats[:, 6:7], stats[:, 9:10], ALU.subtract, ALU.mult).then_inc(s["xn"], 1)


def norm_vector(dve, n, b, dst, stats, s):
    norm_stats(dve, n, b, stats, s)
    norm_apply(dve, n, b, dst, stats, s)


def norm_pool(pool, n, b, stats, s):
    pool.wait_ge(s["aggr"], b + 1)
    pool.tensor_tensor(stats[:, 8:9], stats[:, 7:8], n.EPS[:], ALU.add).then_inc(s["var_eps"], 1)
    pool.wait_ge(s["var_eps"], b + 1)
    pool.tensor_tensor(stats[:, 9:10], stats[:, 8:9], n.NHALF[:], ALU.pow).then_inc(s["rstd"], 1)


def norm_all_vector(dve, n, dst, stats, s):
    for b in range(B):
        dve.bn_stats(stats[:, b, 0:6], n.X[:, cols(b, C)]).then_inc(s["stats"], 1)
    dve.wait_ge(s["stats"], B)
    for b in range(B):
        dve.bn_aggr(stats[:, b, 6:8], stats[:, b, 0:6]).then_inc(s["aggr"], 1)
    dve.wait_ge(s["rstd"], 1)
    for b in range(B):
        dve.tensor_scalar(dst[:, b], n.X[:, cols(b, C)], stats[:, b, 6:7], stats[:, b, 9:10], ALU.subtract, ALU.mult).then_inc(s["xn"], 1)


def norm_all_pool(pool, n, stats, s):
    pool.wait_ge(s["aggr"], B)
    pool.tensor_tensor(stats[:, :, 8:9], stats[:, :, 7:8], n.EPS[:].unsqueeze(1).to_broadcast([128, B, 1]), ALU.add).then_inc(s["var_eps"], 1)
    pool.wait_ge(s["var_eps"], 1)
    pool.tensor_tensor(stats[:, :, 9:10], stats[:, :, 8:9], n.NHALF[:].unsqueeze(1).to_broadcast([128, B, 1]), ALU.pow).then_inc(s["rstd"], 1)


NORM_SEMS = ("stats", "aggr", "rstd", "xn", "var_eps")


def rope(dve, src, a, c, dst, nh, n, done, base):
    v = src.rearrange("p (h d) -> p h d", d=D)
    cos = n.CF[:, CCOS:CCOS + D].unsqueeze(1).to_broadcast([128, nh, D])
    sin = n.CF[:, CSIN:CSIN + D].unsqueeze(1).to_broadcast([128, nh, D])
    av = a.rearrange("p (h d) -> p h d", d=D)
    cv = c.rearrange("p (h d) -> p h d", d=D)
    dve.tensor_tensor(av, v, cos, ALU.mult).then_inc(done, 1)
    dve.tensor_tensor(cv, v, sin, ALU.mult).then_inc(done, 1)
    dve.wait_ge(done, base + 2)
    a2 = a.rearrange("p (h t two) -> p h t two", t=D // 2, two=2)
    c2 = c.rearrange("p (h t two) -> p h t two", t=D // 2, two=2)
    o = dst.rearrange("p (h d) -> p h d", d=D)
    dve.tensor_tensor(o[:, :, 0:4], a2[:, :, :, 0], c2[:, :, :, 1], ALU.subtract).then_inc(done, 1)
    dve.tensor_tensor(o[:, :, 4:8], c2[:, :, :, 0], a2[:, :, :, 1], ALU.add).then_inc(done, 1)


def self_attention0(nc, w, n):
    NQ = n.NQ
    VC = 32
    with ExitStack() as ctx:
        sb, sem = buffers(nc, ctx, "a0_")
        WQ, WK, WV, WO, bqk, bv, bo = n.WQ, n.WK, n.WV, n.WO, n.bqk, n.bv, n.bo
        loaded = n.self0_loaded
        stats, XN, XT = sb("stats", [128, 11]), sb("XN", [128, C]), sb("XT", [128, T])
        QK, SQ, RA, RB, QR = (sb(k, [128, 512]) for k in ("QK", "SQ", "RA", "RB", "QR"))
        SS, Y, A1, A2 = (sb(k, [128, 64]) for k in ("SS", "Y", "A1", "A2"))
        SI = sb("SI", [128, 64], I32)
        QT, KZ, V = sb("QT", [128, 2, NQ]), sb("KZ", [128, 2, R, T]), sb("V", [128, 2, BR * H * VC])
        WS, P = sb("WS", [128, 2, 2 * NQ]), sb("P", [128, 2, 2 * NQ])
        OT = sb("OT", [128, 2, NQ])
        NUM, RD, CX, CS, CT = sb("NUM", [128, 2, BR * H * (D + 1)]), sb("RD", [128, 64]), sb("CX", [128, 512]), sb("CS", [128, C]), sb("CT", [128, T])
        ps = ctx.enter_context(nc.psum_tensor("a0_ps", [128, 8 * BANK], F32))
        bank = [ps[:, k * BANK:(k + 1) * BANK] for k in range(8)]
        s = {k: sem(k) for k in NORM_SEMS}
        v_ones = sem("v_ones")
        xT_ps, xT, qkv_ps, qk, v_rows, sq, rs = (sem(k) for k in ("xT_ps", "xT", "qkv_ps", "qk", "v_rows", "sq", "rs"))
        qr, qkT_ps, qT, kz = (sem(k) for k in ("qr", "qkT_ps", "qT", "kz"))
        s_ps, w_done, p_done, pv_done, oT, oR_ps = (sem(k) for k in ("s_ps", "w_done", "p_done", "pv_done", "oT", "oR_ps"))
        v_zero = sem("v_zero")
        num3 = sem("num3")
        num, cs, cT_ps, cT, y_ps, x_new = (sem(k) for k in ("num", "cs", "cT_ps", "cT", "y_ps", "x_new"))
        RS, QRN, CSN = 14, 4, 3

        @nc_block(nc, ctx).sync
        def _(sp):
            start_lora(sp, w, n)

        @n.block.gpsimd
        def _(pool):
            norm_pool(pool, n, 0, stats, s)
            pool.memset(V[:], 0.0).then_inc(v_zero, 1)
            pool.wait_ge(v_zero, 1)
            pool.memset(V[:].rearrange("p t (h k) -> p (t h) k", k=VC)[:, :, D:D + 1], 1.0).then_inc(v_ones, 1)
            with pool.Fori(1, B) as b:
                norm_pool(pool, n, b, stats, s)

        @n.block.scalar
        def _(act):
            def a_xt(b, p):
                act.wait_ge(xT_ps, b + 1)
                act.activation(XT[:], bank[4][:, 0:T], ACT.Copy).then_inc(xT, 1)

            def a_sq(b, p):
                act.wait_ge(qk, b + 1)
                act.activation(SQ[:], QK[:], ACT.Square).then_inc(sq, 1)

            def a_qt(b, p):
                act.wait_ge(qkT_ps, b + 1)
                act.activation(QT[:, p], bank[4][:, 0:NQ], ACT.Copy).then_inc(qT, 1)

            def b_pair(b, m):
                act.wait_ge(w_done, 16 * b + 2 * m + 2)
                if not (type(b) is int and b == 0 and m < 2):
                    act.wait_ge(pv_done, 8 * b + m - 1)
                act.activation(P[:, m % 2], WS[:, m % 2], ACT.Exp).then_inc(p_done, 1)

            def b_ctx(b):
                act.wait_ge(cT_ps, b + 1)
                act.activation(CT[:], bank[5][:, 0:T], ACT.Copy).then_inc(cT, 1)

            def b_ot(b, r):
                act.wait_ge(pv_done, 8 * b + 2 * r + 2)
                if not peel(b, r, 2):
                    act.wait_ge(oR_ps, 4 * b + r - 1)
                act.activation(OT[:, r % 2], bank[6 + r % 2][:, 0:NQ], ACT.Copy).then_inc(oT, 1)

            def pairs(b, p, more=True):
                for m in range(8):
                    if m == 0 and not peel(b, 0, 1):
                        b_ot(b - 1, 3)
                    b_pair(b, m)
                    if m in (2, 4, 6):
                        b_ot(b, m // 2 - 1)
                    if m == 0 and more:
                        a_xt(b + 1, 1 - p)
                    if m == 1 and more:
                        a_sq(b + 1, 1 - p)
                    if m == 2 and not peel(b, 0, 1):
                        b_ctx(b - 1)
                    if m == 4 and more:
                        a_qt(b + 1, 1 - p)

            batches(act, pairs, lambda: (a_xt(0, 0), a_sq(0, 0), a_qt(0, 0)),
                    lambda: (pairs(B - 1, 1, False), b_ot(B - 1, 3), b_ctx(B - 1)))

        @n.block.tensor
        def _(pe):
            ident = n.CF[:, CI:CI + 128]

            def a_xt(b, p):
                pe.wait_ge(s["xn"], b + 1)
                if not (type(b) is int and b == 0):
                    pe.wait_ge(qT, b)
                    pe.wait_ge(kz, b)
                pe.transpose(bank[4][:, 0:T], XN[:], ident).then_inc(xT_ps, 1)

            def a_proj(b, p):
                pe.wait_ge(xT, b + 1)
                pe.matmul(bank[4][:, 0:NQ], XT[:], WQ[:], start=True, stop=True)
                pe.matmul(bank[4][:, NQ:512], XT[:], WK[:], start=True, stop=True)
                pe.matmul(bank[5], XT[:], WV[:], start=True, stop=True).then_inc(qkv_ps, 1)

            def a_qkt(b, p):
                pe.wait_ge(qr, QRN * (b + 1))
                if not (type(b) is int and b < 2):
                    pe.wait_ge(x_new, 2 * (b - 1))
                for j in range(3):
                    pe.transpose(bank[4][:, j * 128:(j + 1) * 128], QR[:, j * 128:(j + 1) * 128], ident)
                pe.transpose(bank[5][:, 0:128], QR[:, NQ:512], ident)
                v3 = V[:, p, 3 * H * VC:].rearrange("p (h k) -> p h k", k=VC)[:, :, 0:D + 1]
                pe.matmul(bank[5][:, 128:272].rearrange("p (h k) -> p h k", k=D + 1), n.CF[:, CONE:CONE + 128], v3, start=True, stop=True).then_inc(qkT_ps, 1)

            def score(b, p, k):
                g, r = k % G, k // G
                if k == 0:
                    pe.wait_ge(qT, b + 1)
                    pe.wait_ge(kz, b + 1)
                if not (type(b) is int and b == 0 and k < 4):
                    pe.wait_ge(w_done, 16 * b + k - 3)
                rows = slice(32 * g, 32 * g + 32)
                pe.matmul(bank[k % 4][:, 0:NQ], KZ[rows, p, r], QT[rows, p], start=True, stop=True).then_inc(s_ps, 1)

            def values(b, p, m):
                r = m // 2
                pe.wait_ge(p_done, 8 * b + m + 1)
                if m == 0:
                    pe.wait_ge(v_rows, b + 1)
                if m % 2 == 0 and not peel(b, r, 2):
                    pe.wait_ge(num, 4 * b + r - 1)
                for k in (2 * m, 2 * m + 1):
                    g = k % G
                    for br in range(3):
                        at = (k % 2) * NQ + br * T
                        v = (br * H + G * g + r) * VC
                        last = pe.matmul(bank[6 + r % 2][32 * g:32 * g + 32, br * T:(br + 1) * T], V[:, p, v:v + VC],
                                         P[:, m % 2, at:at + T], start=True, stop=True)
                last.then_inc(pv_done, 1)

            def turn_back(b, r):
                pe.wait_ge(oT, 4 * b + r + 1)
                for br in range(3):
                    last = pe.transpose(bank[6 + r % 2][:, br * T:(br + 1) * T], OT[:, r % 2, br * T:(br + 1) * T], ident)
                last.then_inc(oR_ps, 1)

            def b_transpose(b):
                pe.wait_ge(cs, CSN * (b + 1))
                pe.transpose(bank[5][:, 0:T], CS[:], ident).then_inc(cT_ps, 1)

            def b_project(b):
                pe.wait_ge(cT, b + 1)
                pe.matmul(bank[5][:, 128:128 + C], CT[:], WO[:], start=True, stop=True).then_inc(y_ps, 1)

            def pairs(b, p, more=True):
                for m in range(8):
                    if m < 6:
                        score(b, p, 2 * m + 4), score(b, p, 2 * m + 5)
                    elif more:
                        score(b + 1, 1 - p, 2 * m - 12), score(b + 1, 1 - p, 2 * m - 11)
                    if m == 0 and not peel(b, 0, 1):
                        turn_back(b - 1, 3)
                    if m == 0 and more:
                        a_xt(b + 1, 1 - p)
                    if m == 1 and more:
                        a_proj(b + 1, 1 - p)
                    if m == 2 and not peel(b, 0, 1):
                        if more:
                            pe.wait_ge(v_rows, b + 2)
                        b_transpose(b - 1)
                    if m == 3 and not peel(b, 0, 1):
                        b_project(b - 1)
                    values(b, p, m)
                    if m == 4 and more:
                        a_qkt(b + 1, 1 - p)
                    if m in (2, 4, 6):
                        turn_back(b, m // 2 - 1)

            def first():
                a_xt(0, 0)
                pe.wait_ge(loaded, 16 * 8)
                a_proj(0, 0), a_qkt(0, 0)
                for k in range(4):
                    score(0, 0, k)

            def last():
                pairs(B - 1, 1, False)
                turn_back(B - 1, 3)
                pe.wait_ge(x_new, 2 * (B - 1))
                b_transpose(B - 1), b_project(B - 1)

            batches(pe, pairs, first, last)

        @n.block.vector
        def _(dve):

            def a_bias(b, p):
                dve.wait_ge(qkv_ps, b + 1)
                dve.tensor_tensor(QK[:], bank[4], bqk[:], ALU.add).then_inc(qk, 1)
                out = V[:, p].rearrange("p (h k) -> p h k", k=VC)[:, :, 0:D]
                dve.tensor_tensor(out, bank[5].rearrange("p (h d) -> p h d", d=D), bv[:].rearrange("p (h d) -> p h d", d=D), ALU.add).then_inc(v_rows, 1)

            def a_rms(b, part):
                step = RS * b
                if part == 0:
                    dve.wait_ge(sq, b + 1)
                    dve.tensor_reduce(SS[:], SQ[:].rearrange("p (h d) -> p h d", d=D), AX.X, ALU.add).then_inc(rs, 1)
                    dve.wait_ge(rs, step + 1)
                    dve.tensor_scalar(SS[:, 0:48], SS[:, 0:48], 1.0 / D, RMS_EPS, ALU.mult, ALU.add).then_inc(rs, 1)
                    dve.wait_ge(rs, step + 2)
                    dve.tensor_scalar(SI[:], SS[:].bitcast(I32), 1, None, ALU.arith_shift_right).then_inc(rs, 1)
                    dve.wait_ge(rs, step + 3)
                    dve.tensor_scalar(Y[:].bitcast(I32), SI[:], -1.0, 1597463007.0, ALU.mult, ALU.add).then_inc(rs, 1)
                elif part < 4:
                    k = part - 1
                    dve.wait_ge(rs, step + 4 + 3 * k)
                    dve.tensor_tensor(A1[:], Y[:], Y[:], ALU.mult).then_inc(rs, 1)
                    dve.wait_ge(rs, step + 5 + 3 * k)
                    dve.scalar_tensor_tensor(A2[:], A1[:], -0.5, SS[:], ALU.mult, ALU.mult).then_inc(rs, 1)
                    dve.wait_ge(rs, step + 6 + 3 * k)
                    dve.scalar_tensor_tensor(Y[:], A2[:], 1.5, Y[:], ALU.add, ALU.mult).then_inc(rs, 1)
                else:
                    dve.wait_ge(rs, step + 13)
                    q3 = QK[:].rearrange("p (h d) -> p h d", d=D)
                    dve.tensor_tensor(q3, q3, Y[:].unsqueeze(2).to_broadcast([128, 64, D]), ALU.mult).then_inc(rs, 1)
                    dve.wait_ge(rs, step + 14)

            def a_rms_all(b):
                for part in range(5):
                    a_rms(b, part)

            def a_rope(b, p):
                rope(dve, QK[:], RA[:], RB[:], QR[:], 64, n, qr, QRN * b)

            def a_kz(b, p):
                dve.wait_ge(qkT_ps, b + 1)
                dve.tensor_tensor(NUM[:, p, 432:576], bank[5][:, 128:272], n.SINK[:, 432:576], ALU.add).then_inc(num3, 1)
                dve.tensor_tensor(KZ[:, p], bank[5][:, 0:T].unsqueeze(1).to_broadcast([128, R, T]),
                                  n.CF[:, CHM:CHM + R].unsqueeze(2).to_broadcast([128, R, T]), ALU.mult).then_inc(kz, 1)

            def b_mask(b, k):
                m = k // 2
                dve.wait_ge(s_ps, 16 * b + k + 1)
                if not (type(b) is int and b == 0 and m < 2):
                    dve.wait_ge(p_done, 8 * b + m - 1)
                dve.tensor_tensor(WS[:, m % 2, (k % 2) * NQ:(k % 2 + 1) * NQ], bank[k % 4][:, 0:NQ],
                                  n.CF[:, CM:CM + NQ], ALU.mult).then_inc(w_done, 1)

            def b_num(b, p, r):
                def of_round(a):
                    return a.rearrange("p (br g r k) -> p br g r k", br=BR, g=G, r=R)[:, 0:3, :, r, :]

                dve.wait_ge(oR_ps, 4 * b + r + 1)
                rows = bank[6 + r % 2][:, 0:NQ].rearrange("p (br g k) -> p br g k", br=3, g=G)[:, :, :, 0:D + 1]
                dve.tensor_tensor(of_round(NUM[:, p]), rows, of_round(n.SINK[:]), ALU.add).then_inc(num, 1)

            def b_sums(b, p, part):
                n3 = NUM[:, p].rearrange("p (h k) -> p h k", k=D + 1)
                if part == 0:
                    dve.wait_ge(num, 4 * (b + 1))
                    dve.wait_ge(num3, b + 1)
                    dve.reciprocal(RD[:].unsqueeze(2), n3[:, :, D:D + 1]).then_inc(cs, 1)
                    dve.wait_ge(cs, CSN * b + 1)
                    dve.tensor_tensor(CX[:].rearrange("p (h d) -> p h d", d=D), n3[:, :, 0:D],
                                      RD[:].unsqueeze(2).to_broadcast([128, 64, D]), ALU.mult).then_inc(cs, 1)
                else:
                    dve.wait_ge(cs, CSN * b + 2)
                    dve.tensor_reduce(CS[:], CX[:].rearrange("p (r c) -> p c r", r=BR), AX.X, ALU.add).then_inc(cs, 1)

            def b_out(b):
                dve.wait_ge(y_ps, b + 1)
                x = n.X[:, cols(b, C)]
                dve.scalar_tensor_tensor(x, bank[5][:, 128:128 + C], 1.0 / BR, x, ALU.mult, ALU.add).then_inc(x_new, 1)
                dve.wait_ge(x_new, 2 * b + 1)
                dve.tensor_tensor(x, x, bo[:], ALU.add).then_inc(x_new, 1)

            def masks(b, p, turn, more2, more):
                tail = not peel(b, 0, 1)
                for k in range(16):
                    b_mask(b, k)
                    if tail:
                        if k == 2:
                            b_num(b - 1, 1 - p, 3)
                        if k in (2, 3):
                            b_sums(b - 1, 1 - p, k - 2)
                        if k == 9:
                            b_out(b - 1)
                    if k in (7, 11, 15):
                        b_num(b, p, k // 4 - 1)
                    if more:
                        if k == 4:
                            a_bias(b + 1, 1 - p)
                        if 5 <= k < 10:
                            a_rms(b + 1, k - 5)
                        if k == 10:
                            a_rope(b + 1, 1 - p)
                        if k == 12:
                            a_kz(b + 1, 1 - p)
                    if more2:
                        if k == 13:
                            norm_stats(dve, n, b + 2, stats, s)
                        if k == 15:
                            norm_apply(dve, n, b + 2, XN[:], stats, s)

            def first():
                norm_vector(dve, n, 0, XN[:], stats, s)
                dve.wait_ge(xT_ps, 1)
                norm_vector(dve, n, 1, XN[:], stats, s)
                dve.wait_ge(loaded, 16 * 8)
                dve.wait_ge(v_ones, 1)
                a_bias(0, 0)
                a_rms_all(0)
                a_rope(0, 0), a_kz(0, 0)

            def last():
                b_num(B - 1, 1, 3)
                b_sums(B - 1, 1, 0), b_sums(B - 1, 1, 1)
                b_out(B - 1)
                dve.wait_ge(x_new, 2 * B)

            steps(dve, first, masks, last)


def cross_attention0(nc, w, n):
    SCALE = DX ** -0.5
    with ExitStack() as ctx:
        sb, sem = buffers(nc, ctx, "x0_")
        WKI, bo = sb("WKI", [CC, 1024]), sb("bo", [128, C])
        stats, XN, XT = sb("stats", [128, 11]), sb("XN", [128, C]), sb("XT", [128, T])
        CT, CTI, KTI = sb("CT", [CC, 2, L]), sb("CTI", [CC, B * LI]), sb("KTI", [128, PR, B * LI])
        QT, KT, V = sb("QT", [128, PR * T]), sb("KT", [128, PR * L]), sb("V", [L, 2, 1024])
        MX, SM, RD = sb("MX", [128, 2 * H]), sb("SM", [128, 2 * H]), sb("RD", [128, 2 * H])
        P = sb("P", [128, 2, H * L])
        PT, OT = sb("PT", [L, 2, 4 * T]), sb("OT", [128, PR * T])
        ps = ctx.enter_context(nc.psum_tensor("x0_ps", [128, 8 * BANK], F32))
        bank = [ps[:, k * BANK:(k + 1) * BANK] for k in range(8)]
        s = {k: sem(k) for k in NORM_SEMS}
        loaded = sem("loaded")
        ctx_in = [sem("ctx_even"), sem("ctx_odd")]
        vi_in = [sem("vi_even"), sem("vi_odd")]
        image_ps, image = sem("image_ps"), sem("image")
        xT_ps, xT, q_ps, qT, k_ps, kT, v_ps, v_rows = (sem(k) for k in ("xT_ps", "xT", "q_ps", "qT", "k_ps", "kT", "v_ps", "v_rows"))
        s_ps, mx, sub, p_exp, sm, p_norm = (sem(k) for k in ("s_ps", "mx", "sub", "p_exp", "sm", "p_norm"))
        pT_ps, pT, o_ps, oT, y_ps, x_new = (sem(k) for k in ("pT_ps", "pT", "o_ps", "oT", "y_ps", "x_new"))

        scores = ps[:, 0:4 * BANK].rearrange("p (k n) -> p k n", k=4)[:, :, 0:4 * L].rearrange("p k (h l) -> p k h l", h=4)

        keys = KT[:].rearrange("p (j l) -> p j l", l=L)

        def place(h):
            return 8 * (h % 2) + h // 2

        def spread(a):
            return a.rearrange("p (h t) -> p h t", t=2)

        @nc_block(nc, ctx).sync
        def _(sp):
            sp.dma_start(WKI[:], w["L0_xattn_Wk_ipa"]).then_inc(loaded, 16)
            sp.dma_start(CTI[:], w["ctx_img_T"]).then_inc(loaded, 16)
            sp.dma_start(bo[:], w["L0_xattn_bo"].rearrange("(o n) -> o n", o=1).to_broadcast([128, C])).then_inc(loaded, 16)

            def tokens(b, p, turn):
                if not (type(b) is int and b < 2):
                    sp.wait_ge(v_ps, 2 * (b - 1))
                sp.dma_start(CT[:, p, :], w["ctx_T"][bass.ds(b, 1)].rearrange("o c l -> c (o l)")).then_inc(ctx_in[p], 16)

            each_batch(sp, tokens)

        @n.block.gpsimd
        def _(pool):
            def f(b, p, turn):
                norm_pool(pool, n, b, stats, s)
                if not (type(b) is int and b < 2):
                    pool.wait_ge(o_ps, 4 * (b - 1))
                pool.dma_start(V[LO:L, p, :], n.vi_dram[cols(b, LI), :]).then_inc(vi_in[p], 16)

            each_batch(pool, f)

        @n.block.scalar
        def _(act):
            def a_xt(b, p):
                act.wait_ge(xT_ps, b + 1)
                act.activation(XT[:], bank[4][:, 0:T], ACT.Copy).then_inc(xT, 1)

            def a_q(b, half):
                act.wait_ge(q_ps, 2 * b + half + 1)
                act.activation(QT[:, half * BANK:(half + 1) * BANK], bank[4 + half], ACT.Copy).then_inc(qT, 1)

            def a_k(b, half):
                act.wait_ge(k_ps, 2 * b + half + 1)
                if half == 0:
                    act.activation(keys[:, :, LO:L], KTI[:, :, cols(b, LI)], ACT.Copy).then_inc(kT, 1)
                act.activation(keys[:, 4 * half:4 * half + 4, 0:LO], bank[4 + half][:, 0:4 * LO].rearrange("p (j l) -> p j l", l=LO), ACT.Copy).then_inc(kT, 1)

            def a_v(b, p, half):
                act.wait_ge(v_ps, 2 * b + half + 1)
                act.activation(V[0:LO, p, half * BANK:(half + 1) * BANK], bank[4 + half][0:LO, :], ACT.Copy).then_inc(v_rows, 1)

            def a_exp(b, p):
                act.wait_ge(sub, 2 * (b + 1))
                act.activation(P[:, p, :], P[:, p, :], ACT.Exp, scale=SCALE).then_inc(p_exp, 1)

            def b_pt(b, p, g):
                act.wait_ge(pT_ps, 4 * b + g + 1)
                if not peel(b, g, 2):
                    act.wait_ge(o_ps, 4 * b + g - 1)
                act.activation(PT[:, g % 2, :], bank[6][0:L, :], ACT.Copy).then_inc(pT, 1)

            def step(b, p, turn, projections, scores):
                if projections:
                    a_xt(b + 2, p), a_q(b + 2, 0)
                b_pt(b, p, 0)
                if projections:
                    a_q(b + 2, 1)
                b_pt(b, p, 1)
                if projections:
                    a_k(b + 2, 0)
                b_pt(b, p, 2)
                if projections:
                    a_k(b + 2, 1)
                if scores:
                    a_v(b + 1, 1 - p, 0)
                b_pt(b, p, 3)
                if scores:
                    a_v(b + 1, 1 - p, 1), a_exp(b + 1, 1 - p)

            def first():
                act.wait_ge(image_ps, 1)
                act.activation(KTI[:].rearrange("p j l -> p (j l)"), bank[6][:, 0:PR * B * LI], ACT.Copy).then_inc(image, 1)
                a_xt(0, 0), a_q(0, 0), a_q(0, 1)
                act.wait_ge(image, 1)
                a_k(0, 0), a_k(0, 1)
                a_xt(1, 1), a_q(1, 0), a_q(1, 1), a_k(1, 0), a_k(1, 1)
                a_v(0, 0, 0), a_v(0, 0, 1), a_exp(0, 0)

            steps(act, first, step, lambda: None)

        @n.block.tensor
        def _(pe):
            ident = n.CF[:, CI:CI + 128]

            def a_xt(b, p):
                pe.wait_ge(s["xn"], b + 1)
                if not peel(b, 0, 1):
                    pe.wait_ge(kT, 3 * b)
                if not (type(b) is int and b < 2):
                    pe.wait_ge(v_rows, 2 * (b - 1))
                pe.transpose(bank[4][:, 0:T], XN[:], ident).then_inc(xT_ps, 1)

            def a_q(b, half):
                if half == 0:
                    pe.wait_ge(xT, b + 1)
                for j in range(4):
                    last = pe.matmul(bank[4 + half][:, j * T:(j + 1) * T], n.WQX[:, (4 * half + j) * 128:(4 * half + j + 1) * 128], XT[:],
                                     start=True, stop=True)
                last.then_inc(q_ps, 1)

            def a_k(b, p, half, turn):
                pe.wait_ge(qT, 2 * b + half + 1)
                pe.wait_ge(ctx_in[p], 16 * (turn + 1))
                for j in range(4):
                    last = pe.matmul(bank[4 + half][:, j * LO:(j + 1) * LO], n.WKX[:, (4 * half + j) * 128:(4 * half + j + 1) * 128], CT[:, p, 0:LO],
                                     start=True, stop=True)
                last.then_inc(k_ps, 1)

            def a_v(b, p, half, keys_read):
                pe.wait_ge(kT, keys_read)
                pe.matmul(bank[4 + half][0:LO, :], CT[:, p, 0:LO], n.WVX[:, half * BANK:(half + 1) * BANK],
                          start=True, stop=True).then_inc(v_ps, 1)

            def a_scores(b, p):
                pe.wait_ge(kT, 3 * (b + 1))
                if not peel(b, 0, 1):
                    pe.wait_ge(sub, 2 * b)
                for h in range(H):
                    rows = slice(DX * (h % 2), DX * (h % 2) + DX)
                    j = h // 2
                    at = place(h) // 4 * BANK + place(h) % 4 * L
                    last = pe.matmul(ps[:, at:at + L], QT[rows, j * T:(j + 1) * T], KT[rows, j * L:(j + 1) * L], start=True, stop=True)
                last.then_inc(s_ps, 1)

            def b_pt(b, p, g):
                if g == 0:
                    pe.wait_ge(p_norm, 2 * (b + 1))
                if not peel(b, g, 1):
                    pe.wait_ge(pT, 4 * b + g)
                if g == 0 and not peel(b, 0, 1):
                    pe.wait_ge(x_new, 2 * b)
                for k in range(4):
                    h = 4 * g + k
                    last = pe.transpose(bank[6][0:L, k * T:(k + 1) * T], P[:, p, place(h) * L:(place(h) + 1) * L], ident)
                last.then_inc(pT_ps, 1)

            def b_pv(b, p, g, turn):
                pe.wait_ge(pT, 4 * b + g + 1)
                if g == 0:
                    pe.wait_ge(vi_in[p], 16 * (turn + 1))
                    pe.wait_ge(v_rows, 2 * (b + 1))
                if g % 2 == 0 and not peel(b, g, 1):
                    pe.wait_ge(oT, 2 * b + g // 2)
                for k in range(4):
                    h = 4 * g + k
                    at = (2 * (g % 2) + k // 2) * T
                    last = pe.matmul(bank[7][DX * (h % 2):DX * (h % 2) + DX, at:at + T],
                                     V[:, p, h * DX:(h + 1) * DX], PT[:, g % 2, k * T:(k + 1) * T], start=True, stop=True)
                last.then_inc(o_ps, 1)

            def b_out(b):
                pe.wait_ge(oT, 2 * (b + 1))
                pe.wait_ge(pT, 4 * (b + 1))
                for j in range(PR):
                    last = pe.matmul(bank[6][:, 0:C], OT[:, j * T:(j + 1) * T], n.WOX[:, j * C:(j + 1) * C],
                                     start=(j == 0), stop=(j == PR - 1))
                last.then_inc(y_ps, 1)

            pe.wait_ge(loaded, 48)

            def step(b, p, turn, projections, scores):
                keys_read = 3 * (b + 3) if projections else 3 * B
                if scores:
                    a_scores(b + 1, 1 - p)
                if projections:
                    a_xt(b + 2, p)
                if not peel(b, 0, 1):
                    b_out(b - 1)
                if projections:
                    a_q(b + 2, 0)
                b_pt(b, p, 0)
                if projections:
                    a_q(b + 2, 1)
                b_pv(b, p, 0, turn)
                b_pt(b, p, 1)
                if projections:
                    a_k(b + 2, p, 0, turn + 1)
                b_pv(b, p, 1, turn)
                b_pt(b, p, 2)
                if projections:
                    a_k(b + 2, p, 1, turn + 1)
                b_pv(b, p, 2, turn)
                if scores:
                    a_v(b + 1, 1 - p, 0, keys_read - 1)
                b_pt(b, p, 3)
                if scores:
                    a_v(b + 1, 1 - p, 1, keys_read)
                b_pv(b, p, 3, turn)

            def first():
                for j in range(PR):
                    last = pe.matmul(bank[6][:, j * B * LI:(j + 1) * B * LI], WKI[:, j * 128:(j + 1) * 128], CTI[:], start=True, stop=True)
                last.then_inc(image_ps, 1)
                a_xt(0, 0), a_q(0, 0), a_q(0, 1), a_k(0, 0, 0, 0), a_k(0, 0, 1, 0)
                a_scores(0, 0)
                a_xt(1, 1), a_q(1, 0), a_q(1, 1), a_k(1, 1, 0, 0), a_k(1, 1, 1, 0)
                a_v(0, 0, 0, 5), a_v(0, 0, 1, 6)
                pe.wait_ge(image, 1)

            steps(pe, first, step, lambda: b_out(B - 1))

        @n.block.vector
        def _(dve):
            def a_norm(b, p):
                if not peel(b, 0, 1):
                    dve.wait_ge(xT_ps, b)
                norm_vector(dve, n, b, XN[:], stats, s)

            def a_softmax1(b, p):
                dve.wait_ge(s_ps, b + 1)
                m4 = MX[:].rearrange("p (k h t) -> p k h t", k=4, t=2)
                p4 = P[:, p, :].rearrange("p (k h l) -> p k h l", k=4, l=L)
                dve.tensor_reduce(m4[:, :, :, 0], scores[:, :, :, 0:LO], AX.X, ALU.max).then_inc(mx, 1)
                dve.tensor_reduce(m4[:, :, :, 1], scores[:, :, :, LO:L], AX.X, ALU.max).then_inc(mx, 1)
                dve.wait_ge(mx, 2 * (b + 1))
                for t, (lo, hi) in enumerate(((0, LO), (LO, L))):
                    dve.tensor_tensor(p4[:, :, :, lo:hi], scores[:, :, :, lo:hi],
                                      m4[:, :, :, t:t + 1].to_broadcast([128, 4, 4, hi - lo]), ALU.subtract).then_inc(sub, 1)

            def a_softmax2(b, p):
                dve.wait_ge(p_exp, b + 1)
                p3 = P[:, p, :].rearrange("p (h l) -> p h l", l=L)
                sums = spread(SM[:])
                dve.tensor_reduce(sums[:, :, 0], p3[:, :, 0:LO], AX.X, ALU.add).then_inc(sm, 1)
                dve.tensor_reduce(sums[:, :, 1], p3[:, :, LO:L], AX.X, ALU.add).then_inc(sm, 1)
                dve.wait_ge(sm, 3 * b + 2)
                dve.reciprocal(RD[:], SM[:]).then_inc(sm, 1)
                dve.wait_ge(sm, 3 * b + 3)
                rd = spread(RD[:])
                for t, (lo, hi) in enumerate(((0, LO), (LO, L))):
                    dve.tensor_tensor(p3[:, :, lo:hi], p3[:, :, lo:hi], rd[:, :, t:t + 1].to_broadcast([128, H, hi - lo]), ALU.mult).then_inc(p_norm, 1)

            def b_ot(b, g):
                dve.wait_ge(o_ps, 4 * b + 2 * g + 2)
                if g == 0 and not peel(b, 0, 1):
                    dve.wait_ge(y_ps, b)
                dve.tensor_copy(OT[:, 4 * g * T:4 * (g + 1) * T], bank[7]).then_inc(oT, 1)

            def b_out(b):
                dve.wait_ge(y_ps, b + 1)
                x = n.X[:, cols(b, C)]
                dve.tensor_tensor(x, bank[6][:, 0:C], x, ALU.add).then_inc(x_new, 1)
                dve.wait_ge(x_new, 2 * b + 1)
                dve.tensor_tensor(x, x, bo[:], ALU.add).then_inc(x_new, 1)

            dve.wait_ge(loaded, 48)

            def first():
                a_norm(0, 0), a_norm(1, 1), a_softmax1(0, 0)

            def step(b, p, turn, projections, scores):
                if projections:
                    a_norm(b + 2, p)
                a_softmax2(b, p)
                if not peel(b, 0, 1):
                    b_out(b - 1)
                if scores:
                    a_softmax1(b + 1, 1 - p)
                b_ot(b, 0), b_ot(b, 1)

            def last():
                b_out(B - 1)
                dve.wait_ge(x_new, 2 * B)

            steps(dve, first, step, last)


def each_batch(eng, f):
    f(0, 0, 0)
    f(1, 1, 0)
    with eng.Fori(1, B // 2) as i:
        f(2 * i, 0, i)
        f(2 * i + 1, 1, i)


def carry_wait(dve, n, sem, value, spare):
    dve.wait_ge(sem, value)
    dve.tensor_copy(spare, n.EPS[:])


def group_weights(w, n, g):
    k = E // NG0
    return [(dst[:, g * k:(g + 1) * k, :], w["L0_ffn_w_" + name][g * k:(g + 1) * k].rearrange("e h f -> h e f"))
            for dst, name in ((n.WG, "gate"), (n.WU, "up"), (n.WD, "down"))]


def route0(nc, w, n):
    with ExitStack() as ctx:
        sb, sem = buffers(nc, ctx, "r0_")
        WR, ZERO = sb("WR", [128, E]), sb("ZERO", [128, 1280])
        stats, XN, XT = sb("stats", [128, B, 10]), sb("XN", [128, B, C]), sb("XT", [128, B * T])
        LG, TOP, IDX, IDF = sb("LG", [128, B, E]), sb("TOP", [128, B, 8]), sb("IDX", [128, B, 8], U32), sb("IDF", [128, B, 1])
        EX, PC = sb("EX", [128, B, E]), sb("PC", [128, B, E])
        SE, CNT, OV, SL = (sb(k, [128, B]) for k in ("SE", "CNT", "OV", "SL"))
        OH = sb("OH", [128, B, E], BF16)
        ps = ctx.enter_context(nc.psum_tensor("r0_ps", [128, 4 * BANK], F32))
        bank = [ps[:, k * BANK:(k + 1) * BANK] for k in range(4)]
        s = {k: sem(k) for k in NORM_SEMS}
        loaded, zeroed, cleared, scattered = sem("loaded"), sem("zeroed"), sem("cleared"), sem("scattered")
        xT_ps, xT, l_ps, lg, top, idx, idf, less, ex, se = (sem(k) for k in ("xT_ps", "xT", "l_ps", "lg", "top", "idx", "idf", "less", "ex", "se"))
        one_hot, pos_ps, own, count, over, slot, x_sum = (sem(k) for k in ("one_hot", "pos_ps", "own", "count", "over", "slot", "x_sum"))
        logits = bank[2][:, 0:B * E].rearrange("p (b e) -> p b e", e=E)
        place = bank[3][:, 0:B * E].rearrange("p (b e) -> p b e", e=E)

        @nc_block(nc, ctx).sync
        def _(sp):
            sp.dma_start(WR[:], w["L0_ffn_w_router"]).then_inc(loaded, 16)
            sp.wait_ge(zeroed, 1)
            sp.dma_start(n.buf_dram.rearrange("(p k) c -> p (k c)", p=128), ZERO[:]).then_inc(cleared, 16)
            for g in range(NG0):
                for dma in group_weights(w, n, g):
                    sp.dma_start(*dma).then_inc(n.w_in[g], 16)
            sp.wait_ge(scattered, 16 * B)

        @n.block.gpsimd
        def _(pool):
            pool.memset(ZERO[:], 0.0).then_inc(zeroed, 1)
            norm_all_pool(pool, n, stats, s)
            pool.wait_ge(s["xn"], B)
            pool.tensor_tensor(n.X[:], n.X[:], XN[:].rearrange("p b c -> p (b c)"), ALU.add).then_inc(x_sum, 1)
            pool.wait_ge(cleared, 16)
            pool.wait_ge(slot, 1)
            for b in range(B):
                pool.indirect_dma_start(out=n.buf_dram, out_offset=bass.IndirectOffsetOnAxis(ap=n.SLOT[:, b:b + 1].bitcast(U32), axis=0),
                                        in_=XN[:, b, :], in_offset=None, bounds_check=E * CAP0 - 1,
                                        oob_is_err=False).then_inc(scattered, 16)
            pool.wait_ge(x_sum, 1)

        @n.block.scalar
        def _(act):
            for q in range(2):
                act.wait_ge(xT_ps, q + 1)
                act.activation(XT[:, q * BANK:(q + 1) * BANK], bank[q], ACT.Copy).then_inc(xT, 1)
            act.wait_ge(less, 1)
            act.activation(EX[:], EX[:], ACT.Exp).then_inc(ex, 1)

        @n.block.tensor
        def _(pe):
            for b in range(B):
                pe.wait_ge(s["xn"], b + 1)
                last = pe.transpose(bank[b // 4][:, (b % 4) * T:(b % 4 + 1) * T], XN[:, b], n.CF[:, CI:CI + 128])
                if b % 4 == 3:
                    last.then_inc(xT_ps, 1)
            pe.wait_ge(loaded, 16)
            for b in range(B):
                pe.wait_ge(xT, b // 4 + 1)
                last = pe.matmul(bank[2][:, b * E:(b + 1) * E], XT[:, b * T:(b + 1) * T], WR[:], start=True, stop=True)
            last.then_inc(l_ps, 1)
            count_places(pe, n, OH, bank[3], one_hot).then_inc(pos_ps, 1)

        @n.block.vector
        def _(dve):
            norm_all_vector(dve, n, XN, stats, s)
            dve.wait_ge(l_ps, 1)
            dve.tensor_copy(LG[:], logits).then_inc(lg, 1)
            dve.wait_ge(lg, 1)
            for b in range(B):
                dve.max(TOP[:, b], LG[:, b]).then_inc(top, 1)
            dve.wait_ge(top, B)
            for b in range(B):
                dve.max_index(IDX[:, b], TOP[:, b], LG[:, b]).then_inc(idx, 1)
            dve.tensor_tensor(EX[:], LG[:], TOP[:, :, 0:1].to_broadcast([128, B, E]), ALU.subtract).then_inc(less, 1)
            dve.wait_ge(idx, B)
            dve.tensor_copy(IDF[:], IDX[:, :, 0:1]).then_inc(idf, 1)
            dve.wait_ge(idf, 1)
            iota = n.CF[:, CIOTA:CIOTA + E].unsqueeze(1).to_broadcast([128, B, E])
            dve.tensor_tensor(OH[:], iota, IDF[:].to_broadcast([128, B, E]), ALU.is_equal).then_inc(one_hot, 1)
            dve.wait_ge(ex, 1)
            dve.tensor_reduce(SE[:], EX[:], AX.X, ALU.add).then_inc(se, 1)
            dve.wait_ge(se, 1)
            dve.reciprocal(n.GATE[:], SE[:]).then_inc(se, 1)
            dve.wait_ge(pos_ps, 1)
            dve.wait_ge(one_hot, 1)
            dve.tensor_tensor(PC[:], place, OH[:], ALU.mult).then_inc(own, 1)
            dve.wait_ge(own, 1)
            dve.tensor_reduce(CNT[:], PC[:], AX.X, ALU.add).then_inc(count, 1)
            dve.wait_ge(count, 1)
            dve.tensor_scalar(OV[:], CNT[:], CAP0 + 0.5, BIG, ALU.is_gt, ALU.mult).then_inc(over, 1)
            dve.scalar_tensor_tensor(SL[:], IDF[:].rearrange("p b o -> p (b o)"), float(CAP0), CNT[:], ALU.mult, ALU.add).then_inc(over, 1)
            dve.wait_ge(over, 2)
            dve.scalar_tensor_tensor(n.SLOT[:], SL[:], -1.0, OV[:], ALU.add, ALU.add).then_inc(slot, 1)
            dve.wait_ge(se, 2)
            dve.wait_ge(slot, 1)


def count_places(pe, n, chosen, bank, ready):
    pe.wait_ge(ready, 1)
    pe.matmul(bank[:, 0:B * E], n.CB[:, BTRI:BTRI + 128], chosen[:].rearrange("p b e -> p (b e)"), start=True, stop=False)
    for b in range(B - 1):
        rest = B - 1 - b
        last = pe.matmul(bank[:, (b + 1) * E:B * E].rearrange("p (b e) -> p b e", e=E), n.CB[:, BONE:BONE + 128],
                         chosen[:, b:b + 1].to_broadcast([128, rest, E]), start=False, stop=b == B - 2)
    return last


def experts0(nc, w, n):
    NG, K = NG0, E // NG0
    with ExitStack() as ctx:
        sb, sem = buffers(nc, ctx, "e0_")
        ROWS, BT = sb("ROWS", [128, 10 * C]), sb("BT", [128, E * CAP0])
        SG, HT, Y = sb("SG", [128, 2, K * CAP0]), sb("HT", [128, 2, K * CAP0]), sb("Y", [CAP0, 2, K * C])
        ps = ctx.enter_context(nc.psum_tensor("e0_ps", [128, 8 * BANK], F32))
        bank = [ps[:, k * BANK:(k + 1) * BANK] for k in range(8)]
        rows, rT_ps, bT = sem("rows"), sem("rT_ps"), sem("bT")
        y_out = [sem("y_even"), sem("y_odd")]
        gu_ps, silu, h, y_ps, y = (sem(k) for k in ("gu_ps", "silu", "h", "y_ps", "y"))

        def each_group(eng, f):
            f(0, 0, 0)
            f(1, 1, 0)
            with eng.Fori(1, NG // 2) as i:
                f(2 * i, 0, i)
                f(2 * i + 1, 1, i)

        @nc_block(nc, ctx).sync
        def _(sp):
            sp.dma_start(ROWS[:].rearrange("p (k c) -> p k c", c=C), n.buf_dram.rearrange("(k p) c -> p k c", p=128)).then_inc(rows, 16)

        @n.block.gpsimd
        def _(pool):
            def f(g, p, turn):
                pool.wait_ge(y, g + 1)
                pool.dma_start(n.y_dram[cols(g, K * CAP0), :].rearrange("(e c) d -> c e d", e=K),
                               Y[:, p].rearrange("c (e d) -> c e d", e=K)).then_inc(y_out[p], 16)

            each_group(pool, f)
            for p in range(2):
                pool.wait_ge(y_out[p], 16 * NG // 2)

        @n.block.scalar
        def _(act):
            for k in range(3):
                act.wait_ge(rT_ps, k + 1)
                m = min(4, 10 - 4 * k) * 128
                act.activation(BT[:, k * 512:k * 512 + m], bank[6 + k % 2][:, 0:m], ACT.Copy).then_inc(bT, 1)

            def f(g, p, turn):
                act.wait_ge(gu_ps, g + 1)
                act.activation(SG[:, p], bank[2 * p][:, 0:K * CAP0], ACT.Silu).then_inc(silu, 1)
                act.wait_ge(y_ps, g + 1)
                if not (type(g) is int and g < 2):
                    act.wait_ge(y_out[p], 16 * turn)
                act.activation(Y[:, p], bank[4 + p][0:CAP0, :], ACT.Copy).then_inc(y, 1)

            each_group(act, f)

        @n.block.tensor
        def _(pe):
            pe.wait_ge(rows, 16)
            for k in range(3):
                if k == 2:
                    pe.wait_ge(bT, 1)
                for j in range(min(4, 10 - 4 * k)):
                    last = pe.transpose(bank[6 + k % 2][:, j * 128:(j + 1) * 128], ROWS[:, (4 * k + j) * C:(4 * k + j + 1) * C], n.CF[:, CI:CI + 128])
                last.then_inc(rT_ps, 1)
            pe.wait_ge(bT, 3)

            def gate_up(g):
                p = g % 2
                pe.wait_ge(n.w_in[g], 48)
                if g >= 2:
                    pe.wait_ge(h, g - 1)
                for j in range(K):
                    e = g * K + j
                    x = BT[:, e * CAP0:(e + 1) * CAP0]
                    pe.matmul(bank[2 * p][:, j * CAP0:(j + 1) * CAP0], n.WG[:, e], x, start=True, stop=True)
                    last = pe.matmul(bank[2 * p + 1][:, j * CAP0:(j + 1) * CAP0], n.WU[:, e], x, start=True, stop=True)
                last.then_inc(gu_ps, 1)

            def down(g):
                p = g % 2
                pe.wait_ge(h, g + 1)
                if g >= 2:
                    pe.wait_ge(y, g - 1)
                for j in range(K):
                    last = pe.matmul(bank[4 + p][0:CAP0, j * C:(j + 1) * C], HT[:, p, j * CAP0:(j + 1) * CAP0],
                                     n.WD[:, g * K + j], start=True, stop=True)
                last.then_inc(y_ps, 1)

            gate_up(0)
            for g in range(NG):
                if g + 1 < NG:
                    gate_up(g + 1)
                down(g)

        @n.block.vector
        def _(dve):
            def f(g, p, turn):
                dve.wait_ge(silu, g + 1)
                if not (type(g) is int and g < 2):
                    dve.wait_ge(y_ps, g - 1)
                dve.tensor_tensor(HT[:, p], bank[2 * p + 1][:, 0:K * CAP0], SG[:, p], ALU.mult).then_inc(h, 1)

            each_group(dve, f)


def combine0(nc, w, n):
    with ExitStack() as ctx:
        sb, sem = buffers(nc, ctx, "c0_")
        GY = sb("GY", [128, B * C])
        cleared, summed = sem("cleared"), sem("summed")
        got = [sem(f"got{b}") for b in range(B)]

        @nc_block(nc, ctx).gpsimd
        def _(pool):
            pool.wait_ge(cleared, 1)
            for b in range(B):
                pool.indirect_dma_start(out=GY[:, b * C:(b + 1) * C], out_offset=None, in_=n.y_dram,
                                        in_offset=bass.IndirectOffsetOnAxis(ap=n.SLOT[:, b:b + 1].bitcast(U32), axis=0),
                                        bounds_check=E * CAP0 - 1, oob_is_err=False).then_inc(got[b], 16)

        @n.block.vector
        def _(dve):
            dve.memset(GY[:], 0.0).then_inc(cleared, 1)
            for b in range(B):
                dve.wait_ge(got[b], 16)
                x = n.X[:, b * C:(b + 1) * C]
                dve.scalar_tensor_tensor(x, GY[:, b * C:(b + 1) * C], n.GATE[:, b:b + 1], x, ALU.mult, ALU.add).then_inc(summed, 1)
            dve.wait_ge(summed, B)


def experts_layer0(nc, w, n):
    with ExitStack() as ctx:
        sb, sem = buffers(nc, ctx, "l0_")
        n.WG, n.WU, n.WD = (sb(k, [128, E, 128]) for k in ("WG", "WU", "WD"))
        n.w_in = [sem(f"w_in{g}") for g in range(NG0)]
        route0(nc, w, n)
        experts0(nc, w, n)
        combine0(nc, w, n)


def attention1(nc, w, n, cross):
    SCALE = D ** -0.5
    LK = L if cross else T
    VC = 32
    tag = "x1_" if cross else "a1_"
    with ExitStack() as ctx:
        sb, sem = buffers(nc, ctx, tag)
        stats, XN, XT = sb("stats", [128, 11]), sb("XN", [128, C]), sb("XT", [128, T])
        WO, bo = sb("WO", [128, C]), sb("bo", [128, C])
        if cross:
            WQ, WK, WV = sb("WQ", [128, C]), sb("WK", [CC, C]), sb("WV", [CC, C])
            bq, bk, bv = sb("bq", [128, 1]), sb("bk", [128, 1]), sb("bv", [L, C])
            CT = sb("CT", [CC, 2, L])
        else:
            WQKV, bqkv = sb("WQKV", [128, 3 * C]), sb("bqkv", [128, 3 * C])
            QK, RA, RB, QR = (sb(k, [128, 2 * C]) for k in ("QK", "RA", "RB", "QR"))
        VB = sb("VB", [LK, C])
        QT, KZ, V = sb("QT", [128, T]), sb("KZ", [128, R * LK]), sb("V", [LK, 2, H * VC])
        MX, P = sb("MX", [128, H]), sb("P", [128, 2, H * LK])
        PT, OT = sb("PT", [LK, 2, 4 * T]), sb("OT", [128, G * T])
        RD, CX, CTX = sb("RD", [128, H]), sb("CX", [128, C]), sb("CTX", [128, T])
        ps = ctx.enter_context(nc.psum_tensor(tag + "ps", [128, 8 * BANK], F32))
        bank = [ps[:, k * BANK:(k + 1) * BANK] for k in range(8)]
        s = {k: sem(k) for k in NORM_SEMS}
        loaded, v_zero, v_ones = sem("loaded"), sem("v_zero"), sem("v_ones")
        ctx_in = [sem("ctx_even"), sem("ctx_odd")]
        xT_ps, xT, proj_ps, v_copied, v_rows, qk, qr, qkT_ps, qT, kz = (sem(k) for k in ("xT_ps", "xT", "proj_ps", "v_copied", "v_rows", "qk", "qr", "qkT_ps", "qT", "kz"))
        s_ps, mx, sub, p_exp = (sem(k) for k in ("s_ps", "mx", "sub", "p_exp"))
        pT_ps, pT, o_ps, oT, oR_ps, cx, cT_ps, cT, y_ps, x_new = (sem(k) for k in ("pT_ps", "pT", "o_ps", "oT", "oR_ps", "cx", "cT_ps", "cT", "y_ps", "x_new"))
        scores = ps[:, 0:4 * BANK].rearrange("p (g n) -> p g n", g=4)[:, :, 0:R * LK].rearrange("p g (r l) -> p g r l", r=R)
        NL = 8 if cross else 4
        NSUB = 2 if cross else 1

        @nc_block(nc, ctx).sync
        def _(sp):
            row = lambda a: a.rearrange("(o n) -> o n", o=1)
            if cross:
                for dst, name in ((WQ, "Wq"), (WK, "Wk"), (WV, "Wv"), (WO, "Wo")):
                    sp.dma_start(dst[:], w["L1_xattn_" + name]).then_inc(loaded, 16)
                sp.dma_start(bq[:], w["L1_xattn_bq"].rearrange("(n o) -> n o", o=1)).then_inc(loaded, 16)
                sp.dma_start(bk[:], w["L1_xattn_bk"].rearrange("(n o) -> n o", o=1)).then_inc(loaded, 16)
                sp.dma_start(bv[:], row(w["L1_xattn_bv"]).to_broadcast([L, C])).then_inc(loaded, 16)
                sp.dma_start(bo[:], row(w["L1_xattn_bo"]).to_broadcast([128, C])).then_inc(loaded, 16)

                def a(b, p, turn):
                    if not peel(b, p, 2):
                        sp.wait_ge(proj_ps, b - 1)
                    sp.dma_start(CT[:, p, :], w["ctx_T"][bass.ds(b, 1)].rearrange("o c l -> c (o l)")).then_inc(ctx_in[p], 16)

                each_batch(sp, a)
            else:
                sp.dma_start(WQKV[:], w["L1_attn_wqkv_T"]).then_inc(loaded, 16)
                sp.dma_start(WO[:], w["L1_attn_wp_T"]).then_inc(loaded, 16)
                sp.dma_start(bqkv[:], row(w["L1_attn_bqkv"]).to_broadcast([128, 3 * C])).then_inc(loaded, 16)
                sp.dma_start(bo[:], row(w["L1_attn_bp"]).to_broadcast([128, C])).then_inc(loaded, 16)

        @n.block.gpsimd
        def _(pool):
            pool.memset(V[:], 0.0).then_inc(v_zero, 1)
            pool.wait_ge(v_zero, 1)
            pool.memset(V[:].rearrange("p t (h k) -> p (t h) k", k=VC)[:, :, D:D + 1], 1.0).then_inc(v_ones, 1)

            def f(b, p, turn):
                norm_pool(pool, n, b, stats, s)
                pool.wait_ge(v_copied, b + 1)
                if not (type(b) is int and b < 2):
                    pool.wait_ge(o_ps, 4 * (b - 1))
                bias = bv[:] if cross else bqkv[:, 2 * C:3 * C]
                pool.tensor_tensor(V[:, p].rearrange("p (h k) -> p h k", k=VC)[:, :, 0:D], VB[:].rearrange("p (h d) -> p h d", d=D),
                                   bias.rearrange("p (h d) -> p h d", d=D), ALU.add).then_inc(v_rows, 1)

            pool.wait_ge(v_ones, 1)
            pool.wait_ge(loaded, 16 * NL)
            each_batch(pool, f)

        @n.block.scalar
        def _(act):
            def a_xt(b, p):
                act.wait_ge(xT_ps, b + 1)
                act.activation(XT[:], bank[4][:, 0:T], ACT.Copy).then_inc(xT, 1)

            def a_q(b, p):
                if cross:
                    act.wait_ge(proj_ps, b + 1)
                    act.activation(QT[:], bank[4][:, 0:T], ACT.Identity, bias=bq[:]).then_inc(qT, 1)
                else:
                    act.wait_ge(qkT_ps, b + 1)
                    act.activation(QT[:], bank[4][:, 0:T], ACT.Copy).then_inc(qT, 1)

            def a_exp(b, p):
                act.wait_ge(sub, NSUB * (b + 1))
                act.activation(P[:, p, :], P[:, p, :], ACT.Exp, scale=SCALE).then_inc(p_exp, 1)

            def b_pt(b, p, g):
                act.wait_ge(pT_ps, 4 * b + g + 1)
                if not peel(b, g, 2):
                    act.wait_ge(o_ps, 4 * b + g - 1)
                act.activation(PT[:, g % 2, :], bank[6][0:LK, :], ACT.Copy).then_inc(pT, 1)

            def b_ot(b):
                act.wait_ge(o_ps, 4 * (b + 1))
                if not peel(b, 0, 1):
                    act.wait_ge(oR_ps, b)
                act.activation(OT[:], bank[7], ACT.Copy).then_inc(oT, 1)

            def b_ctx(b):
                act.wait_ge(cT_ps, b + 1)
                act.activation(CTX[:], bank[5][:, 0:T], ACT.Copy).then_inc(cT, 1)

            def step(b, p, turn, projections, scores):
                if projections:
                    a_xt(b + 2, p)
                tail = not peel(b, 0, 1)
                b_pt(b, p, 0)
                if tail and not cross:
                    b_ctx(b - 1)
                b_pt(b, p, 1)
                if projections and cross:
                    a_q(b + 2, p)
                if tail and cross:
                    b_ctx(b - 1)
                b_pt(b, p, 2)
                if projections and not cross:
                    a_q(b + 2, p)
                b_pt(b, p, 3)
                b_ot(b)
                if scores:
                    a_exp(b + 1, 1 - p)

            steps(act, lambda: (a_xt(0, 0), a_q(0, 0), a_xt(1, 1), a_exp(0, 0), a_q(1, 1)), step, lambda: b_ctx(B - 1))

        @n.block.tensor
        def _(pe):
            ident = n.CF[:, CI:CI + 128]

            def a_xt(b, p):
                pe.wait_ge(s["xn"], b + 1)
                if not peel(b, 0, 1):
                    pe.wait_ge(qT, b)
                    pe.wait_ge(kz, b)
                pe.transpose(bank[4][:, 0:T], XN[:], ident).then_inc(xT_ps, 1)

            def a_proj(b, p, turn):
                pe.wait_ge(xT, b + 1)
                if not peel(b, 0, 1):
                    pe.wait_ge(v_copied, b)
                if not (type(b) is int and b < 3):
                    pe.wait_ge(cx, 2 * (b - 2))
                if cross:
                    pe.wait_ge(ctx_in[p], 16 * (turn + 1))
                    pe.matmul(bank[4][:, 0:T], WQ[:], XT[:], start=True, stop=True)
                    pe.matmul(bank[5][:, 0:L], WK[:], CT[:, p, :], start=True, stop=True)
                    pe.matmul(bank[5][0:L, 2 * C:3 * C], CT[:, p, :], WV[:], start=True, stop=True).then_inc(proj_ps, 1)
                else:
                    pe.matmul(bank[5][:, 0:3 * C], XT[:], WQKV[:], start=True, stop=True).then_inc(proj_ps, 1)

            def a_qkt(b, p):
                if not cross:
                    pe.wait_ge(qr, 4 * (b + 1))
                    pe.transpose(bank[4][:, 0:T], QR[:, 0:C], ident)
                    pe.transpose(bank[4][:, T:2 * T], QR[:, C:2 * C], ident).then_inc(qkT_ps, 1)

            def a_scores(b, g0):
                if g0 == 0:
                    pe.wait_ge(qT, b + 1)
                    pe.wait_ge(kz, b + 1)
                    if not peel(b, 0, 1):
                        pe.wait_ge(sub, NSUB * b)
                for g in (g0, g0 + 1):
                    rows = slice(32 * g, 32 * g + 32)
                    last = pe.matmul(bank[g][:, 0:R * LK], QT[rows, :], KZ[rows, :], start=True, stop=cross)
                if cross and g0 == 2:
                    last.then_inc(s_ps, 1)

            def a_causal(b):
                if not cross:
                    for g in range(G):
                        last = pe.matmul(bank[g].rearrange("p (r l) -> p r l", r=R), n.CB[:, BI:BI + 128],
                                         n.CB[:, BNEG:BNEG + 128].unsqueeze(1).to_broadcast([128, R, T]), start=False, stop=True)
                    last.then_inc(s_ps, 1)

            def b_pt(b, p, g):
                if g == 0:
                    pe.wait_ge(p_exp, b + 1)
                if not peel(b, g, 1):
                    pe.wait_ge(pT, 4 * b + g)
                for r in range(R):
                    h = R * g + r
                    last = pe.transpose(bank[6][0:LK, r * T:(r + 1) * T], P[:, p, h * LK:(h + 1) * LK], ident)
                last.then_inc(pT_ps, 1)

            def b_pv(b, p, g):
                pe.wait_ge(pT, 4 * b + g + 1)
                if g == 0:
                    pe.wait_ge(v_rows, b + 1)
                    if not peel(b, 0, 1):
                        pe.wait_ge(oT, b)
                for r in range(R):
                    h = R * g + r
                    last = pe.matmul(bank[7][32 * r:32 * r + 32, g * T:(g + 1) * T], V[:, p, h * VC:(h + 1) * VC],
                                     PT[:, g % 2, r * T:(r + 1) * T], start=True, stop=True)
                last.then_inc(o_ps, 1)

            def turn_back(b, projected):
                pe.wait_ge(oT, b + 1)
                if not peel(b, 0, 1):
                    pe.wait_ge(x_new, 2 * b)
                pe.wait_ge(v_copied, projected)
                for g in range(G):
                    last = pe.transpose(bank[5][:, g * T:(g + 1) * T], OT[:, g * T:(g + 1) * T], ident)
                last.then_inc(oR_ps, 1)

            def b_transpose(b, projected):
                pe.wait_ge(cx, 2 * (b + 1))
                pe.wait_ge(v_copied, projected)
                pe.transpose(bank[5][:, 0:T], CX[:], ident).then_inc(cT_ps, 1)

            def b_project(b):
                pe.wait_ge(cT, b + 1)
                pe.matmul(bank[5][:, T:T + C], CTX[:], WO[:], start=True, stop=True).then_inc(y_ps, 1)

            pe.wait_ge(loaded, 16 * NL)
            pe.wait_ge(v_ones, 1)

            def first():
                a_xt(0, 0), a_proj(0, 0, 0), a_qkt(0, 0)
                a_scores(0, 0), a_scores(0, 2), a_causal(0)
                a_xt(1, 1), a_proj(1, 1, 0), a_qkt(1, 1)

            def step(b, p, turn, projections, scores):
                tail = not peel(b, 0, 1)
                if scores:
                    a_scores(b + 1, 0)
                if tail:
                    turn_back(b - 1, b + 2 if scores else B)
                if projections:
                    a_xt(b + 2, p)
                if scores:
                    a_scores(b + 1, 2)
                if projections and not cross:
                    a_proj(b + 2, p, turn + 1)
                if scores:
                    a_causal(b + 1)
                b_pt(b, p, 0)
                if projections and cross:
                    a_proj(b + 2, p, turn + 1)
                if tail and not cross:
                    b_transpose(b - 1, b + 3 if projections else B)
                b_pt(b, p, 1)
                b_pv(b, p, 0)
                if tail and cross:
                    b_transpose(b - 1, b + 3 if projections else B)
                if tail and not cross:
                    b_project(b - 1)
                if projections:
                    a_qkt(b + 2, p)
                b_pt(b, p, 2)
                b_pv(b, p, 1)
                if tail and cross:
                    b_project(b - 1)
                b_pt(b, p, 3)
                b_pv(b, p, 2)
                b_pv(b, p, 3)

            def last():
                turn_back(B - 1, B), b_transpose(B - 1, B), b_project(B - 1)

            steps(pe, first, step, last)

        @n.block.vector
        def _(dve):
            def a_norm(b, p):
                norm_vector(dve, n, b, XN[:], stats, s)

            def a_proj(b, p):
                dve.wait_ge(proj_ps, b + 1)
                if cross:
                    kz4 = KZ[:].rearrange("p (r l) -> p r l", r=R)
                    dve.scalar_tensor_tensor(kz4, bank[5][:, 0:L].unsqueeze(1).to_broadcast([128, R, L]), bk[:],
                                             n.CF[:, CHM:CHM + R].unsqueeze(2).to_broadcast([128, R, L]), ALU.add, ALU.mult).then_inc(kz, 1)
                else:
                    dve.tensor_tensor(QK[:], bank[5][:, 0:2 * C], bqkv[:, 0:2 * C], ALU.add).then_inc(qk, 1)
                if not peel(b, 0, 1):
                    dve.wait_ge(v_rows, b)
                dve.tensor_copy(VB[:], bank[5][0:LK, 2 * C:3 * C]).then_inc(v_copied, 1)
                if not cross:
                    dve.wait_ge(qk, b + 1)
                    rope(dve, QK[:], RA[:], RB[:], QR[:], 2 * H, n, qr, 4 * b)

            def a_kz(b, p):
                if not cross:
                    dve.wait_ge(qT, b + 1)
                    dve.tensor_tensor(KZ[:].rearrange("p (r l) -> p r l", r=R), bank[4][:, T:2 * T].unsqueeze(1).to_broadcast([128, R, T]),
                                      n.CF[:, CHM:CHM + R].unsqueeze(2).to_broadcast([128, R, T]), ALU.mult).then_inc(kz, 1)

            def a_softmax(b, p):
                dve.wait_ge(s_ps, b + 1)
                p4 = P[:, p, :].rearrange("p (g r l) -> p g r l", g=4, l=LK)
                m3 = MX[:].rearrange("p (g r) -> p g r", g=4)
                dve.tensor_reduce(m3, scores, AX.X, ALU.max).then_inc(mx, 1)
                top = m3.unsqueeze(3).to_broadcast([128, 4, R, LK])
                if cross:
                    lim = 10000.0 / SCALE
                    dve.tensor_scalar(p4, scores, lim, -lim, ALU.min, ALU.max).then_inc(sub, 1)
                    dve.wait_ge(mx, 2 * b + 1)
                    dve.tensor_scalar(MX[:], MX[:], lim, -lim, ALU.min, ALU.max).then_inc(mx, 1)
                    dve.wait_ge(mx, 2 * b + 2)
                    dve.wait_ge(sub, 2 * b + 1)
                    dve.tensor_tensor(p4, p4, top, ALU.subtract).then_inc(sub, 1)
                else:
                    dve.wait_ge(mx, b + 1)
                    dve.tensor_tensor(p4, scores, top, ALU.subtract).then_inc(sub, 1)

            def b_cx(b):
                dve.wait_ge(oR_ps, b + 1)
                o = bank[5].rearrange("p (h k) -> p h k", k=VC)
                dve.reciprocal(RD[:].unsqueeze(2), o[:, :, D:D + 1]).then_inc(cx, 1)
                dve.wait_ge(cx, 2 * b + 1)
                dve.tensor_tensor(CX[:].rearrange("p (h d) -> p h d", d=D), o[:, :, 0:D],
                                  RD[:].unsqueeze(2).to_broadcast([128, H, D]), ALU.mult).then_inc(cx, 1)

            def b_out(b):
                dve.wait_ge(y_ps, b + 1)
                x = n.X[:, cols(b, C)]
                dve.tensor_tensor(x, bank[5][:, T:T + C], x, ALU.add).then_inc(x_new, 1)
                dve.wait_ge(x_new, 2 * b + 1)
                dve.tensor_tensor(x, x, bo[:], ALU.add).then_inc(x_new, 1)

            dve.wait_ge(loaded, 16 * NL)
            dve.wait_ge(v_ones, 1)

            def first():
                a_norm(0, 0), a_proj(0, 0), a_norm(1, 1), a_kz(0, 0), a_softmax(0, 0)
                a_proj(1, 1), a_kz(1, 1)

            def step(b, p, turn, projections, scores):
                tail = not peel(b, 0, 1)
                if projections:
                    a_norm(b + 2, p)
                if tail:
                    b_cx(b - 1)
                if projections:
                    a_proj(b + 2, p)
                if scores:
                    a_softmax(b + 1, 1 - p)
                if tail:
                    b_out(b - 1)
                if projections:
                    a_kz(b + 2, p)

            def last():
                b_cx(B - 1), b_out(B - 1)
                dve.wait_ge(x_new, 2 * B)

            steps(dve, first, step, last)


def self_attention1(nc, w, n):
    attention1(nc, w, n, cross=False)


def cross_attention1(nc, w, n):
    attention1(nc, w, n, cross=True)


SLOTS = 4


def pair_weights(w, n, i, k):
    both = lambda name: w["L1_ffn_" + name][bass.ds(2 * i, 2)].rearrange("e c f -> c e f")
    return ((n.W1[:, k].rearrange("c (e f) -> c e f", e=2), both("W1")), (n.W3[:, k].rearrange("c (e f) -> c e f", e=2), both("W3")),
            (n.W2[:, k], w["L1_ffn_W2"].rearrange("e f d -> (e f) d")[bass.ds(128 * i, 128), :]))


def route1(nc, w, n):
    with ExitStack() as ctx:
        sb, sem = buffers(nc, ctx, "r1_")
        WR = sb("WR", [128, E])
        stats, XN = sb("stats", [128, B, 10]), sb("XN", [128, B, C])
        LG, TOP, IDX, IDF = sb("LG", [128, B, E]), sb("TOP", [128, B, 8]), sb("IDX", [128, B, 8], U32), sb("IDF", [128, B, 8])
        EX, SE, RS, W, R1, R2 = (sb(k, [128, B, m]) for k, m in (("EX", E), ("SE", 1), ("RS", 1), ("W", E), ("R1", E), ("R2", E)))
        EQ = [sb(f"EQ{k}", [128, B, E]) for k in range(TOPK)]
        SEL = sb("SEL", [128, B, E], BF16)
        WS = sb("WS", [128, B, 3 * E], BF16)
        ps = ctx.enter_context(nc.psum_tensor("r1_ps", [128, 5 * BANK], F32))
        psb = ctx.enter_context(nc.psum_tensor("r1_psb", [128, 2 * BANK], BF16))
        bank = [ps[:, k * BANK:(k + 1) * BANK] for k in range(5)]
        s = {k: sem(k) for k in NORM_SEMS}
        loaded, weights_in = sem("loaded"), sem("weights_in")
        xT_ps, xta, l_ps, lg, top, idx, idf, equal, selected = (sem(k) for k in ("xT_ps", "xta", "l_ps", "lg", "top", "idx", "idf", "equal", "selected"))
        less, ex, se, rs, pos_ps, kept, parts, wT_ps, wT = (sem(k) for k in ("less", "ex", "se", "rs", "pos_ps", "kept", "parts", "wT_ps", "wT"))
        logits = bank[2][:, 0:B * E].rearrange("p (b e) -> p b e", e=E)
        place = bank[3][:, 0:B * E].rearrange("p (b e) -> p b e", e=E)

        @nc_block(nc, ctx).sync
        def _(sp):
            sp.dma_start(WR[:], w["L1_ffn_Wg"]).then_inc(loaded, 16)
            for dst, name in ((n.S1, "Ws1"), (n.S3, "Ws3"), (n.S2, "Ws2")):
                sp.dma_start(dst[:], w["L1_ffn_" + name]).then_inc(weights_in, 16)
            sp.dma_start(n.SELF[:], w["const_sel"]).then_inc(weights_in, 16)
            for i in range(SLOTS):
                for dma in pair_weights(w, n, i, i):
                    sp.dma_start(*dma).then_inc(weights_in, 16)
            sp.wait_ge(weights_in, 16 * (4 + 3 * SLOTS))

        @n.block.gpsimd
        def _(pool):
            norm_all_pool(pool, n, stats, s)

        @n.block.scalar
        def _(act):
            for q in range(2):
                act.wait_ge(xT_ps, q + 1)
                act.activation(n.XTA[:, q * BANK:(q + 1) * BANK], bank[q], ACT.Copy).then_inc(xta, 1)
            act.wait_ge(less, 1)
            act.activation(EX[:], EX[:], ACT.Exp).then_inc(ex, 1)
            act.wait_ge(wT_ps, 1)
            act.activation(n.WT[:], psb[0:96, :], ACT.Copy).then_inc(wT, 1)
            act.wait_ge(wT, 1)

        @n.block.tensor
        def _(pe):
            for b in range(B):
                pe.wait_ge(s["xn"], b + 1)
                last = pe.transpose(bank[b // 4][:, (b % 4) * T:(b % 4 + 1) * T], XN[:, b], n.CF[:, CI:CI + 128])
                if b % 4 == 3:
                    last.then_inc(xT_ps, 1)
            pe.wait_ge(loaded, 16)
            for b in range(B):
                pe.wait_ge(xta, b // 4 + 1)
                last = pe.matmul(bank[2][:, b * E:(b + 1) * E], n.XTA[:, b * T:(b + 1) * T], WR[:], start=True, stop=True)
            last.then_inc(l_ps, 1)
            count_places(pe, n, SEL, bank[3], selected).then_inc(pos_ps, 1)
            pe.wait_ge(parts, 4)
            for b in range(B):
                last = pe.transpose(psb[0:96, b * T:(b + 1) * T], WS[:, b], n.CB[:, BI:BI + 128])
            last.then_inc(wT_ps, 1)

        @n.block.vector
        def _(dve):
            norm_all_vector(dve, n, XN, stats, s)
            dve.wait_ge(l_ps, 1)
            dve.tensor_copy(LG[:], logits).then_inc(lg, 1)
            dve.wait_ge(lg, 1)
            for b in range(B):
                dve.max(TOP[:, b], LG[:, b]).then_inc(top, 1)
            dve.wait_ge(top, B)
            dve.tensor_tensor(EX[:], LG[:], TOP[:, :, 0:1].to_broadcast([128, B, E]), ALU.subtract).then_inc(less, 1)
            for b in range(B):
                dve.max_index(IDX[:, b], TOP[:, b], LG[:, b]).then_inc(idx, 1)
            dve.wait_ge(idx, B)
            dve.tensor_copy(IDF[:], IDX[:]).then_inc(idf, 1)
            dve.wait_ge(idf, 1)
            iota = n.CF[:, CIOTA:CIOTA + E].unsqueeze(1).to_broadcast([128, B, E])
            for k in range(TOPK):
                dve.tensor_tensor(EQ[k][:], iota, IDF[:, :, k:k + 1].to_broadcast([128, B, E]), ALU.is_equal).then_inc(equal, 1)
            dve.wait_ge(equal, 4)
            dve.tensor_tensor(EQ[0][:], EQ[0][:], EQ[1][:], ALU.add).then_inc(equal, 1)
            dve.tensor_tensor(EQ[2][:], EQ[2][:], EQ[3][:], ALU.add).then_inc(equal, 1)
            dve.wait_ge(equal, 6)
            dve.tensor_tensor(SEL[:], EQ[0][:], EQ[2][:], ALU.add).then_inc(selected, 1)
            dve.wait_ge(ex, 1)
            dve.tensor_reduce(SE[:].rearrange("p b o -> p (b o)"), EX[:], AX.X, ALU.add).then_inc(se, 1)
            dve.wait_ge(se, 1)
            dve.reciprocal(RS[:], SE[:]).then_inc(rs, 1)
            dve.wait_ge(selected, 1)
            dve.tensor_tensor(R1[:], EX[:], SEL[:], ALU.mult).then_inc(rs, 1)
            dve.wait_ge(rs, 2)
            dve.tensor_tensor(R2[:], R1[:], RS[:].to_broadcast([128, B, E]), ALU.mult).then_inc(rs, 1)
            dve.wait_ge(pos_ps, 1)
            dve.wait_ge(rs, 3)
            dve.scalar_tensor_tensor(W[:], place, CAP1 + 0.5, R2[:], ALU.is_lt, ALU.mult).then_inc(kept, 1)
            dve.wait_ge(kept, 1)
            dve.tensor_copy(WS[:, :, 0:E], W[:]).then_inc(parts, 1)
            dve.wait_ge(parts, 1)
            dve.tensor_tensor(R1[:], W[:], WS[:, :, 0:E], ALU.subtract).then_inc(parts, 1)
            dve.wait_ge(parts, 2)
            dve.tensor_copy(WS[:, :, E:2 * E], R1[:]).then_inc(parts, 1)
            dve.wait_ge(parts, 3)
            dve.tensor_tensor(WS[:, :, 2 * E:3 * E], R1[:], WS[:, :, E:2 * E], ALU.subtract).then_inc(parts, 1)


def experts1(nc, w, n, out):
    NP = E // 2
    with ExitStack() as ctx:
        sb, sem = buffers(nc, ctx, "e1_")
        SELB = sb("SELB", [96, NP * 128], BF16)
        SG, HU, HW = (sb(k, [128, 2, BANK]) for k in ("SG", "HU", "HW"))
        YT = sb("YT", [128, B * T])
        ps = ctx.enter_context(nc.psum_tensor("e1_ps", [128, 8 * BANK], F32))
        bank = [ps[:, k * BANK:(k + 1) * BANK] for k in range(8)]
        sel_ready = sem("sel_ready")
        w_in = [sem(f"w_in{k}") for k in range(SLOTS)]
        gu_ps, wb_ps, silu, hu, hw, y_ps = (sem(k) for k in ("gu_ps", "wb_ps", "silu", "hu", "hw", "y_ps"))
        yT, yr_ps, x_new, stored = sem("yT"), sem("yr_ps"), sem("x_new"), sem("stored")

        @nc_block(nc, ctx).sync
        def _(sp):
            with sp.Fori(1, NP // SLOTS) as t:
                for k in range(SLOTS):
                    i = SLOTS * t + k
                    sp.wait_ge(y_ps, 2 * i + 4 - 2 * SLOTS)
                    for dma in pair_weights(w, n, i, k):
                        sp.dma_start(*dma).then_inc(w_in[k], 16)
            for b in range(B):
                sp.wait_ge(x_new, b + 1)
                sp.dma_start(out[b], n.X[:, b * C:(b + 1) * C]).then_inc(stored, 16)
            sp.wait_ge(stored, 16 * B)

        def each_pair(eng, shared, f):
            shared()
            with eng.Fori(0, NP) as i:
                f(i)

        @n.block.scalar
        def _(act):
            def half(u, q):
                act.wait_ge(gu_ps, u + 1)
                if not (type(u) is int and u < 2):
                    act.wait_ge(hu, u - 1)
                act.activation(SG[:, q], bank[q], ACT.Silu).then_inc(silu, 1)

            each_pair(act, lambda: (half(0, 0), half(1, 1)), lambda i: (half(2 * i + 2, 0), half(2 * i + 3, 1)))
            for q in range(2):
                act.wait_ge(y_ps, 2 * NP + 1 + q)
                act.activation(YT[:, q * BANK:(q + 1) * BANK], bank[6 + q], ACT.Copy).then_inc(yT, 1)

        @n.block.tensor
        def _(pe):
            def half(u, q, w1, w3, sel):
                x = n.XTA[:, q * BANK:(q + 1) * BANK]
                if not (type(u) is int and u < 2):
                    pe.wait_ge(hu, u - 1)
                pe.matmul(bank[q], w1, x, start=True, stop=True)
                pe.matmul(bank[2 + q], w3, x, start=True, stop=True).then_inc(gu_ps, 1)
                if sel is not None:
                    if not (type(u) is int and u < 4):
                        pe.wait_ge(hw, u - 3)
                    pe.matmul(bank[4 + q], sel, n.WT[:, q * BANK:(q + 1) * BANK], start=True, stop=True).then_inc(wb_ps, 1)

            def down(u, q, w2, start, stop):
                if type(u) is int and u < 2:
                    pe.wait_ge(hu, u + 1)
                else:
                    pe.wait_ge(hw, u - 1)
                pe.matmul(bank[6 + q], w2, HU[:, q] if type(u) is int and u < 2 else HW[:, q], start=start, stop=stop).then_inc(y_ps, 1)

            def pair(i, k, turn, down_w, start):
                if not type(turn) is int:
                    pe.wait_ge(w_in[k], 48 * turn)
                for q in range(2):
                    half(2 * i + 2 + q, q, n.W1[:, k], n.W3[:, k], SELB[:, cols(i, 128)])
                    down(2 * i + q, q, down_w, start, False)

            half(0, 0, n.S1[:], n.S3[:], None)
            half(1, 1, n.S1[:], n.S3[:], None)
            pe.wait_ge(sel_ready, 1)
            for k in range(SLOTS):
                pair(k, k, 0, n.W2[:, k - 1] if k else n.S2[:], k == 0)
            with pe.Fori(1, NP // SLOTS) as t:
                for k in range(SLOTS):
                    pair(SLOTS * t + k, k, t, n.W2[:, (k - 1) % SLOTS], False)
            for q in range(2):
                down(2 * NP + q, q, n.W2[:, SLOTS - 1], False, True)
            pe.wait_ge(hu, 2 * NP + 2)
            for b in range(B):
                pe.wait_ge(yT, b // 4 + 1)
                pe.transpose(bank[b // 4][:, (b % 4) * T:(b % 4 + 1) * T], YT[:, b * T:(b + 1) * T], n.CF[:, CI:CI + 128])\
                    .then_inc(yr_ps, 1)

        @n.block.vector
        def _(dve):
            def shared(u, q):
                dve.wait_ge(silu, u + 1)
                dve.tensor_tensor(HU[:, q], bank[2 + q], SG[:, q], ALU.mult).then_inc(hu, 1)

            def half(u, q):
                dve.wait_ge(silu, u + 1)
                dve.wait_ge(y_ps, u - 1)
                dve.tensor_tensor(HU[:, q], bank[2 + q], SG[:, q], ALU.mult).then_inc(hu, 1)
                dve.wait_ge(wb_ps, u - 1)
                dve.wait_ge(hu, u + 1)
                dve.tensor_tensor(HW[:, q], bank[4 + q], HU[:, q], ALU.mult).then_inc(hw, 1)

            dve.tensor_copy(SELB[:], n.SELF[:]).then_inc(sel_ready, 1)
            each_pair(dve, lambda: (shared(0, 0), shared(1, 1)), lambda i: (half(2 * i + 2, 0), half(2 * i + 3, 1)))
            for b in range(B):
                dve.wait_ge(yr_ps, 4 * (b // 4) + 4)
                x = n.X[:, b * C:(b + 1) * C]
                dve.tensor_tensor(x, bank[b // 4][:, (b % 4) * T:(b % 4 + 1) * T], x, ALU.add).then_inc(x_new, 1)


def program(nc, w, out, upto=99, only=0):
    n = Net()
    with ExitStack() as ctx:
        sb, sem = buffers(nc, ctx, "")
        n.X = sb("X", [128, B * C])
        n.CF, n.CB = sb("CF", [128, NCF]), sb("CB", [128, NCB], BF16)
        n.NHALF, n.EPS = sb("NHALF", [128, 1]), sb("EPS", [128, 1])
        n.SINK = sb("SINK", [128, 64 * (D + 1)])
        n.WQX, n.WKX, n.WVX, n.WOX = sb("WQX", [128, 1024]), sb("WKX", [CC, 1024]), sb("WVX", [CC, 1024]), sb("WOX", [128, 1024])
        n.vi_dram = nc.dram_tensor("vi_scratch", (B * LI, 1024), F32, kind="Internal").ap()
        n.buf_dram = nc.dram_tensor("slots_scratch", (E * CAP0, C), F32, kind="Internal").ap()
        n.y_dram = nc.dram_tensor("rows_scratch", (E * CAP0, C), F32, kind="Internal").ap()
        n.SLOT, n.GATE = sb("SLOT", [128, B], I32), sb("GATE", [128, B])
        with ExitStack() as lora:
            lora_buffers(nc, lora, n)
            self0_buffers(nc, lora, n)
            load_phase(nc, w, n)
            if only == 0:
                self_attention0(nc, w, n)
            else:
                with ExitStack() as ctx:
                    nc_block(nc, ctx).sync(lambda sp: start_lora(sp, w, n))
            fold_phase(nc, w, n)
        phases = [cross_attention0, experts_layer0, self_attention1, cross_attention1]
        for phase in phases[max(only - 1, 0):max(upto - 1, 0)]:
            phase(nc, w, n)
        if upto == 99:
            n.XTA, n.WT = sb("XTA", [128, B * T]), sb("WT", [96, B * T], BF16)
            n.W1, n.W3, n.W2 = (sb(k, [128, SLOTS, 128]) for k in ("W1", "W3", "W2"))
            n.S1, n.S3, n.S2, n.SELF = sb("S1", [128, 128]), sb("S3", [128, 128]), sb("S2", [128, 128]), sb("SELF", [96, E // 2 * 128])
            route1(nc, w, n)
            experts1(nc, w, n, out)
        else:
            store_phase(nc, w, n, out)


def constants():
    import numpy as np

    f = np.zeros((128, NCF), np.float32)
    p = np.arange(128)[:, None]
    q = np.arange(128)[None, :]
    f[:, CI:CI + 128] = p == q
    for br, (h, g) in enumerate(((16, 0), (128, 16), (128, 0))):
        f[:, CM + br * 128:CM + (br + 1) * 128] = (q - p >= g) & (q - p < h)
    angle = np.arange(T, dtype=np.float32)[:, None] * (1.0 / np.float32(10000.0) ** (np.arange(0, D, 2, dtype=np.float32) / D))[None, :]
    angle = np.repeat(angle.astype(np.float32), 2, axis=1)
    f[:, CCOS:CCOS + D] = np.cos(angle)
    f[:, CSIN:CSIN + D] = np.sin(angle)
    f[:, CHM:CHM + R] = (p % 32) // D == np.arange(R)[None, :]
    f[:, CIOTA:CIOTA + E] = np.arange(E)[None, :]
    f[:, CONE:CONE + 128] = 1.0
    h = np.zeros((128, NCB), np.float32)
    h[:, BI:BI + 128] = p == q
    h[:, BNEG:BNEG + 128] = np.where(q <= p, 0.0, -1e30)
    h[:, BTRI:BTRI + 128] = p <= q
    h[:, BONE:BONE + 128] = 1.0
    sel = np.zeros((96, 16, 128), np.float32)
    k, i, m = np.arange(96)[:, None, None], np.arange(16)[None, :, None], np.arange(128)[None, None, :]
    sel[:] = k % 32 == 2 * i + m // 64
    return {"const_f32": f, "const_half": h, "const_sel": sel.reshape(96, 2048)}


def layout(inputs):
    import numpy as np

    a = {k: np.asarray(v) for k, v in inputs.items()}
    out = {k: a[k] for k in a if k != "ctx_768"}
    for t in "qkvo":
        out[f"L0_xattn_{t}_down_T"] = a[f"L0_xattn_{t}_down"].T
        del out[f"L0_xattn_{t}_down"]
    out["ctx_T"] = a["ctx_768"].transpose(0, 2, 1)
    out["ctx_img_T"] = a["ctx_768"][:, LO:, :].reshape(B * LI, CC).T
    out["L1_attn_wqkv_T"] = np.concatenate([out.pop(f"L1_attn_w{t}").T for t in "qkv"], axis=1)
    out["L1_attn_bqkv"] = np.concatenate([out.pop(f"L1_attn_b{t}") for t in "qkv"])
    out["L1_attn_wp_T"] = out.pop("L1_attn_wp").T
    out.update(constants())
    return {k: np.ascontiguousarray(v) for k, v in out.items()}


def kernel(**inputs):
    import numpy as np
    import concourse.bacc as bacc
    from concourse.bass_utils import run_bass_kernel_spmd

    nc = bacc.Bacc("TRN2", target_bir_lowering=False, num_devices=1)
    arrays = {f"in_{k}": v for k, v in layout(inputs).items()}
    w = {k[3:]: nc.dram_tensor(k, v.shape, mybir.dt.from_np(v.dtype), kind="ExternalInput").ap() for k, v in arrays.items()}
    out = nc.dram_tensor("out_x", (B, T, C), F32, kind="ExternalOutput").ap()
    program(nc, w, out)
    r = run_bass_kernel_spmd(nc, [arrays], core_ids=[0])
    return r.results[0]["out_x"]
```
